# Optimizing a Trainium2 kernel written in Bass

```python
import numpy as np
import jax
import jax.numpy as jnp

def _softmax(x, axis=-1):
    return jax.nn.softmax(x, axis=axis)

def _gelu(x):
    return jax.nn.gelu(x, approximate=True)

def _silu(x):
    return jax.nn.silu(x)

def _sigmoid(x):
    return jax.nn.sigmoid(x)

def _layernorm(x, axis=-1, eps=1e-05):
    m = jnp.mean(x, axis=axis, keepdims=True)
    v = jnp.var(x, axis=axis, keepdims=True)
    return (x - m) / jnp.sqrt(v + eps)

def _scatter_add(tgt, idx, src, axis=0):
    return tgt.at[idx].add(src)

def _segment_sum(src, seg, n):
    return jax.ops.segment_sum(src, seg, n)
kernel_name = 'mk_gnn_ffn_d4_gnn_r32_e91161'

def setup_inputs(seed: int=0):
    np.random.seed(seed)
    _w = jnp.asarray

    def _rec_inputs():
        import jax
        import jax.numpy as jnp
        _gk = jax.random.key(seed)
        x = -8.776e-05 + 1 * jax.random.normal(jax.random.fold_in(_gk, 1), (625, 256), jnp.float32)
        src = jax.random.randint(jax.random.fold_in(_gk, 2), (20000,), 0, 625, jnp.int32)
        dst = jax.random.randint(jax.random.fold_in(_gk, 3), (20000,), 0, 625, jnp.int32)
        _o = jnp.argsort(dst, stable=True)
        src = src[_o]
        dst = dst[_o]
        return (x, src, dst)
    x, src, dst = _rec_inputs()

    def _L0_gnn_setup():
        import jax, jax.numpy as jnp
        import numpy as np
        N = 625
        E = 20000
        D = 256
        H = 4
        Dh = 64
        L = 3
        BN_EPS = 1e-05

        def _transformer_conv(x, src, dst, Wq, bq, Wk, bk, Wv, bv, Ws, bs):
            q = (x @ Wq + bq).reshape(N, H, Dh)
            k = (x @ Wk + bk).reshape(N, H, Dh)
            v = (x @ Wv + bv).reshape(N, H, Dh)
            qd = q[dst]
            ks_ = k[src]
            score = jnp.einsum('ehd,ehd->eh', qd, ks_) / np.sqrt(Dh)
            m = jax.ops.segment_max(score, dst, num_segments=N)
            ex = jnp.exp(score - m[dst])
            denom = jax.ops.segment_sum(ex, dst, num_segments=N)
            alpha = ex / denom[dst]
            msg = alpha[:, :, None] * v[src]
            out = jax.ops.segment_sum(msg, dst, num_segments=N)
            out = out.reshape(N, H * Dh)
            return out + x @ Ws + bs

        def _batch_norm(x, gamma, beta):
            mean = jnp.mean(x, axis=0)
            var = jnp.var(x, axis=0)
            return gamma * (x - mean) * jax.lax.rsqrt(var + BN_EPS) + beta
        key = jax.random.key(seed)
        ks = jax.random.split(key, 14)
        s = 1.0 / np.sqrt(D)
        f32 = jnp.float32
        return {'x': jax.random.normal(ks[0], (N, D), f32), 'edge_index': jax.random.randint(ks[1], (2, E), 0, N, dtype=jnp.int32), 'Wq': jax.random.normal(ks[2], (L, D, D), f32) * s, 'bq': jax.random.normal(ks[3], (L, D), f32) * 0.02, 'Wk': jax.random.normal(ks[4], (L, D, D), f32) * s, 'bk': jax.random.normal(ks[5], (L, D), f32) * 0.02, 'Wv': jax.random.normal(ks[6], (L, D, D), f32) * s, 'bv': jax.random.normal(ks[7], (L, D), f32) * 0.02, 'Ws': jax.random.normal(ks[8], (L, D, D), f32) * s, 'bs': jax.random.normal(ks[9], (L, D), f32) * 0.02, 'bn_gamma': 1.0 + 0.1 * jax.random.normal(ks[10], (L - 1, D), f32), 'bn_beta': 0.1 * jax.random.normal(ks[11], (L - 1, D), f32)}
    _L0_gnn_all = _L0_gnn_setup()
    _L0_gnn_in = {k: v for k, v in _L0_gnn_all.items() if k in ('Wq', 'bq', 'Wk', 'bk', 'Wv', 'bv', 'Ws', 'bs', 'bn_gamma', 'bn_beta')}
    del _L0_gnn_all

    def _L0_ffn_setup():
        import jax, jax.numpy as jnp
        import numpy as np
        TOP_K = 2
        key = jax.random.key(seed)
        ks = jax.random.split(key, 4)
        B, L, D, H, E = (8, 128, 256, 1024, 8)
        s = 0.02
        return {'x': jax.random.normal(ks[0], (B, L, D), jnp.float32), 'Wg': jax.random.normal(ks[1], (D, E), jnp.float32) * s, 'bg': jnp.zeros((E,), jnp.float32), 'W1': jax.random.normal(ks[2], (E, D, H), jnp.float32) * s, 'b1': jnp.zeros((E, H), jnp.float32), 'W2': jax.random.normal(ks[3], (E, H, D), jnp.float32) * s, 'b2': jnp.zeros((E, D), jnp.float32)}
    _L0_ffn_all = _L0_ffn_setup()
    _L0_ffn_in = {k: v for k, v in _L0_ffn_all.items() if k in ('Wg', 'bg', 'W1', 'b1', 'W2', 'b2')}
    del _L0_ffn_all

    def _L1_gnn_setup():
        import jax, jax.numpy as jnp
        import numpy as np
        NEG = -1000.0
        SLOPE = 0.01
        N_NODES, N_EDGES, D_IN, D_OUT, N_HEADS = (3125, 50000, 256, 64, 4)
        key = jax.random.key(seed)
        k0, k1, k2, k3, k4 = jax.random.split(key, 5)
        h = jax.random.normal(k0, (N_NODES, D_IN), jnp.float32)
        src = jax.random.randint(k1, (N_EDGES,), 0, N_NODES)
        dst = jax.random.randint(k2, (N_EDGES,), 0, N_NODES)
        W = jax.random.normal(k3, (N_HEADS, D_IN, D_OUT), jnp.float32) / np.sqrt(D_IN)
        att = jax.random.normal(k4, (N_HEADS, 2 * D_OUT), jnp.float32) / np.sqrt(2.0 * D_OUT)
        return {'h': h, 'W': W, 'att': att, 'src': src, 'dst': dst}
    _L1_gnn_all = _L1_gnn_setup()
    _L1_gnn_in = {k: v for k, v in _L1_gnn_all.items() if k in ('W', 'att')}
    del _L1_gnn_all

    def _L1_ffn_setup():
        import jax, jax.numpy as jnp
        import numpy as np
        TOP_K = 2
        LN_EPS = 1e-05
        key = jax.random.key(seed)
        ks = jax.random.split(key, 8)
        B, S, D, E, H = (16, 1024, 256, 8, 1024)
        x = jax.random.normal(ks[0], (B, S, D), dtype=jnp.float32)
        Wr = jax.random.normal(ks[1], (D, E), dtype=jnp.float32) * 0.1
        br = jnp.zeros((E,), dtype=jnp.float32)
        ln_g = jnp.ones((E, D), dtype=jnp.float32)
        ln_b = jnp.zeros((E, D), dtype=jnp.float32)
        W1 = jax.random.normal(ks[2], (E, D, H), dtype=jnp.float32) * (1.0 / np.sqrt(D))
        b1 = jnp.zeros((E, H), dtype=jnp.float32)
        W2 = jax.random.normal(ks[3], (E, H, D), dtype=jnp.float32) * (1.0 / np.sqrt(H))
        b2 = jnp.zeros((E, D), dtype=jnp.float32)
        return {'x': x, 'Wr': Wr, 'br': br, 'ln_g': ln_g, 'ln_b': ln_b, 'W1': W1, 'b1': b1, 'W2': W2, 'b2': b2}
    _L1_ffn_all = _L1_ffn_setup()
    _L1_ffn_in = {k: v for k, v in _L1_ffn_all.items() if k in ('Wr', 'br', 'ln_g', 'ln_b', 'W1', 'b1', 'W2', 'b2')}
    del _L1_ffn_all

    def _L2_gnn_setup():
        import jax, jax.numpy as jnp
        import numpy as np
        N, D, H = (50000, 256, 8)
        C = D // H
        E = 50000
        NEG_SLOPE = 0.2
        EPS = 1e-05

        def _gat_block(x, src, dst, W, att_src, att_dst, bias, ln_w, ln_b):
            n = x.shape[0]
            h = (x @ W).reshape(n, H, C)
            a_src = jnp.einsum('nhc,hc->nh', h, att_src)
            a_dst = jnp.einsum('nhc,hc->nh', h, att_dst)
            e = a_src[src] + a_dst[dst]
            e = jnp.where(e > 0, e, NEG_SLOPE * e)
            m = jax.ops.segment_max(e, dst, num_segments=n)
            m = jnp.where(jnp.isfinite(m), m, 0.0)
            ex = jnp.exp(e - m[dst])
            denom = jax.ops.segment_sum(ex, dst, num_segments=n)
            alpha = ex / denom[dst]
            msg = h[src] * alpha[..., None]
            out = jax.ops.segment_sum(msg, dst, num_segments=n).reshape(n, H * C) + bias
            y = out + x
            mu = y.mean(axis=-1, keepdims=True)
            var = y.var(axis=-1, keepdims=True)
            return (y - mu) / jnp.sqrt(var + EPS) * ln_w + ln_b
        key = jax.random.key(seed)
        ks = jax.random.split(key, 8)
        x = jax.random.normal(ks[0], (N, D), dtype=jnp.float32)
        edge_index = jax.random.randint(ks[1], (2, E), 0, N, dtype=jnp.int32)
        scale = 1.0 / np.sqrt(D)
        W = jax.random.normal(ks[2], (D, H * C), dtype=jnp.float32) * scale
        att_src = jax.random.normal(ks[3], (H, C), dtype=jnp.float32) * scale
        att_dst = jax.random.normal(ks[4], (H, C), dtype=jnp.float32) * scale
        bias = jnp.zeros((H * C,), dtype=jnp.float32)
        ln_w = jnp.ones((D,), dtype=jnp.float32)
        ln_b = jnp.zeros((D,), dtype=jnp.float32)
        return {'x': x, 'edge_index': edge_index, 'W': W, 'att_src': att_src, 'att_dst': att_dst, 'bias': bias, 'ln_w': ln_w, 'ln_b': ln_b}
    _L2_gnn_all = _L2_gnn_setup()
    _L2_gnn_in = {k: v for k, v in _L2_gnn_all.items() if k in ('W', 'att_src', 'att_dst', 'bias', 'ln_w', 'ln_b')}
    del _L2_gnn_all

    def _L2_ffn_setup():
        import math
        import jax, jax.numpy as jnp
        import numpy as np
        CAPACITY_FACTOR = 1.25
        TOP_K = 2
        LN_EPS = 1e-05

        def _layer_norm(x, gamma, beta):
            mu = jnp.mean(x, axis=-1, keepdims=True)
            var = jnp.var(x, axis=-1, keepdims=True)
            return (x - mu) * jax.lax.rsqrt(var + LN_EPS) * gamma + beta
        key = jax.random.key(seed)
        ks = jax.random.split(key, 4)
        B, S, D, F, E = (8, 128, 256, 512, 8)
        x = jax.random.normal(ks[0], (B, S, D), dtype=jnp.float32)
        Wr = jax.random.normal(ks[1], (D, E), dtype=jnp.float32) / np.sqrt(D)
        br = jnp.zeros((E,), jnp.float32)
        W1 = jax.random.normal(ks[2], (E, D, F), dtype=jnp.float32) / np.sqrt(D)
        b1 = jnp.zeros((E, F), jnp.float32)
        W2 = jax.random.normal(ks[3], (E, F, D), dtype=jnp.float32) / np.sqrt(F)
        b2 = jnp.zeros((E, D), jnp.float32)
        gamma = jnp.ones((D,), jnp.float32)
        beta = jnp.zeros((D,), jnp.float32)
        return {'x': x, 'Wr': Wr, 'br': br, 'W1': W1, 'b1': b1, 'W2': W2, 'b2': b2, 'gamma': gamma, 'beta': beta}
    _L2_ffn_all = _L2_ffn_setup()
    _L2_ffn_in = {k: v for k, v in _L2_ffn_all.items() if k in ('Wr', 'br', 'W1', 'b1', 'W2', 'b2', 'gamma', 'beta')}
    del _L2_ffn_all

    def _L3_gnn_setup():
        import jax, jax.numpy as jnp
        import numpy as np
        N_NODES = 50000
        N_EDGES = 25000
        D_IN = 256
        D_OUT = 256
        BN_EPS = 1e-05

        def _forward(x, edge_index, w1, b1, gamma, beta, w2, b2, w_gcn, b_gcn):
            n = x.shape[0]
            h = x @ w1.T + b1
            mean = jnp.mean(h, axis=0)
            var = jnp.var(h, axis=0)
            h = (h - mean) * jax.lax.rsqrt(var + BN_EPS) * gamma + beta
            h = jax.nn.relu(h)
            h = h @ w2.T + b2
            xw = h @ w_gcn.T
            src = jnp.concatenate([edge_index[0], jnp.arange(n, dtype=edge_index.dtype)])
            dst = jnp.concatenate([edge_index[1], jnp.arange(n, dtype=edge_index.dtype)])
            deg = jax.ops.segment_sum(jnp.ones_like(dst, dtype=xw.dtype), dst, num_segments=n)
            dinv = jnp.where(deg > 0, jax.lax.rsqrt(jnp.maximum(deg, 1.0)), 0.0)
            norm = dinv[src] * dinv[dst]
            msgs = xw[src] * norm[:, None]
            out = jax.ops.segment_sum(msgs, dst, num_segments=n) + b_gcn
            return out
        key = jax.random.key(seed)
        ks = jax.random.split(key, 8)
        x = jax.random.normal(ks[0], (N_NODES, D_IN), dtype=jnp.float32)
        edge_index = jax.random.randint(ks[1], (2, N_EDGES), 0, N_NODES, dtype=jnp.int64)
        s1 = 1.0 / np.sqrt(D_IN)
        s2 = 1.0 / np.sqrt(D_OUT)
        w1 = jax.random.uniform(ks[2], (D_OUT, D_IN), jnp.float32, -s1, s1)
        b1 = jax.random.uniform(ks[3], (D_OUT,), jnp.float32, -s1, s1)
        gamma = jnp.ones((D_OUT,), jnp.float32)
        beta = jnp.zeros((D_OUT,), jnp.float32)
        w2 = jax.random.uniform(ks[4], (D_OUT, D_OUT), jnp.float32, -s2, s2)
        b2 = jax.random.uniform(ks[5], (D_OUT,), jnp.float32, -s2, s2)
        w_gcn = jax.random.uniform(ks[6], (D_OUT, D_OUT), jnp.float32, -s2, s2)
        b_gcn = jnp.zeros((D_OUT,), jnp.float32)
        return {'x': x, 'edge_index': edge_index, 'w1': w1, 'b1': b1, 'gamma': gamma, 'beta': beta, 'w2': w2, 'b2': b2, 'w_gcn': w_gcn, 'b_gcn': b_gcn}
    _L3_gnn_all = _L3_gnn_setup()
    _L3_gnn_in = {k: v for k, v in _L3_gnn_all.items() if k in ('w1', 'b1', 'gamma', 'beta', 'w2', 'b2', 'w_gcn', 'b_gcn')}
    del _L3_gnn_all

    def _L3_ffn_setup():
        import jax, jax.numpy as jnp
        import numpy as np
        N_EXPERTS = 8
        TOP_K = 2
        key = jax.random.key(seed)
        ks = jax.random.split(key, 5)
        B, T, C, E, H = (8, 64, 256, 8, 682)
        scale = 1.0 / np.sqrt(C)
        return {'x': jax.random.normal(ks[0], (B, T, C), dtype=jnp.float32), 'router_w': jax.random.normal(ks[1], (E, C), dtype=jnp.float32) * scale, 'w1': jax.random.normal(ks[2], (E, H, C), dtype=jnp.float32) * scale, 'w2': jax.random.normal(ks[3], (E, C, H), dtype=jnp.float32) * (1.0 / np.sqrt(H)), 'w3': jax.random.normal(ks[4], (E, H, C), dtype=jnp.float32) * scale}
    _L3_ffn_all = _L3_ffn_setup()
    _L3_ffn_in = {k: v for k, v in _L3_ffn_all.items() if k in ('router_w', 'w1', 'w2', 'w3')}
    del _L3_ffn_all
    return {'x': x, 'src': src, 'dst': dst, 'L0_gnn_Wq': _L0_gnn_in['Wq'], 'L0_gnn_bq': _L0_gnn_in['bq'], 'L0_gnn_Wk': _L0_gnn_in['Wk'], 'L0_gnn_bk': _L0_gnn_in['bk'], 'L0_gnn_Wv': _L0_gnn_in['Wv'], 'L0_gnn_bv': _L0_gnn_in['bv'], 'L0_gnn_Ws': _L0_gnn_in['Ws'], 'L0_gnn_bs': _L0_gnn_in['bs'], 'L0_gnn_bn_gamma': _L0_gnn_in['bn_gamma'], 'L0_gnn_bn_beta': _L0_gnn_in['bn_beta'], 'L0_ffn_Wg': _L0_ffn_in['Wg'], 'L0_ffn_bg': _L0_ffn_in['bg'], 'L0_ffn_W1': _L0_ffn_in['W1'], 'L0_ffn_b1': _L0_ffn_in['b1'], 'L0_ffn_W2': _L0_ffn_in['W2'], 'L0_ffn_b2': _L0_ffn_in['b2'], 'L1_gnn_W': _L1_gnn_in['W'], 'L1_gnn_att': _L1_gnn_in['att'], 'L1_ffn_Wr': _L1_ffn_in['Wr'], 'L1_ffn_br': _L1_ffn_in['br'], 'L1_ffn_ln_g': _L1_ffn_in['ln_g'], 'L1_ffn_ln_b': _L1_ffn_in['ln_b'], 'L1_ffn_W1': _L1_ffn_in['W1'], 'L1_ffn_b1': _L1_ffn_in['b1'], 'L1_ffn_W2': _L1_ffn_in['W2'], 'L1_ffn_b2': _L1_ffn_in['b2'], 'L2_gnn_W': _L2_gnn_in['W'], 'L2_gnn_att_src': _L2_gnn_in['att_src'], 'L2_gnn_att_dst': _L2_gnn_in['att_dst'], 'L2_gnn_bias': _L2_gnn_in['bias'], 'L2_gnn_ln_w': _L2_gnn_in['ln_w'], 'L2_gnn_ln_b': _L2_gnn_in['ln_b'], 'L2_ffn_Wr': _L2_ffn_in['Wr'], 'L2_ffn_br': _L2_ffn_in['br'], 'L2_ffn_W1': _L2_ffn_in['W1'], 'L2_ffn_b1': _L2_ffn_in['b1'], 'L2_ffn_W2': _L2_ffn_in['W2'], 'L2_ffn_b2': _L2_ffn_in['b2'], 'L2_ffn_gamma': _L2_ffn_in['gamma'], 'L2_ffn_beta': _L2_ffn_in['beta'], 'L3_gnn_w1': _L3_gnn_in['w1'], 'L3_gnn_b1': _L3_gnn_in['b1'], 'L3_gnn_gamma': _L3_gnn_in['gamma'], 'L3_gnn_beta': _L3_gnn_in['beta'], 'L3_gnn_w2': _L3_gnn_in['w2'], 'L3_gnn_b2': _L3_gnn_in['b2'], 'L3_gnn_w_gcn': _L3_gnn_in['w_gcn'], 'L3_gnn_b_gcn': _L3_gnn_in['b_gcn'], 'L3_ffn_router_w': _L3_ffn_in['router_w'], 'L3_ffn_w1': _L3_ffn_in['w1'], 'L3_ffn_w2': _L3_ffn_in['w2'], 'L3_ffn_w3': _L3_ffn_in['w3']}

def reference(x, src, dst, L0_gnn_Wq, L0_gnn_bq, L0_gnn_Wk, L0_gnn_bk, L0_gnn_Wv, L0_gnn_bv, L0_gnn_Ws, L0_gnn_bs, L0_gnn_bn_gamma, L0_gnn_bn_beta, L0_ffn_Wg, L0_ffn_bg, L0_ffn_W1, L0_ffn_b1, L0_ffn_W2, L0_ffn_b2, L1_gnn_W, L1_gnn_att, L1_ffn_Wr, L1_ffn_br, L1_ffn_ln_g, L1_ffn_ln_b, L1_ffn_W1, L1_ffn_b1, L1_ffn_W2, L1_ffn_b2, L2_gnn_W, L2_gnn_att_src, L2_gnn_att_dst, L2_gnn_bias, L2_gnn_ln_w, L2_gnn_ln_b, L2_ffn_Wr, L2_ffn_br, L2_ffn_W1, L2_ffn_b1, L2_ffn_W2, L2_ffn_b2, L2_ffn_gamma, L2_ffn_beta, L3_gnn_w1, L3_gnn_b1, L3_gnn_gamma, L3_gnn_beta, L3_gnn_w2, L3_gnn_b2, L3_gnn_w_gcn, L3_gnn_b_gcn, L3_ffn_router_w, L3_ffn_w1, L3_ffn_w2, L3_ffn_w3):
    import jax
    import jax.numpy as jnp

    def _L0_gnn_ref(x, edge_index, Wq, bq, Wk, bk, Wv, bv, Ws, bs, bn_gamma, bn_beta):
        import jax, jax.numpy as jnp
        import numpy as np
        N = 625
        E = 20000
        D = 256
        H = 4
        Dh = 64
        L = 3
        BN_EPS = 1e-05

        def _transformer_conv(x, src, dst, Wq, bq, Wk, bk, Wv, bv, Ws, bs):
            q = (x @ Wq + bq).reshape(N, H, Dh)
            k = (x @ Wk + bk).reshape(N, H, Dh)
            v = (x @ Wv + bv).reshape(N, H, Dh)
            qd = q[dst]
            ks_ = k[src]
            score = jnp.einsum('ehd,ehd->eh', qd, ks_) / np.sqrt(Dh)
            m = jax.ops.segment_max(score, dst, num_segments=N)
            ex = jnp.exp(score - m[dst])
            denom = jax.ops.segment_sum(ex, dst, num_segments=N)
            alpha = ex / denom[dst]
            msg = alpha[:, :, None] * v[src]
            out = jax.ops.segment_sum(msg, dst, num_segments=N)
            out = out.reshape(N, H * Dh)
            return out + x @ Ws + bs

        def _batch_norm(x, gamma, beta):
            mean = jnp.mean(x, axis=0)
            var = jnp.var(x, axis=0)
            return gamma * (x - mean) * jax.lax.rsqrt(var + BN_EPS) + beta
        src, dst = (edge_index[0], edge_index[1])
        for i in range(L):
            x = _transformer_conv(x, src, dst, Wq[i], bq[i], Wk[i], bk[i], Wv[i], bv[i], Ws[i], bs[i])
            if i < L - 1:
                x = jax.nn.relu(_batch_norm(x, bn_gamma[i], bn_beta[i]))
        return x

    def _L0_ffn_ref(x, Wg, bg, W1, b1, W2, b2):
        import jax, jax.numpy as jnp
        import numpy as np
        TOP_K = 2
        B, L, D = x.shape
        E = W1.shape[0]
        xf = x.reshape(-1, D)
        gate_logits = xf @ Wg + bg
        top_w, top_i = jax.lax.top_k(gate_logits, TOP_K)
        top_w = jax.nn.softmax(top_w, axis=-1)
        w_dense = jnp.sum(jax.nn.one_hot(top_i, E, dtype=xf.dtype) * top_w[..., None], axis=1)
        out = jnp.zeros_like(xf)
        for e in range(E):
            h = jax.nn.gelu(xf @ W1[e] + b1[e], approximate=False)
            out = out + w_dense[:, e:e + 1] * (h @ W2[e] + b2[e])
        return out.reshape(B, L, D)

    def _L1_gnn_ref(h, W, att, src, dst):
        import jax, jax.numpy as jnp
        import numpy as np
        NEG = -1000.0
        SLOPE = 0.01
        N_NODES, N_EDGES, D_IN, D_OUT, N_HEADS = (3125, 50000, 256, 64, 4)
        N = h.shape[0]
        H, _, F = W.shape
        z = jnp.einsum('nd,hdf->nhf', h, W)
        a_src, a_dst = (att[:, :F], att[:, F:])
        es = jnp.einsum('nhf,hf->nh', z, a_src)
        ed = jnp.einsum('nhf,hf->nh', z, a_dst)
        e = jax.nn.leaky_relu(es[src] + ed[dst], SLOPE)
        e = jnp.where(e == 0.0, NEG, e)
        m = jax.ops.segment_max(e, dst, num_segments=N)
        m = jnp.where(jnp.isfinite(m), m, 0.0)
        ex = jnp.exp(e - m[dst])
        denom = jax.ops.segment_sum(ex, dst, num_segments=N)
        safe = jnp.where(denom[dst] > 0.0, denom[dst], 1.0)
        alpha = ex / safe
        out = jax.ops.segment_sum(alpha[:, :, None] * z[src], dst, num_segments=N)
        return out.reshape(N, H * F)

    def _L1_ffn_ref(x, Wr, br, ln_g, ln_b, W1, b1, W2, b2):
        import jax, jax.numpy as jnp
        import numpy as np
        TOP_K = 2
        LN_EPS = 1e-05
        B, S, D = x.shape
        N = B * S
        xt = x.reshape(N, D)
        logits = xt @ Wr + br
        probs = jax.nn.softmax(logits, axis=-1)
        top_p, top_idx = jax.lax.top_k(probs, TOP_K)
        weights = top_p / top_p.sum(axis=-1, keepdims=True)
        mu = xt.mean(axis=-1, keepdims=True)
        var = ((xt - mu) ** 2).mean(axis=-1, keepdims=True)
        xn = (xt - mu) * jax.lax.rsqrt(var + LN_EPS)
        xe = xn[None, :, :] * ln_g[:, None, :] + ln_b[:, None, :]
        h = jax.nn.gelu(jnp.einsum('end,edh->enh', xe, W1) + b1[:, None, :], approximate=False)
        y = jnp.einsum('enh,ehd->end', h, W2) + b2[:, None, :]
        y_tok = jnp.transpose(y, (1, 0, 2))
        sel = jnp.take_along_axis(y_tok, top_idx[:, :, None], axis=1)
        out = (weights[:, :, None] * sel).sum(axis=1)
        return out.reshape(B, S, D)

    def _L2_gnn_ref(x, edge_index, W, att_src, att_dst, bias, ln_w, ln_b):
        import jax, jax.numpy as jnp
        import numpy as np
        N, D, H = (50000, 256, 8)
        C = D // H
        E = 50000
        NEG_SLOPE = 0.2
        EPS = 1e-05

        def _gat_block(x, src, dst, W, att_src, att_dst, bias, ln_w, ln_b):
            n = x.shape[0]
            h = (x @ W).reshape(n, H, C)
            a_src = jnp.einsum('nhc,hc->nh', h, att_src)
            a_dst = jnp.einsum('nhc,hc->nh', h, att_dst)
            e = a_src[src] + a_dst[dst]
            e = jnp.where(e > 0, e, NEG_SLOPE * e)
            m = jax.ops.segment_max(e, dst, num_segments=n)
            m = jnp.where(jnp.isfinite(m), m, 0.0)
            ex = jnp.exp(e - m[dst])
            denom = jax.ops.segment_sum(ex, dst, num_segments=n)
            alpha = ex / denom[dst]
            msg = h[src] * alpha[..., None]
            out = jax.ops.segment_sum(msg, dst, num_segments=n).reshape(n, H * C) + bias
            y = out + x
            mu = y.mean(axis=-1, keepdims=True)
            var = y.var(axis=-1, keepdims=True)
            return (y - mu) / jnp.sqrt(var + EPS) * ln_w + ln_b
        n = x.shape[0]
        loop = jnp.arange(n, dtype=edge_index.dtype)
        src = jnp.concatenate([edge_index[0], loop])
        dst = jnp.concatenate([edge_index[1], loop])
        return _gat_block(x, src, dst, W, att_src, att_dst, bias, ln_w, ln_b)

    def _L2_ffn_ref(x, Wr, br, W1, b1, W2, b2, gamma, beta):
        import math
        import jax, jax.numpy as jnp
        import numpy as np
        CAPACITY_FACTOR = 1.25
        TOP_K = 2
        LN_EPS = 1e-05

        def _layer_norm(x, gamma, beta):
            mu = jnp.mean(x, axis=-1, keepdims=True)
            var = jnp.var(x, axis=-1, keepdims=True)
            return (x - mu) * jax.lax.rsqrt(var + LN_EPS) * gamma + beta
        B, S, D = x.shape
        E = Wr.shape[1]
        N = B * S
        K = TOP_K
        logits = jnp.mean(x, axis=1) @ Wr + br
        routing_weights = jax.nn.softmax(logits, axis=-1)
        capacity = float(math.ceil(N * CAPACITY_FACTOR / E))
        expected_loads = routing_weights.sum(axis=0) * (N / B)
        scale = jnp.where(expected_loads > capacity, capacity / expected_loads, 1.0)
        routing_weights = jax.nn.softmax(routing_weights * scale, axis=-1)
        rw_tok = jnp.broadcast_to(routing_weights[:, None, :], (B, S, E)).reshape(N, E)
        top_w, top_i = jax.lax.top_k(rw_tok, K)
        top_w = jax.nn.softmax(top_w, axis=-1)
        xf = x.reshape(N, D)
        h = jax.nn.gelu(jnp.einsum('nd,edf->enf', xf, W1) + b1[:, None, :], approximate=False)
        y = jnp.einsum('enf,efd->end', h, W2) + b2[:, None, :]
        w_dense = jnp.zeros((N, E), x.dtype).at[jnp.arange(N)[:, None], top_i].add(top_w)
        out = jnp.einsum('ne,end->nd', w_dense, y).reshape(B, S, D)
        out = _layer_norm(out + x, gamma, beta)
        return out

    def _L3_gnn_ref(x, edge_index, w1, b1, gamma, beta, w2, b2, w_gcn, b_gcn):
        import jax, jax.numpy as jnp
        import numpy as np
        N_NODES = 50000
        N_EDGES = 25000
        D_IN = 256
        D_OUT = 256
        BN_EPS = 1e-05

        def _forward(x, edge_index, w1, b1, gamma, beta, w2, b2, w_gcn, b_gcn):
            n = x.shape[0]
            h = x @ w1.T + b1
            mean = jnp.mean(h, axis=0)
            var = jnp.var(h, axis=0)
            h = (h - mean) * jax.lax.rsqrt(var + BN_EPS) * gamma + beta
            h = jax.nn.relu(h)
            h = h @ w2.T + b2
            xw = h @ w_gcn.T
            src = jnp.concatenate([edge_index[0], jnp.arange(n, dtype=edge_index.dtype)])
            dst = jnp.concatenate([edge_index[1], jnp.arange(n, dtype=edge_index.dtype)])
            deg = jax.ops.segment_sum(jnp.ones_like(dst, dtype=xw.dtype), dst, num_segments=n)
            dinv = jnp.where(deg > 0, jax.lax.rsqrt(jnp.maximum(deg, 1.0)), 0.0)
            norm = dinv[src] * dinv[dst]
            msgs = xw[src] * norm[:, None]
            out = jax.ops.segment_sum(msgs, dst, num_segments=n) + b_gcn
            return out
        return _forward(x, edge_index, w1, b1, gamma, beta, w2, b2, w_gcn, b_gcn)

    def _L3_ffn_ref(x, router_w, w1, w2, w3):
        import jax, jax.numpy as jnp
        import numpy as np
        N_EXPERTS = 8
        TOP_K = 2
        B, T, C = x.shape
        flat = x.reshape(-1, C)
        logits = flat @ router_w.T
        probs = jax.nn.softmax(logits, axis=-1)
        topk_probs, topk_idx = jax.lax.top_k(probs, TOP_K)
        topk_probs = topk_probs / (jnp.sum(topk_probs, axis=-1, keepdims=True) + 1e-09)
        onehot = jax.nn.one_hot(topk_idx, N_EXPERTS, dtype=flat.dtype)
        gates = jnp.einsum('nk,nke->ne', topk_probs, onehot)
        h1 = jnp.einsum('nc,ehc->neh', flat, w1)
        h3 = jnp.einsum('nc,ehc->neh', flat, w3)
        h = jax.nn.silu(h1) * h3
        y = jnp.einsum('neh,ech->nec', h, w2)
        out = jnp.einsum('ne,nec->nc', gates, y)
        return out.reshape(B, T, C)
    edge_index = jnp.stack([src, dst])
    x = x + _L0_gnn_ref(_layernorm(x, axis=-1), edge_index, L0_gnn_Wq, L0_gnn_bq, L0_gnn_Wk, L0_gnn_bk, L0_gnn_Wv, L0_gnn_bv, L0_gnn_Ws, L0_gnn_bs, L0_gnn_bn_gamma, L0_gnn_bn_beta)
    x = x + _L0_ffn_ref(_layernorm(x, axis=-1)[None], L0_ffn_Wg, L0_ffn_bg, L0_ffn_W1, L0_ffn_b1, L0_ffn_W2, L0_ffn_b2)[0]
    x = x + _L1_gnn_ref(_layernorm(x, axis=-1), L1_gnn_W, L1_gnn_att, src, dst)
    x = x + _L1_ffn_ref(_layernorm(x, axis=-1)[None], L1_ffn_Wr, L1_ffn_br, L1_ffn_ln_g, L1_ffn_ln_b, L1_ffn_W1, L1_ffn_b1, L1_ffn_W2, L1_ffn_b2)[0]
    x = x + _L2_gnn_ref(_layernorm(x, axis=-1), edge_index, L2_gnn_W, L2_gnn_att_src, L2_gnn_att_dst, L2_gnn_bias, L2_gnn_ln_w, L2_gnn_ln_b)
    x = x + _L2_ffn_ref(_layernorm(x, axis=-1)[None], L2_ffn_Wr, L2_ffn_br, L2_ffn_W1, L2_ffn_b1, L2_ffn_W2, L2_ffn_b2, L2_ffn_gamma, L2_ffn_beta)[0]
    x = x + _L3_gnn_ref(_layernorm(x, axis=-1), edge_index, L3_gnn_w1, L3_gnn_b1, L3_gnn_gamma, L3_gnn_beta, L3_gnn_w2, L3_gnn_b2, L3_gnn_w_gcn, L3_gnn_b_gcn)
    x = x + _L3_ffn_ref(_layernorm(x, axis=-1)[None], L3_ffn_router_w, L3_ffn_w1, L3_ffn_w2, L3_ffn_w3)[0]
    return x

_drawn_inputs = setup_inputs


def setup_inputs(seed=0):
    import zlib

    import numpy as np

    out = dict(_drawn_inputs(seed))
    spreads = {'L0_ffn_bg': (0.0, 0.1),
     'L0_ffn_b1': (0.0, 0.1),
     'L0_ffn_b2': (0.0, 0.1),
     'L1_ffn_br': (0.0, 0.1),
     'L1_ffn_ln_g': (1.0, 0.2),
     'L1_ffn_ln_b': (0.0, 0.1),
     'L1_ffn_b1': (0.0, 0.1),
     'L1_ffn_b2': (0.0, 0.1),
     'L2_gnn_bias': (0.0, 0.1),
     'L2_gnn_ln_w': (1.0, 0.2),
     'L2_gnn_ln_b': (0.0, 0.1),
     'L2_ffn_br': (0.0, 0.1),
     'L2_ffn_b1': (0.0, 0.465),
     'L2_ffn_b2': (0.0, 0.359),
     'L2_ffn_gamma': (1.0, 0.2),
     'L2_ffn_beta': (0.0, 0.1),
     'L3_gnn_gamma': (1.0, 0.6),
     'L3_gnn_beta': (0.0, 0.8),
     'L3_gnn_b_gcn': (0.0, 0.1)}
    factors = {'L0_gnn_bq': 3.601,
     'L0_gnn_bk': 8.0,
     'L2_gnn_att_src': 2.875,
     'L2_gnn_att_dst': 5.39,
     'L3_gnn_w1': 4.467,
     'L3_gnn_b1': 8.0,
     'L3_gnn_b2': 6.455}
    for name, (base, spread) in spreads.items():
        noise = np.random.default_rng([zlib.crc32(name.encode()), seed]).standard_normal(out[name].shape)
        drawn = base * np.exp(spread * noise) if base else spread * noise
        out[name] = jnp.asarray(drawn.astype(out[name].dtype))
    for name, factor in factors.items():
        out[name] = (out[name] * factor).astype(out[name].dtype)
    return out
```

```python
from contextlib import ExitStack

import concourse.bass as bass
import concourse.mybir as mybir

F32 = mybir.dt.float32
F16 = mybir.dt.float16
I32 = mybir.dt.int32
U32 = mybir.dt.uint32
ALU = mybir.AluOpType
ACT = mybir.ActivationFunctionType
AX = mybir.AxisListType

N, D, EDGES = 625, 256, 20000
R, T = 125, 5
P, KC = 128, D // 128
SPLITS = [(0, 512), (512, N - 512)]
HALF = 313
FIELD = 12
PER_BLOCK, BLOCKS, GROUPS = R, EDGES // R, 5
GROUP = BLOCKS // GROUPS
RING = 4
NEVER = -1.0e30
FLOOR = -1.0e29
EXPERTS = 8
LAYERS = 3
EPS = 1e-5
HID01, HID2 = [128] * 8, [128] * 4
HID3 = [128] * 5 + [682 - 640]

V = {}
_at = 0
for _name, _n in [("bq", 6), ("bk", 6), ("bn_g", 4), ("bn_b", 4), ("l0_b1", 64), ("l1_b1", 64), ("l1_g", 16),
                  ("l1_b", 16), ("l1_as", 2), ("l1_ad", 2), ("l2_as", 2), ("l2_ad", 2), ("l3_b1", 2),
                  ("l3_g", 2), ("l3_b", 2), ("l3_b2", 2)]:
    V[_name] = _at
    _at += _n
NV = _at
W = {}
_at = 0
for _name, _n in [("bvs", 3 * 512), ("bg", 8), ("br1", 8), ("br2", 8), ("bias2", D), ("ln_w", D), ("ln_b", D),
                  ("gamma", D), ("beta", D), ("b_gcn", D)]:
    W[_name] = _at
    _at += _n
NW = _at


class Steps:

    def __init__(self, eng, sem):
        self.eng, self.sem, self.base, self.n = eng, sem, 0, 0

    def step(self, ins):
        ins.then_inc(self.sem, 1)
        self.n += 1

    def wait(self):
        self.eng.wait_ge(self.sem, self.base + self.n)

    def enter(self, i, per):
        self.base0, self.n0 = self.base, self.n
        self.base, self.n = self.base + self.n + i * per, 0

    def leave(self, count, per):
        assert self.n == per, self.n
        self.base, self.n = self.base0, self.n0 + count * per


def graph_network(nc, a, out):
    with ExitStack() as ctx:
        def sb(name, shape, dt=F32):
            return ctx.enter_context(nc.sbuf_tensor(name, shape, dt))

        def sem(name):
            return ctx.enter_context(nc.semaphore(name))

        X = sb("X", [R, T, D])
        Z = sb("Z", [R, T, D])
        XT = sb("XT", [P, KC, N])
        QT = sb("QT", [P, KC, N])
        KT = sb("KT", [P, KC, N])
        XE = [KT, sb("XE1", [P, KC, N])]
        VS = sb("VS", [R, T, 2 * D])
        HT = sb("HT", [P, 8, N])
        C = sb("C", [R, T, 2 * HALF])
        LNC = sb("LNC", [R, T, 2 * HALF])
        LNC2 = sb("LNC2", [R, T, 2 * HALF])
        CT = sb("CT", [R, T, N])
        WA = [sb(f"WA{s}", [P, 2 * KC * 682]) for s in range(2)]
        WB = [sb(f"WB{s}", [P, 8 * D]) for s in range(2)]
        GQK = sb("GQK", [P, 2, KC, D])
        GVS = sb("GVS", [P, KC, 2 * D])
        B1S = sb("B1S", [P, 2, 4])
        vec = sb("vec", [P, NV])
        bq8 = sb("bq8", [P, 6])
        rows = sb("rows", [R, NW])
        wr = sb("wr", [P, 4, KC, EXPERTS])
        b2 = sb("b2", [EXPERTS, 3, D])
        src_i = sb("src_i", [R, BLOCKS], I32)
        dst_i = sb("dst_i", [R, BLOCKS], I32)
        src_f = sb("src_f", [R, BLOCKS])
        dst_f = sb("dst_f", [R, BLOCKS])
        src_field = sb("src_field", [R, BLOCKS])
        src_lo = sb("src_lo", [R, BLOCKS])
        src_val = sb("src_val", [R, BLOCKS])
        iota_h = sb("iota_h", [R, N], F16)
        iota8 = sb("iota8", [R, T, EXPERTS])
        ident = sb("ident", [P, P])
        mean_of = sb("mean_of", [R, R])
        half = sb("half", [P, 8])
        SG = sb("SG", [P, 2, N])
        OHD = SG[0:R, :, :].bitcast(F16).rearrange("p a (b n) -> p (a b) n", n=N)
        OHS = sb("OHS", [R, RING, HALF], F16)
        CI = VS[:, :, 0:HALF].bitcast(I32)
        CF = HT[0:R, 0:T, 0:HALF].bitcast(I32)
        SM = sb("SM", [R, 2, N])
        PR = sb("PR", [R, 2, N])
        PT = sb("PT", [R, 2, T, R])
        T1, T2 = XE[1][0:R, 0, :], XE[1][0:R, 1, :]
        mx = sb("mx", [R, 2])
        nmx = sb("nmx", [R, 2])
        den = sb("den", [R, T, 8])
        rden = sb("rden", [R, T, 8])
        ON = sb("ON", [R, D])
        AB = sb("AB", [P, KC, R])
        AD = sb("AD", [P, KC, 8])
        ED = sb("ED", [R, T, 8])
        ST = sb("ST", [R, T, 6])
        MV = sb("MV", [R, T, 2])
        VE = sb("VE", [R, 8])
        RS = sb("RS", [R, 8])
        FST = sb("FST", [P, KC, 2, 6])
        FMV = sb("FMV", [P, KC, 2])
        FVE = sb("FVE", [P, KC])
        FRS = sb("FRS", [P, KC])
        FSC = sb("FSC", [P, KC])
        FBI = sb("FBI", [P, KC])
        LG = sb("LG", [R, T, EXPERTS])
        LX = sb("LX", [R, T, EXPERTS])
        LE = sb("LE", [R, T, EXPERTS])
        M8 = sb("M8", [R, T, 8])
        I8 = sb("I8", [R, T, 8], U32)
        IF = sb("IF", [R, T, 2])
        E2 = sb("E2", [R, T])
        ZS = sb("ZS", [R, T])
        TW = sb("TW", [R, T, 2])
        OH0 = sb("OH0", [R, T, EXPERTS])
        WD = sb("WD", [R, T, EXPERTS])
        WT = sb("WT", [EXPERTS, T, R])
        deg = sb("deg", [R, T])
        dinv = sb("dinv", [R, T])

        PS = ctx.enter_context(nc.psum_tensor("PS", [P, 8, 512], F32))
        flat = PS[:, :, :].rearrange("p b n -> p (b n)")
        H = [flat[:, 0:1024], flat[:, 1024:2048]]
        H5 = [h.rearrange("p (s n) -> p s n", n=128) for h in H]
        Y = [PS[:, 4, :], PS[:, 5, :]]
        G5 = flat[:, 3072:4096].rearrange("p (s n) -> p s n", n=128)
        G0, G1 = PS[:, 6, :], PS[:, 7, :]

        waits_taken = sem("waits_taken")
        in_edges = sem("in_edges")
        in_x = sem("in_x")
        in_small = sem("in_small")
        in_graph_w = sem("in_graph_w")
        in_WA = [sem(f"in_WA{s}") for s in range(2)]
        in_WB = [sem(f"in_WB{s}") for s in range(2)]
        WA_free = sem("WA_free")
        WB_free = sem("WB_free")
        consts = sem("consts")
        vec_step = sem("vec_step")
        act_step = sem("act_step")
        pool_step = sem("pool_step")
        onehot_ready = sem("onehot_ready")
        onehot_free = sem("onehot_free")
        counts_free = sem("counts_free")
        count_all = sem("count_all")
        lnc_in = sem("lnc_in")
        lnc_ln = sem("lnc_ln")
        count_turned = sem("count_turned")
        ct_copied = sem("ct_copied")
        ln_var = sem("ln_var")
        ln_rstd = sem("ln_rstd")
        ln_out = sem("ln_out")
        bn_var = sem("bn_var")
        bn_rstd = sem("bn_rstd")
        bn_affine = sem("bn_affine")
        turned = sem("turned")
        xt_ready = sem("xt_ready")
        qk_ready = sem("qk_ready")
        qk_done = sem("qk_done")
        vs_ready = sem("vs_ready")
        vs_done = sem("vs_done")
        ab_ready = sem("ab_ready")
        ed_ready = sem("ed_ready")
        es_ready = sem("es_ready")
        es_done = sem("es_done")
        score_ready = sem("score_ready")
        masked = sem("masked")
        negmax = sem("negmax")
        prob = sem("prob")
        prob_turned = sem("prob_turned")
        probT = sem("probT")
        mixed = sem("mixed")
        tile_out = sem("tile_out")
        logits = sem("logits")
        logits_sb = sem("logits_sb")
        mean_logits = sem("mean_logits")
        route_arg = sem("route_arg")
        route_exp = sem("route_exp")
        routed = sem("routed")
        picked = sem("picked")
        wt_ready = sem("wt_ready")
        wt_done = sem("wt_done")
        h_ready = sem("h_ready")
        h_free = sem("h_free")
        h1_ready = sem("h1_ready")
        h1_free = sem("h1_free")
        h3_ready = sem("h3_ready")
        h3_free = sem("h3_free")
        y_ready = sem("y_ready")
        y_free = sem("y_free")
        xe_ready = sem("xe_ready")
        xe_free = sem("xe_free")
        in_sel = sem("in_sel")
        x_ready = sem("x_ready")
        out_sent = sem("out_sent")

        def vcol(name, k=0, n=1):
            return vec[:, V[name] + k:V[name] + k + n]

        def row(name, n, k=0):
            return rows[:, W[name] + k:W[name] + k + n]

        def over_tiles(ap, n):
            return ap.unsqueeze(1).broadcast_to([R, T, n])

        LN = {k: i for i, k in enumerate(["l0g", "l0f", "l1g", "l1f", "l1n", "l2g", "l2o", "l2f", "l2p", "l3g", "l3f"])}
        TURN = {k: i for i, k in enumerate(["l0_0", "l0_1", "l0_2", "l0f", "l1g", "l1f", "l1n", "l2g", "l2f", "l3g", "l3f"])}
        ROUTE = {"l0": 0, "l1": 1, "l2": 2, "l3": 3}
        UNITS = {"l1": 60, "l2": 80}
        TILES = {"l1": 15, "l2": 20}
        HBASE = {"l0": 0, "l1": 64, "l2": 128}
        YBASE = {"l0": 0, "l1": 45, "l2": 90, "l3": 105}
        EBASE = {"l0": 0, "l1": 8, "l2": 16, "l3": 18}
        HEADS = {"l0": 4, "l1": 4, "l2": 8}

        block = ctx.enter_context(nc.Block())

        @block.sync
        def _(sp):
            sp.dma_start(src_i[:, :], a["src"]).then_inc(in_edges, 16)
            sp.dma_start(dst_i[:, :], a["dst"]).then_inc(in_edges, 16)
            sp.dma_start(X[:, :, :], a["x"]).then_inc(in_x, 16)

            def experts(w1, w2, base, n1, n2):
                with sp.Fori(0, EXPERTS // 2) as i:
                    for s in range(2):
                        e = 2 * i + s
                        sp.wait_ge(WA_free, e + (base + 1))
                        sp.dma_start(WA[s][:, 0:n1], w1[e]).then_inc(in_WA[s], 16)
                        sp.wait_ge(WB_free, e + (base + 1))
                        if n2 == len(HID3) * D:
                            sp.dma_start(WB[s][:, 0:5 * D], w2[e, :, 0:5 * D]).then_inc(in_WB[s], 16)
                            sp.dma_start(WB[s][0:HID3[5], 5 * D:6 * D], w2[e, 0:HID3[5], 5 * D:6 * D])\
                              .then_inc(in_WB[s], 16)
                        else:
                            sp.dma_start(WB[s][:, 0:n2], w2[e]).then_inc(in_WB[s], 16)

            experts(a["l0_w1"], a["l0_w2"], EBASE["l0"], 2048, 2048)
            experts(a["l1_w1"], a["l1_w2"], EBASE["l1"], 2048, 2048)
            sp.wait_ge(picked, 1)
            for k in range(2):
                e = sp.value_load(I8[0:1, 0, k:k + 1], min_val=0, max_val=EXPERTS - 1)
                sp.wait_ge(WA_free, EBASE["l2"] + k + 1)
                sp.dma_start(WA[k][:, 0:1024], a["l2_w1"][e]).then_inc(in_WA[k], 16)
                sp.wait_ge(WB_free, EBASE["l2"] + k + 1)
                sp.dma_start(WB[k][:, 0:1024], a["l2_w2"][e]).then_inc(in_WB[k], 16)
                sp.dma_start(B1S[:, k, :], a["l2_b1"][e]).then_inc(in_sel, 16)
            experts(a["l3_w13"], a["l3_w2"], EBASE["l3"], 2 * KC * 682, len(HID3) * D)
            sp.wait_ge(x_ready, 1)
            sp.dma_start(out, X[:, :, :]).then_inc(out_sent, 16)
            sp.wait_ge(out_sent, 16)

        @block.gpsimd
        def _(pool):
            own = Steps(pool, pool_step)
            pool.dma_start(vec[:, :], a["vec"]).then_inc(in_small, 16)
            pool.dma_start(rows[:, :], a["rows"].partition_broadcast(R)).then_inc(in_small, 16)
            pool.dma_start(wr[:, :, :, :], a["wr"]).then_inc(in_small, 16)
            pool.dma_start(b2[:, :, :], a["b2"]).then_inc(in_small, 16)

            pool.iota(iota_h[:, :], [[1, N]], base=0, channel_multiplier=0, allow_small_or_imprecise_dtypes=True)\
                .then_inc(consts, 1)
            pool.iota(iota8[:, :, :], [[0, T], [1, EXPERTS]], base=0, channel_multiplier=0,
                      allow_small_or_imprecise_dtypes=True).then_inc(consts, 1)
            pool.memset(half[:, :], -0.5).then_inc(consts, 1)
            pool.memset(mean_of[:, :], 1.0 / N).then_inc(consts, 1)
            own.step(pool.memset(ident[:, :], 0.0))
            own.wait()
            pool.affine_select(out=ident[:, :], in_=ident[:, :], compare_op=ALU.not_equal, fill=1.0, base=0,
                               pattern=[[-1, P]], channel_multiplier=1).then_inc(consts, 1)

            def layer_weights(i):
                pool.dma_start(GQK[:, :, :, :], a["l0_wqk"][i]).then_inc(in_graph_w, 16)
                pool.dma_start(GVS[:, :, :], a["l0_wvs"][i]).then_inc(in_graph_w, 16)

            def power(out_, in_, n, wait, value, done):
                pool.wait_ge(wait, value)
                nc.gpsimd.tensor_tensor(out_, in_, half[0:n, 0:in_.shape[1]], ALU.pow).then_inc(done, 1)

            def ln_power(name):
                power(RS[:, 0:T], VE[:, 0:T], R, ln_var, LN[name] + 1, ln_rstd)

            layer_weights(0)
            pool.wait_ge(consts, 5)
            ln_power("l0g")
            with pool.Fori(0, LAYERS - 1) as i:
                pool.wait_ge(vs_ready, i * T + T)
                layer_weights(i + 1)
                power(FRS[:, :], FVE[:, :], P, bn_var, i + 1, bn_rstd)
            pool.wait_ge(vs_ready, LAYERS * T)
            pool.dma_start(GQK[:, 0, :, :], a["l1_w"]).then_inc(in_graph_w, 16)
            ln_power("l0f")
            ln_power("l1g")
            pool.wait_ge(qk_ready, 4 * LAYERS + 2)
            pool.dma_start(GQK[:, 1, :, :], a["l2_w"]).then_inc(in_graph_w, 16)
            pool.dma_start(GVS[:, :, 0:D], a["l3_wg"]).then_inc(in_graph_w, 16)
            for name in ["l1f", "l1n", "l2g", "l2o", "l2f", "l2p"]:
                ln_power(name)
            pool.dma_start(GQK[:, :, :, :], a["l3_w"]).then_inc(in_graph_w, 16)
            ln_power("l3g")
            power(FRS[:, :], FVE[:, :], P, bn_var, LAYERS, bn_rstd)
            power(dinv[:, :], deg[:, :], R, bn_affine, LAYERS, bn_rstd)
            ln_power("l3f")

        @block.tensor
        def _(pe):
            def turn(src, n, wait, value):
                pe.wait_ge(wait, value)
                for c in range(KC):
                    for t in range(T):
                        last = pe.transpose(H5[c][:, t, 0:R], src[:, t, c * 128:(c + 1) * 128], ident[0:R, 0:R])
                    last.then_inc(turned, 1)

            def wide(slot, lhs, rhs, rows_out, done):
                for lo, w in SPLITS:
                    for c in range(len(lhs)):
                        last = pe.matmul(slot[0:rows_out, lo:lo + w], lhs[c], rhs[c][:, lo:lo + w],
                                         start=(c == 0), stop=(c == len(lhs) - 1))
                last.then_inc(done, 1)

            pe.sem_inc(onehot_free, RING)
            pe.sem_inc(WA_free, 2)
            pe.sem_inc(WB_free, 2)
            with pe.Fori(0, GROUPS) as g:
                pe.wait_ge(counts_free, g + 1)
                for b in range(GROUP):
                    pe.wait_ge(onehot_ready, g * GROUP + (b + 1))
                    for t in range(T):
                        last = pe.matmul(PS[0:R, t, 0:HALF], OHD[:, b % RING, t * R:(t + 1) * R],
                                         OHS[:, b % RING, :], start=(b == 0), stop=(b == GROUP - 1))
                    last.then_inc(onehot_free, 1)

            pe.wait_ge(count_all, 1)
            pe.wait_ge(consts, 5)
            for t in range(T):
                if t >= 2:
                    pe.wait_ge(ct_copied, t - 1)
                for s in range(T):
                    last = pe.transpose(H5[t % 2][0:R, s, 0:R], C[:, t, s * R:(s + 1) * R], ident[0:R, 0:R])
                last.then_inc(count_turned, 1)
            pe.wait_ge(ct_copied, T)

            def attention(ubase, tbase, heads, dh, scored):
                units = T * heads

                def score(k):
                    t, h = divmod(k, heads)
                    if k >= 2:
                        pe.wait_ge(masked, ubase + (k - 1))
                    r = slice(dh * (h % 2), dh * (h % 2) + dh)
                    for lo, w in SPLITS:
                        last = pe.matmul(H[k % 2][0:R, lo:lo + w], QT[r, h // 2, t * R:(t + 1) * R],
                                         KT[r, h // 2, lo:lo + w], start=True, stop=True)
                    last.then_inc(score_ready, 1)

                def turn_probs(k):
                    pe.wait_ge(prob, ubase + (k + 1))
                    if k >= 1:
                        pe.wait_ge(probT, ubase + k)
                    for s in range(T):
                        last = pe.transpose(G5[0:R, s, 0:R], PR[:, k % 2, s * R:(s + 1) * R], ident[0:R, 0:R])
                    last.then_inc(prob_turned, 1)

                def mix(k):
                    t, h = divmod(k, heads)
                    pe.wait_ge(probT, ubase + (k + 1))
                    if h == 0 and t >= 2:
                        pe.wait_ge(tile_out, tbase + (t - 1))
                    for s in range(T):
                        last = pe.matmul(Y[t % 2][0:R, h * dh:(h + 1) * dh], PT[:, k % 2, s, :],
                                         VS[:, s, h * dh:(h + 1) * dh], start=(s == 0), stop=(s == T - 1))
                    last.then_inc(mixed, 1)

                for k in range(units + 2):
                    if scored and k < units:
                        score(k)
                    if 1 <= k <= units:
                        turn_probs(k - 1)
                    if k >= 2:
                        mix(k - 2)

            def l0_layer(i):
                pe.wait_ge(xt_ready, 2 * i + 2)
                pe.wait_ge(in_graph_w, 32 * i + 32)
                for j in range(4):
                    if j >= 2:
                        pe.wait_ge(qk_done, 4 * i + (j - 1))
                    q, m = divmod(j, 2)
                    wide(H[j % 2], [GQK[:, q, c, m * 128:(m + 1) * 128] for c in range(KC)],
                         [XT[:, c, :] for c in range(KC)], P, qk_ready)
                for t in range(T):
                    if t >= 2:
                        pe.wait_ge(vs_done, T * i + (t - 1))
                    for c in range(KC):
                        last = pe.matmul(Y[t % 2][0:R, :], XT[:, c, t * R:(t + 1) * R], GVS[:, c, :],
                                         start=(c == 0), stop=(c == KC - 1))
                    last.then_inc(vs_ready, 1)
                pe.wait_ge(qk_done, 4 * i + 4)
                pe.wait_ge(vs_done, T * i + T)
                attention(20 * i, T * i, 4, 64, True)

            turn(Z, 0, ln_out, LN["l0g"] + 1)
            with pe.Fori(0, LAYERS - 1) as i:
                l0_layer(i)
                turn(Z, i + 1, tile_out, T * i + T)
            l0_layer(LAYERS - 1)

            def route(k, n):
                pe.wait_ge(xt_ready, 2 * n + 2)
                pe.wait_ge(in_small, 64)
                for t in range(T):
                    for c in range(KC):
                        last = pe.matmul(G1[0:R, t * 8:t * 8 + 8], XT[:, c, t * R:(t + 1) * R], wr[:, k, c, :],
                                         start=(c == 0), stop=(c == KC - 1))
                last.then_inc(logits, 1)

            def experts(name, i, s, xin, hid, n1, per_slot16):
                e = 2 * i + s
                g = e + EBASE[name]
                nh = len(hid)
                pe.wait_ge(in_WA[s], 16 * i + (16 * (EBASE[name] // 2 + 1)))
                for m in range(nh):
                    idx = nh * e + (HBASE[name] + m)
                    pe.wait_ge(h_free, idx + 1)
                    wide(H[m % 2], [WA[s][:, c * n1 + m * 128:c * n1 + (m + 1) * 128] for c in range(KC)],
                         [xin[:, c, :] for c in range(KC)], P, h_ready)
                pe.wait_ge(in_WB[s], 16 * i + (16 * (EBASE[name] // 2 + 1)))
                for t in range(T):
                    idx = T * e + (YBASE[name] + t)
                    pe.wait_ge(y_free, idx + 1)
                    for m in range(nh):
                        if t == 0:
                            pe.wait_ge(h_free, nh * e + (HBASE[name] + m + 3))
                        last = pe.matmul(Y[(YBASE[name] + T * s + t) % 2][0:R, 0:D], HT[:, m, t * R:(t + 1) * R],
                                         WB[s][:, m * D:(m + 1) * D], start=(m == 0), stop=(m == nh - 1))
                    last.then_inc(y_ready, 1)
                pe.wait_ge(y_ready, T * e + (YBASE[name] + T))
                pe.sem_inc(WA_free, 1)
                pe.sem_inc(WB_free, 1)

            def bias2(k, name, ybase):
                pe.wait_ge(routed, k + 1)
                for t in range(T):
                    last = pe.transpose(G5[0:EXPERTS, t, 0:R], WD[:, t, :], ident[0:R, 0:R])
                last.then_inc(wt_ready, 1)
                pe.wait_ge(wt_done, k + 1)
                for t in range(T):
                    pe.wait_ge(y_free, ybase + t + 1)
                    pe.matmul(Y[(ybase + t) % 2][0:R, 0:D], WT[:, t, :], b2[:, k, :], start=True, stop=True)\
                      .then_inc(y_ready, 1)

            turn(Z, TURN["l0f"], ln_out, LN["l0f"] + 1)
            route(0, TURN["l0f"])
            with pe.Fori(0, EXPERTS // 2) as i:
                for s in range(2):
                    experts("l0", i, s, XT, HID01, 1024, 0)
            bias2(0, "l0", YBASE["l0"] + T * EXPERTS)

            def gat(name, n, w, wload, qbase, vbase, esbase):
                heads = HEADS[name]
                dh = D // heads
                pe.wait_ge(xt_ready, 2 * n + 2)
                pe.wait_ge(in_graph_w, wload)
                for t in range(T):
                    if t >= 2:
                        pe.wait_ge(vs_done, vbase + t - 1)
                    for c in range(KC):
                        last = pe.matmul(Y[t % 2][0:R, 0:D], XT[:, c, t * R:(t + 1) * R], w[:, c, :],
                                         start=(c == 0), stop=(c == KC - 1))
                    last.then_inc(vs_ready, 1)
                for m in range(KC):
                    wide(H[m], [w[:, c, m * 128:(m + 1) * 128] for c in range(KC)],
                         [XT[:, c, :] for c in range(KC)], P, qk_ready)
                pe.wait_ge(qk_done, qbase + 2)
                k = {"l1": 0, "l2": 1}[name]
                pe.wait_ge(ab_ready, k + 1)
                for t in range(T):
                    for c in range(KC):
                        last = pe.matmul(G1[0:R, t * 8:t * 8 + heads], QT[:, c, t * R:(t + 1) * R],
                                         AD[:, c, 0:heads], start=(c == 0), stop=(c == KC - 1))
                last.then_inc(ed_ready, 1)
                per = P // dh
                for h in range(heads):
                    if h >= 2:
                        pe.wait_ge(es_done, esbase + h - 1)
                    r = slice(dh * (h % per), dh * (h % per) + dh)
                    wide(H[h % 2], [AB[r, h // per, :]], [QT[r, h // per, :]], R, es_ready)
                pe.wait_ge(vs_done, vbase + T)
                attention(UNITS[name], TILES[name], heads, dh, False)

            turn(Z, TURN["l1g"], ln_out, LN["l1g"] + 1)
            gat("l1", TURN["l1g"], GQK[:, 0, :, :], 112, 12, 15, 0)

            turn(Z, TURN["l1f"], ln_out, LN["l1f"] + 1)
            route(1, TURN["l1f"])
            pe.wait_ge(xt_ready, 2 * TURN["l1f"] + 2)
            turn(VS[:, :, 0:D], TURN["l1n"], ln_out, LN["l1n"] + 1)
            with pe.Fori(0, EXPERTS // 2) as i:
                for s in range(2):
                    pe.wait_ge(xe_ready, 2 * i + (s + 1))
                    experts("l1", i, s, XE[s], HID01, 1024, 0)
            bias2(1, "l1", YBASE["l1"] + T * EXPERTS)

            turn(Z, TURN["l2g"], ln_out, LN["l2g"] + 1)
            gat("l2", TURN["l2g"], GQK[:, 1, :, :], 144, 14, 20, 4)

            turn(Z, TURN["l2f"], ln_out, LN["l2f"] + 1)
            route(2, TURN["l2f"])
            pe.wait_ge(logits_sb, 1)
            for t in range(T):
                last = pe.matmul(G0[0:R, 0:8], mean_of[:, :], LG[:, t, :], start=(t == 0), stop=(t == T - 1))
            last.then_inc(mean_logits, 1)
            for s in range(2):
                experts("l2", 0, s, XT, HID2, 512, 0)
            bias2(2, "l2", YBASE["l2"] + 2 * T)

            turn(Z, TURN["l3g"], ln_out, LN["l3g"] + 1)
            pe.wait_ge(xt_ready, 2 * TURN["l3g"] + 2)
            pe.wait_ge(in_graph_w, 160)
            for m in range(KC):
                wide(H[m], [GQK[:, 0, c, m * 128:(m + 1) * 128] for c in range(KC)],
                     [XT[:, c, :] for c in range(KC)], P, qk_ready)
            pe.wait_ge(qk_done, 16 + 2)
            pe.wait_ge(es_done, 12 + 2)
            for m in range(KC):
                wide(H[m], [GQK[:, 1, c, m * 128:(m + 1) * 128] for c in range(KC)],
                     [KT[:, c, :] for c in range(KC)], P, qk_ready)
            pe.wait_ge(qk_done, 18 + 2)
            for t in range(T):
                if t >= 2:
                    pe.wait_ge(vs_done, 25 + t - 1)
                for c in range(KC):
                    last = pe.matmul(Y[t % 2][0:R, 0:D], QT[:, c, t * R:(t + 1) * R], GVS[:, c, 0:D],
                                     start=(c == 0), stop=(c == KC - 1))
                last.then_inc(vs_ready, 1)
            pe.wait_ge(vs_done, 25 + T)
            for t in range(T):
                if t >= 2:
                    pe.wait_ge(tile_out, 25 + t - 1)
                for s in range(T):
                    last = pe.matmul(Y[t % 2][0:R, 0:D], CT[:, s, t * R:(t + 1) * R], VS[:, s, 0:D],
                                     start=(s == 0), stop=(s == T - 1))
                last.then_inc(mixed, 1)

            turn(Z, TURN["l3f"], ln_out, LN["l3f"] + 1)
            route(3, TURN["l3f"])
            nh = len(HID3)
            with pe.Fori(0, EXPERTS // 2) as i:
                for s in range(2):
                    e = 2 * i + s
                    pe.wait_ge(in_WA[s], 16 * i + 16 * (EBASE["l3"] // 2 + 1))
                    for m, w in enumerate(HID3):
                        idx = nh * e + m
                        for j, (free, ready) in enumerate([(h1_free, h1_ready), (h3_free, h3_ready)]):
                            pe.wait_ge(free, idx + (j + 1))
                            wide(H[j], [WA[s][:, (2 * j + c) * 682 + m * 128:(2 * j + c) * 682 + m * 128 + w]
                                        for c in range(KC)], [XT[:, c, :] for c in range(KC)], w, ready)
                    pe.wait_ge(in_WB[s], 32 * i + (16 * (EBASE["l3"] // 2) + 32))
                    for t in range(T):
                        idx = T * e + (YBASE["l3"] + t)
                        pe.wait_ge(y_free, idx + 1)
                        for m, w in enumerate(HID3):
                            if t == 0:
                                pe.wait_ge(h3_free, nh * e + (m + 3))
                            last = pe.matmul(Y[(YBASE["l3"] + T * s + t) % 2][0:R, 0:D],
                                             HT[0:w, m, t * R:(t + 1) * R], WB[s][0:w, m * D:(m + 1) * D],
                                             start=(m == 0), stop=(m == nh - 1))
                        last.then_inc(y_ready, 1)
                    pe.wait_ge(y_ready, T * e + (YBASE["l3"] + T))
                    pe.sem_inc(WA_free, 1)
                    pe.sem_inc(WB_free, 1)

        @block.scalar
        def _(act):
            own = Steps(act, act_step)
            act.sem_inc(h_free, 2)
            act.sem_inc(h1_free, 1)
            act.wait_ge(in_small, 64)
            own.step(act.activation(bq8[:, :], vcol("bq", 0, 6), ACT.Copy, scale=0.125))
            for k, L in enumerate([LNC, LNC2]):
                act.wait_ge(lnc_in, k + 1)
                act.activation(L[:, :, :], L[:, :, :], ACT.Ln).then_inc(lnc_ln, 1)
            for t in range(T):
                act.wait_ge(count_turned, t + 1)
                act.activation(CT[:, :, t * R:(t + 1) * R], H5[t % 2][0:R, 0:T, 0:R], ACT.Copy).then_inc(ct_copied, 1)

            def turned_in(n, dst):
                for c in range(KC):
                    act.wait_ge(turned, 2 * n + (c + 1))
                    act.activation(dst[:, c, :].rearrange("p (t r) -> p t r", r=R), H5[c][:, 0:T, 0:R], ACT.Copy)\
                       .then_inc(xt_ready, 1)

            def normal_relu(n, dst, done):
                for c in range(KC):
                    act.activation(dst[:, c, :].rearrange("p (t r) -> p t r", r=R), H5[c][:, 0:T, 0:R], ACT.Relu,
                                   bias=FBI[:, c:c + 1], scale=FSC[:, c:c + 1]).then_inc(done, 1)

            def attention(ubase, tbase, heads):
                units = T * heads

                def exps(k):
                    t, h = divmod(k, heads)
                    act.wait_ge(negmax, ubase + (k + 1))
                    if k >= 2:
                        act.wait_ge(prob_turned, ubase + (k - 1))
                    act.activation(PR[:, k % 2, :], SM[:, k % 2, :], ACT.Exp, bias=nmx[:, k % 2:k % 2 + 1],
                                   accum_out=den[:, t, h:h + 1]).then_inc(prob, 1)

                def copy(k):
                    act.wait_ge(prob_turned, ubase + (k + 1))
                    if k >= 2:
                        act.wait_ge(mixed, ubase + (k - 1))
                    act.activation(PT[:, k % 2, :, :], G5[0:R, 0:T, 0:R], ACT.Copy).then_inc(probT, 1)

                for k in range(units + 1):
                    if k < units:
                        exps(k)
                    if k >= 1:
                        copy(k - 1)

            def l0_layer(i):
                for j in range(4):
                    q, m = divmod(j, 2)
                    act.wait_ge(qk_ready, 4 * i + (j + 1))
                    if q == 0:
                        act.activation(QT[:, m, :], H[j % 2][:, 0:N], ACT.Identity,
                                       bias=bq8[:, bass.ds(2 * i + m, 1)], scale=0.125).then_inc(qk_done, 1)
                    else:
                        act.activation(KT[:, m, :], H[j % 2][:, 0:N], ACT.Identity,
                                       bias=vec[:, bass.ds(2 * i + (V["bk"] + m), 1)]).then_inc(qk_done, 1)
                attention(20 * i, T * i, 4)

            own.wait()
            turned_in(0, XT)
            with act.Fori(0, LAYERS - 1) as i:
                l0_layer(i)
                act.wait_ge(bn_affine, i + 1)
                normal_relu(i + 1, XT, xt_ready)
            l0_layer(LAYERS - 1)

            def route(k):
                act.wait_ge(route_arg, k + 1)
                if k == 3:
                    act.activation(LE[:, :, :], LX[:, :, :], ACT.Exp).then_inc(route_exp, 1)
                else:
                    act.activation(E2[:, :], E2[:, :], ACT.Exp).then_inc(route_exp, 1)

            def gelus(name, i, s, hid, bias):
                nh = len(hid)
                for m in range(nh):
                    idx = nh * (2 * i + s) + (HBASE[name] + m)
                    act.wait_ge(h_ready, idx + 1)
                    act.activation(HT[:, m, :], H[m % 2][:, 0:N], ACT.Gelu, bias=bias(m)).then_inc(h_free, 1)

            turned_in(TURN["l0f"], XT)
            route(0)
            with act.Fori(0, EXPERTS // 2) as i:
                for s in range(2):
                    gelus("l0", i, s, HID01, lambda m: vec[:, bass.ds(16 * i + (V["l0_b1"] + 8 * s + m), 1)])

            def gat(name, n, qbase, esbase):
                turned_in(n, XT)
                for m in range(KC):
                    act.wait_ge(qk_ready, qbase + m + 1)
                    act.activation(QT[:, m, :], H[m][:, 0:N], ACT.Copy).then_inc(qk_done, 1)
                for h in range(HEADS[name]):
                    act.wait_ge(es_ready, esbase + h + 1)
                    act.activation(HT[0:R, h, :], H[h % 2][0:R, 0:N], ACT.Copy).then_inc(es_done, 1)
                attention(UNITS[name], TILES[name], HEADS[name])

            gat("l1", TURN["l1g"], 12, 0)
            turned_in(TURN["l1f"], XT)
            turned_in(TURN["l1n"], QT)
            route(1)
            with act.Fori(0, EXPERTS // 2) as i:
                for s in range(2):
                    gelus("l1", i, s, HID01, lambda m: vec[:, bass.ds(16 * i + (V["l1_b1"] + 8 * s + m), 1)])
            gat("l2", TURN["l2g"], 14, 4)
            turned_in(TURN["l2f"], XT)
            for j in range(2):
                act.wait_ge(route_arg, 3 + j)
                act.activation(LE[:, 0, :], LX[:, 0, :], ACT.Exp, accum_out=ZS[:, 0:1]).then_inc(route_exp, 1)
            act.wait_ge(route_arg, 5)
            act.activation(E2[:, 0:1], E2[:, 0:1], ACT.Exp).then_inc(route_exp, 1)
            act.wait_ge(in_sel, 32)
            for s in range(2):
                gelus("l2", 0, s, HID2, lambda m: B1S[:, s, m:m + 1])

            turned_in(TURN["l3g"], XT)
            for m in range(KC):
                act.wait_ge(qk_ready, 16 + m + 1)
                act.activation(QT[:, m, :], H[m][:, 0:N], ACT.Identity, bias=vcol("l3_b1", m)).then_inc(qk_done, 1)
            act.wait_ge(bn_affine, LAYERS + 1)
            for m in range(KC):
                act.activation(KT[:, m, :], QT[:, m, :], ACT.Relu, bias=FBI[:, m:m + 1], scale=FSC[:, m:m + 1])\
                   .then_inc(es_done, 1)
            for m in range(KC):
                act.wait_ge(qk_ready, 18 + m + 1)
                act.activation(QT[:, m, :], H[m][:, 0:N], ACT.Identity, bias=vcol("l3_b2", m)).then_inc(qk_done, 1)

            turned_in(TURN["l3f"], XT)
            act.wait_ge(route_arg, 6)
            act.activation(LE[:, :, :], LX[:, :, :], ACT.Exp).then_inc(route_exp, 1)
            nh = len(HID3)
            with act.Fori(0, EXPERTS // 2) as i:
                for s in range(2):
                    for m, w in enumerate(HID3):
                        idx = nh * (2 * i + s) + m
                        act.wait_ge(h1_ready, idx + 1)
                        act.wait_ge(h3_free, idx + 1)
                        act.activation(SG[0:w, m % 2, :], H[0][0:w, 0:N], ACT.Silu).then_inc(h1_free, 1)

        @block.vector
        def _(dve):
            own = Steps(dve, vec_step)
            v = nc.vector
            v.sem_inc(y_free, 2)
            v.sem_inc(h3_free, 2)
            v.sem_inc(counts_free, 1)
            v.sem_inc(xe_free, 2)

            dve.wait_ge(in_edges, 32)
            own.step(v.tensor_copy(src_f[:, :], src_i[:, :]))
            own.step(v.tensor_copy(dst_f[:, :], dst_i[:, :]))
            own.wait()
            own.step(v.tensor_scalar(src_field[:, :], src_f[:, :], float(HALF), None, ALU.is_ge))
            own.wait()
            own.step(v.scalar_tensor_tensor(src_lo[:, :], src_field[:, :], -float(HALF), src_f[:, :], ALU.mult, ALU.add))
            own.step(v.tensor_scalar(src_val[:, :], src_field[:, :], float(2 ** FIELD - 1), 1.0, ALU.mult, ALU.add))
            own.step(v.memset(C[:, :, :], 0.0))
            own.wait()
            dve.wait_ge(consts, 5)

            def normalise(name, src, dst):
                for t in range(T):
                    own.step(v.bn_stats(ST[:, t, :], src[:, t, :]))
                own.wait()
                for t in range(T):
                    own.step(v.bn_aggr(MV[:, t, :], ST[:, t, :]))
                own.wait()
                v.tensor_scalar(VE[:, 0:T], MV[:, :, 1], EPS, None, ALU.add).then_inc(ln_var, 1)
                dve.wait_ge(ln_rstd, LN[name] + 1)
                for t in range(T):
                    last = v.tensor_scalar(dst[:, t, :], src[:, t, :], MV[:, t, 0:1], RS[:, t:t + 1],
                                           ALU.subtract, ALU.mult)
                last.then_inc(ln_out, 1)

            dve.wait_ge(in_x, 16)
            normalise("l0g", X, Z)

            with dve.Fori(0, GROUPS) as g:
                own.enter(g, 4)
                for b in range(GROUP):
                    dve.wait_ge(onehot_free, g * GROUP + (b + 1))
                    v.tensor_scalar(OHD[:, b % RING, :], iota_h[:, :], dst_f[:, bass.ds(g * GROUP + b, 1)], None,
                                    ALU.is_equal)
                    v.tensor_scalar(OHS[:, b % RING, :], iota_h[:, 0:HALF], src_lo[:, bass.ds(g * GROUP + b, 1)],
                                    src_val[:, bass.ds(g * GROUP + b, 1)], ALU.is_equal, ALU.mult)\
                     .then_inc(onehot_ready, 1)
                dve.wait_ge(onehot_free, g * GROUP + (GROUP + RING))
                v.tensor_copy(CI, PS[0:R, 0:T, 0:HALF]).then_inc(counts_free, 1)
                dve.wait_ge(counts_free, g + 2)
                own.step(v.tensor_scalar(CF, CI, 2 ** FIELD - 1, None, ALU.bitwise_and))
                own.wait()
                own.step(v.tensor_tensor(C[:, :, 0:HALF], C[:, :, 0:HALF], CF, ALU.add))
                own.wait()
                own.step(v.tensor_scalar(CF, CI, FIELD, None, ALU.logical_shift_right))
                own.wait()
                own.step(v.tensor_tensor(C[:, :, HALF:2 * HALF], C[:, :, HALF:2 * HALF], CF, ALU.add))
                own.wait()
                own.leave(GROUPS, 4)

            own.step(v.tensor_reduce(deg[:, :], C[:, :, 0:N], AX.X, ALU.add))
            v.tensor_scalar(LNC[:, :, :], C[:, :, :], 1.0, None, ALU.max).then_inc(count_all, 1)
            dve.wait_ge(count_all, 1)
            own.step(v.tensor_copy(LNC2[:, :, :], C[:, :, :]))
            own.wait()
            for t in range(T):
                diag = slice(t * R, (t + 1) * R)
                own.step(v.tensor_tensor(LNC2[:, t, diag], C[:, t, diag], ident[0:R, 0:R], ALU.add))
            own.wait()
            M1 = HT[0:R, :, :].rearrange("p a b -> p (a b)")[:, 0:T * 2 * HALF].rearrange("p (t n) -> p t n", t=T)
            v.engine_nop().then_inc(lnc_in, 1)
            own.step(v.tensor_scalar(M1, LNC2[:, :, :], 0.0, NEVER, ALU.is_equal, ALU.mult))
            own.wait()
            v.tensor_scalar(LNC2[:, :, :], LNC2[:, :, :], 1.0, None, ALU.max).then_inc(lnc_in, 1)
            dve.wait_ge(lnc_ln, 2)
            own.step(v.tensor_tensor(LNC2[:, :, :], LNC2[:, :, :], M1, ALU.add))
            own.wait()
            own.step(v.tensor_scalar(M1, C[:, :, :], 0.0, NEVER, ALU.is_equal, ALU.mult))
            own.wait()
            own.step(v.tensor_tensor(LNC[:, :, :], LNC[:, :, :], M1, ALU.add))
            own.wait()

            def take_waits():
                v.sem_inc(waits_taken, 1)

            def attention(ubase, tbase, heads, lnc, scores, finish):
                units = T * heads
                dh = D // heads

                def tile(t):
                    dve.wait_ge(mixed, ubase + heads * (t + 1))
                    own.step(v.tensor_scalar(rden[:, t, 0:heads], den[:, t, 0:heads], 1e-30, None, ALU.max))
                    own.wait()
                    own.step(v.reciprocal(rden[:, t, 0:heads], rden[:, t, 0:heads]))
                    own.wait()
                    own.step(v.tensor_tensor(
                        ON[:, :].rearrange("p (h d) -> p h d", h=heads),
                        Y[t % 2][0:R, 0:D].rearrange("p (h d) -> p h d", h=heads),
                        rden[:, t, 0:heads].unsqueeze(2).broadcast_to([R, heads, dh]), ALU.mult))
                    own.wait()
                    finish(t)

                for k in range(units + 3):
                    if k < units:
                        t, h = divmod(k, heads)
                        sc = scores(k, t, h)
                        if k >= 2:
                            dve.wait_ge(prob, ubase + (k - 1))
                        take_waits()
                        v.tensor_tensor_reduce(SM[:, k % 2, :], sc, lnc[:, t, 0:N], 1.0, FLOOR, ALU.add, ALU.max,
                                               mx[:, k % 2:k % 2 + 1]).then_inc(masked, 1)
                        dve.wait_ge(masked, ubase + (k + 1))
                        v.tensor_scalar(nmx[:, k % 2:k % 2 + 1], mx[:, k % 2:k % 2 + 1], -1.0, None, ALU.mult)\
                         .then_inc(negmax, 1)
                    if k - 2 >= heads and (k - 2) % heads == 0:
                        tile((k - 2) // heads - 1)

            def l0_layer(i):
                for t in range(T):
                    dve.wait_ge(vs_ready, T * i + (t + 1))
                    v.tensor_tensor(VS[:, t, :], Y[t % 2][0:R, :], rows[:, bass.ds(512 * i + W["bvs"], 512)], ALU.add)\
                     .then_inc(vs_done, 1)
                dve.wait_ge(vs_done, T * i + T)

                def scores(k, t, h):
                    dve.wait_ge(score_ready, 20 * i + (k + 1))
                    return H[k % 2][0:R, 0:N]

                def finish(t):
                    v.tensor_tensor(Z[:, t, :], ON[:, :], VS[:, t, D:2 * D], ALU.add).then_inc(tile_out, 1)

                attention(20 * i, T * i, 4, LNC, scores, finish)

            def affine(gamma, beta, count):
                own.wait()
                take_waits()
                for c in range(KC):
                    own.step(v.bn_aggr(FMV[:, c, :], FST[:, c, :, :].rearrange("p a b -> p (a b)")))
                own.wait()
                v.tensor_scalar(FVE[:, :], FMV[:, :, 1], EPS, None, ALU.add).then_inc(bn_var, 1)
                dve.wait_ge(bn_rstd, count + 1)
                own.step(v.tensor_tensor(FSC[:, :], gamma, FRS[:, :], ALU.mult))
                own.wait()
                own.step(v.tensor_tensor(FBI[:, :], FMV[:, :, 0], FSC[:, :], ALU.mult))
                own.wait()
                v.tensor_tensor(FBI[:, :], beta, FBI[:, :], ALU.subtract).then_inc(bn_affine, 1)

            PER_LAYER = 3 * T + 2 * KC + KC + 2
            dve.wait_ge(in_small, 64)
            with dve.Fori(0, LAYERS - 1) as i:
                own.enter(i, PER_LAYER)
                l0_layer(i)
                for c in range(KC):
                    dve.wait_ge(turned, 2 * i + (c + 3))
                    own.step(v.bn_stats(FST[:, c, 0, :], H5[c][:, 0:4, 0:R]))
                    own.step(v.bn_stats(FST[:, c, 1, :], H5[c][:, 4, 0:R]))
                affine(vec[:, bass.ds(2 * i + V["bn_g"], 2)], vec[:, bass.ds(2 * i + V["bn_b"], 2)], i)
                own.leave(LAYERS - 1, PER_LAYER)
            l0_layer(LAYERS - 1)
            dve.wait_ge(tile_out, LAYERS * T)
            own.step(v.tensor_tensor(X[:, :, :], X[:, :, :], Z[:, :, :], ALU.add))
            own.wait()

            def top_two(k, tiles):
                for t in tiles:
                    own.step(v.max(M8[:, t, :], LG[:, t, :]))
                own.wait()
                for t in tiles:
                    own.step(v.max_index(I8[:, t, :], M8[:, t, :], LG[:, t, :]))
                own.wait()

            def dense_weights():
                own.step(v.tensor_copy(IF[:, :, :], I8[:, :, 0:2]))
                own.wait()
                for j, dst in enumerate([OH0, WD]):
                    own.step(v.tensor_tensor(dst[:, :, :], iota8[:, :, :],
                                             IF[:, :, j].unsqueeze(2).broadcast_to([R, T, EXPERTS]), ALU.is_equal))
                    own.wait()
                    own.step(v.tensor_tensor(dst[:, :, :], dst[:, :, :],
                                             TW[:, :, j].unsqueeze(2).broadcast_to([R, T, EXPERTS]), ALU.mult))
                    own.wait()
                v.tensor_tensor(WD[:, :, :], WD[:, :, :], OH0[:, :, :], ALU.add).then_inc(routed, 1)

            def route(k, bias):
                dve.wait_ge(logits, k + 1)
                lg = G1[0:R, 0:T * EXPERTS].rearrange("p (t e) -> p t e", t=T)
                if bias is None:
                    own.step(v.tensor_copy(LG[:, :, :], lg))
                else:
                    own.step(v.tensor_tensor(LG[:, :, :], lg, over_tiles(bias, EXPERTS), ALU.add))
                own.wait()
                top_two(k, range(T))
                if k == 3:
                    v.tensor_tensor(LX[:, :, :], LG[:, :, :], M8[:, :, 0].unsqueeze(2).broadcast_to([R, T, EXPERTS]),
                                    ALU.subtract).then_inc(route_arg, 1)
                    dve.wait_ge(route_exp, 6)
                    own.step(v.tensor_reduce(ZS[:, :], LE[:, :, :], AX.X, ALU.add))
                    own.step(v.max(M8[:, 0, :], LE[:, 0, :]))
                    for t in range(1, T):
                        own.step(v.max(M8[:, t, :], LE[:, t, :]))
                    own.wait()
                    own.step(v.tensor_scalar(ZS[:, :], ZS[:, :], 1e-9, None, ALU.mult))
                    own.step(v.tensor_tensor(E2[:, :], M8[:, :, 0], M8[:, :, 1], ALU.add))
                    own.wait()
                    own.step(v.tensor_tensor(E2[:, :], E2[:, :], ZS[:, :], ALU.add))
                    own.wait()
                    own.step(v.reciprocal(E2[:, :], E2[:, :]))
                    own.wait()
                    own.step(v.tensor_tensor(TW[:, :, :], M8[:, :, 0:2],
                                             E2[:, :].unsqueeze(2).broadcast_to([R, T, 2]), ALU.mult))
                else:
                    v.tensor_tensor(E2[:, :], M8[:, :, 1], M8[:, :, 0], ALU.subtract).then_inc(route_arg, 1)
                    dve.wait_ge(route_exp, k + 1)
                    own.step(v.tensor_scalar(ZS[:, :], E2[:, :], 1.0, None, ALU.add))
                    own.wait()
                    own.step(v.reciprocal(TW[:, :, 0], ZS[:, :]))
                    own.wait()
                    own.step(v.tensor_tensor(TW[:, :, 1], TW[:, :, 0], E2[:, :], ALU.mult))
                own.wait()
                dense_weights()
                dve.wait_ge(routed, k + 1)

            def combine(name, i, s, acc, weight):
                for t in range(T):
                    idx = T * (2 * i + s) + (YBASE[name] + t)
                    dve.wait_ge(y_ready, idx + 1)
                    dve.wait_ge(y_free, idx + 2)
                    v.scalar_tensor_tensor(acc[:, t, :], Y[(YBASE[name] + T * s + t) % 2][0:R, 0:D], weight(t),
                                           acc[:, t, :], ALU.mult, ALU.add).then_inc(y_free, 1)

            def bias2(k, acc, ybase):
                dve.wait_ge(wt_ready, k + 1)
                v.tensor_copy(WT[:, :, :], G5[0:EXPERTS, 0:T, 0:R]).then_inc(wt_done, 1)
                for t in range(T):
                    dve.wait_ge(y_ready, ybase + t + 1)
                    v.tensor_tensor(acc[:, t, :], acc[:, t, :], Y[(ybase + t) % 2][0:R, 0:D], ALU.add)\
                     .then_inc(y_free, 1)
                dve.wait_ge(y_free, ybase + T + 2)

            normalise("l0f", X, Z)
            route(0, row("bg", 8))
            with dve.Fori(0, EXPERTS // 2) as i:
                for s in range(2):
                    combine("l0", i, s, X, lambda t: WD[:, t, bass.ds(2 * i + s, 1)])
            dve.wait_ge(y_free, YBASE["l0"] + T * EXPERTS + 2)
            bias2(0, X, YBASE["l0"] + T * EXPERTS)

            def gat(name, slope, lnc, vbase, finish):
                heads = HEADS[name]
                dh = D // heads
                per = P // dh
                own.step(v.memset(AD[:, :, :], 0.0))
                own.step(v.tensor_copy(AB[:, :, :], vcol(name + "_as", 0, 2).unsqueeze(2).broadcast_to([P, KC, R])))
                own.wait()
                for h in range(heads):
                    r = slice(dh * (h % per), dh * (h % per) + dh)
                    c = h // per
                    last = v.tensor_copy(AD[r, c, h:h + 1], vec[r, V[name + "_ad"] + c:V[name + "_ad"] + c + 1])
                last.then_inc(ab_ready, 1)
                for t in range(T):
                    dve.wait_ge(vs_ready, vbase + t + 1)
                    v.tensor_copy(VS[:, t, 0:D], Y[t % 2][0:R, 0:D]).then_inc(vs_done, 1)
                k = {"l1": 0, "l2": 1}[name]
                dve.wait_ge(ed_ready, k + 1)
                own.step(v.tensor_copy(ED[:, :, 0:heads],
                                       G1[0:R, 0:T * 8].rearrange("p (t e) -> p t e", t=T)[:, :, 0:heads]))
                own.wait()
                dve.wait_ge(es_done, {"l1": 4, "l2": 12}[name])

                def scores(k, t, h):
                    es, ed = HT[0:R, h, :], ED[:, t, h:h + 1]
                    own.step(v.tensor_scalar(T1, es, ed, slope, ALU.add, ALU.mult))
                    own.wait()
                    own.step(v.scalar_tensor_tensor(T2, es, ed, T1, ALU.add, ALU.max))
                    own.wait()
                    if name == "l1":
                        own.step(v.tensor_scalar(T1, T2, 0.0, -1000.0, ALU.is_equal, ALU.mult))
                        own.wait()
                        own.step(v.tensor_tensor(T2, T2, T1, ALU.add))
                        own.wait()
                    return T2

                attention(UNITS[name], TILES[name], heads, lnc, scores, finish)

            normalise("l1g", X, Z)

            def add_to_x(t):
                v.tensor_tensor(X[:, t, :], X[:, t, :], ON[:, :], ALU.add).then_inc(tile_out, 1)

            gat("l1", 0.01, LNC, 15, add_to_x)
            dve.wait_ge(tile_out, 20)

            normalise("l1f", X, Z)
            dve.wait_ge(ln_out, LN["l1f"] + 1)
            normalise("l1n", Z, VS[:, :, 0:D])
            route(1, row("br1", 8))

            def expert_input(i, s):
                dve.wait_ge(xe_free, 2 * i + (s + 1))
                for c in range(KC):
                    last = v.tensor_scalar(XE[s][:, c, :], QT[:, c, :],
                                           vec[:, bass.ds(4 * i + (V["l1_g"] + 2 * s + c), 1)],
                                           vec[:, bass.ds(4 * i + (V["l1_b"] + 2 * s + c), 1)], ALU.mult, ALU.add)
                last.then_inc(xe_ready, 1)

            dve.wait_ge(xt_ready, 2 * TURN["l1n"] + 2)
            with dve.Fori(0, EXPERTS // 2) as i:
                for s in range(2):
                    expert_input(i, s)
                for s in range(2):
                    combine("l1", i, s, X, lambda t: WD[:, t, bass.ds(2 * i + s, 1)])
                v.sem_inc(xe_free, 2)
            dve.wait_ge(y_free, YBASE["l1"] + T * EXPERTS + 2)
            bias2(1, X, YBASE["l1"] + T * EXPERTS)

            normalise("l2g", X, Z)

            def add_bias_and_input(t):
                own.step(v.tensor_tensor(ON[:, :], ON[:, :], row("bias2", D), ALU.add))
                own.wait()
                v.tensor_tensor(Z[:, t, :], Z[:, t, :], ON[:, :], ALU.add).then_inc(tile_out, 1)

            gat("l2", 0.2, LNC2, 20, add_bias_and_input)
            dve.wait_ge(tile_out, 25)

            def affine_add(scale, shift, name):
                dve.wait_ge(ln_out, LN[name] + 1)
                own.step(v.tensor_tensor(Z[:, :, :], Z[:, :, :], over_tiles(scale, D), ALU.mult))
                own.wait()
                own.step(v.tensor_tensor(Z[:, :, :], Z[:, :, :], over_tiles(shift, D), ALU.add))
                own.wait()
                own.step(v.tensor_tensor(X[:, :, :], X[:, :, :], Z[:, :, :], ALU.add))
                own.wait()

            normalise("l2o", Z, Z)
            affine_add(row("ln_w", D), row("ln_b", D), "l2o")

            normalise("l2f", X, Z)
            dve.wait_ge(logits, 3)
            v.tensor_copy(LG[:, :, :], G1[0:R, 0:T * EXPERTS].rearrange("p (t e) -> p t e", t=T)).then_inc(logits_sb, 1)
            dve.wait_ge(mean_logits, 1)
            one = LG[:, 0, :]
            own.step(v.tensor_tensor(one, G0[0:R, 0:EXPERTS], row("br2", 8), ALU.add))
            own.wait()

            def softmax_row(n):
                own.step(v.tensor_reduce(M8[:, 0, 0:1], one, AX.X, ALU.max))
                own.wait()
                v.tensor_scalar(LX[:, 0, :], one, M8[:, 0, 0:1], None, ALU.subtract).then_inc(route_arg, 1)
                dve.wait_ge(route_exp, n)
                own.step(v.reciprocal(ZS[:, 1:2], ZS[:, 0:1]))
                own.wait()
                own.step(v.tensor_scalar(one, LE[:, 0, :], ZS[:, 1:2], None, ALU.mult))
                own.wait()

            softmax_row(3)
            load, cap = OH0[:, 0, :], OH0[:, 1, :]
            own.step(v.tensor_scalar(load, one, float(N), None, ALU.mult))
            own.wait()
            own.step(v.tensor_scalar(load, load, 98.0, 1.0 / 98.0, ALU.max, ALU.mult))
            own.wait()
            own.step(v.reciprocal(cap, load))
            own.wait()
            own.step(v.tensor_tensor(one, one, cap, ALU.mult))
            own.wait()
            softmax_row(4)
            own.step(v.max(M8[:, 0, :], one))
            own.wait()
            v.max_index(I8[:, 0, :], M8[:, 0, :], one).then_inc(picked, 1)
            v.tensor_tensor(E2[:, 0:1], M8[:, 0, 1:2], M8[:, 0, 0:1], ALU.subtract).then_inc(route_arg, 1)
            dve.wait_ge(route_exp, 5)
            own.step(v.tensor_scalar(ZS[:, 0:1], E2[:, 0:1], 1.0, None, ALU.add))
            own.wait()
            own.step(v.reciprocal(TW[:, 0, 0:1], ZS[:, 0:1]))
            own.wait()
            own.step(v.tensor_tensor(TW[:, 0, 1:2], TW[:, 0, 0:1], E2[:, 0:1], ALU.mult))
            own.wait()
            dve.wait_ge(picked, 1)
            for t in range(1, T):
                own.step(v.tensor_copy(TW[:, t, :], TW[:, 0, :]))
                own.step(v.tensor_copy(I8[:, t, :], I8[:, 0, :]))
            own.wait()
            dense_weights()
            dve.wait_ge(routed, 3)
            for s in range(2):
                combine("l2", 0, s, Z, lambda t: TW[:, 0, s:s + 1])
            dve.wait_ge(y_free, YBASE["l2"] + 2 * T + 2)
            bias2(2, Z, YBASE["l2"] + 2 * T)
            normalise("l2p", Z, Z)
            affine_add(row("gamma", D), row("beta", D), "l2p")

            own.step(v.tensor_scalar(deg[:, :], deg[:, :], 1.0, None, ALU.add))
            own.wait()
            v.engine_nop().then_inc(bn_affine, 1)
            normalise("l3g", X, Z)
            for c in range(KC):
                dve.wait_ge(qk_done, 16 + c + 1)
                own.step(v.bn_stats(FST[:, c, 0, :], QT[:, c, 0:500]))
                own.step(v.bn_stats(FST[:, c, 1, :], QT[:, c, 500:N]))
            affine(vcol("l3_g", 0, 2), vcol("l3_b", 0, 2), LAYERS - 1)
            dve.wait_ge(bn_rstd, LAYERS + 1)
            for t in range(T):
                dve.wait_ge(vs_ready, 25 + t + 1)
                v.tensor_scalar(VS[:, t, 0:D], Y[t % 2][0:R, 0:D], dinv[:, t:t + 1], None, ALU.mult).then_inc(vs_done, 1)
            dve.wait_ge(vs_done, 25 + T)
            for t in range(T):
                dve.wait_ge(mixed, 120 + t + 1)
                dve.wait_ge(tile_out, 25 + t)
                own.step(v.tensor_tensor(ON[:, :], Y[t % 2][0:R, 0:D], VS[:, t, 0:D], ALU.add))
                own.wait()
                own.step(v.scalar_tensor_tensor(ON[:, :], ON[:, :], dinv[:, t:t + 1], row("b_gcn", D), ALU.mult, ALU.add))
                own.wait()
                v.tensor_tensor(X[:, t, :], X[:, t, :], ON[:, :], ALU.add).then_inc(tile_out, 1)
            dve.wait_ge(tile_out, 25 + T)

            normalise("l3f", X, Z)
            route(3, None)
            nh = len(HID3)
            with dve.Fori(0, EXPERTS // 2) as i:
                for s in range(2):
                    for m, w in enumerate(HID3):
                        idx = nh * (2 * i + s) + m
                        dve.wait_ge(h3_ready, idx + 1)
                        dve.wait_ge(h1_free, idx + 2)
                        v.tensor_tensor(HT[0:w, m, :], H[1][0:w, 0:N], SG[0:w, m % 2, :], ALU.mult).then_inc(h3_free, 1)
                    combine("l3", i, s, X, lambda t: WD[:, t, bass.ds(2 * i + s, 1)])
            dve.wait_ge(y_free, YBASE["l3"] + T * EXPERTS + 2)
            v.engine_nop().then_inc(x_ready, 1)


def kernel(**inp):
    import numpy as np
    import concourse.bacc as bacc
    from concourse.bass_utils import run_bass_kernel_spmd

    def features(v):
        v = v.reshape(-1, v.shape[-1] // 128, 128)
        return v.reshape(-1, 128).T

    def chunks(w):
        k, m = w.shape[-2:]
        return np.moveaxis(w.reshape(w.shape[:-2] + (k // 128, 128, m)), -3, -2)

    def pad_rows(w, n):
        full = np.zeros(w.shape[:-2] + (n, w.shape[-1]), w.dtype)
        full[..., :w.shape[-2], :] = w
        return full

    i = {k: np.asarray(v) for k, v in inp.items()}
    A = {}
    A["x"] = i["x"].reshape(T, R, D).transpose(1, 0, 2)
    A["src"] = i["src"].reshape(R, BLOCKS)
    A["dst"] = i["dst"].reshape(R, BLOCKS)
    A["vec"] = np.concatenate([
        features(i["L0_gnn_bq"]), features(i["L0_gnn_bk"]), features(i["L0_gnn_bn_gamma"]),
        features(i["L0_gnn_bn_beta"]), features(i["L0_ffn_b1"]), features(i["L1_ffn_b1"]),
        features(i["L1_ffn_ln_g"]), features(i["L1_ffn_ln_b"]),
        features(i["L1_gnn_att"][:, :64].reshape(1, D)), features(i["L1_gnn_att"][:, 64:].reshape(1, D)),
        features(i["L2_gnn_att_src"].reshape(1, D)), features(i["L2_gnn_att_dst"].reshape(1, D)),
        features(i["L3_gnn_b1"][None]), features(i["L3_gnn_gamma"][None]), features(i["L3_gnn_beta"][None]),
        features(i["L3_gnn_b2"][None])], axis=1)
    bvs = np.concatenate([i["L0_gnn_bv"], i["L0_gnn_bs"]], axis=1).reshape(-1)
    A["rows"] = np.concatenate([bvs, i["L0_ffn_bg"], i["L1_ffn_br"], i["L2_ffn_br"], i["L2_gnn_bias"],
                                i["L2_gnn_ln_w"], i["L2_gnn_ln_b"], i["L2_ffn_gamma"], i["L2_ffn_beta"],
                                i["L3_gnn_b_gcn"]])
    A["wr"] = np.stack([chunks(i["L0_ffn_Wg"]), chunks(i["L1_ffn_Wr"]), chunks(i["L2_ffn_Wr"]),
                        chunks(i["L3_ffn_router_w"].T)], axis=1)
    A["b2"] = np.stack([i["L0_ffn_b2"], i["L1_ffn_b2"], i["L2_ffn_b2"]], axis=1)
    A["l0_wqk"] = np.stack([chunks(i["L0_gnn_Wq"]), chunks(i["L0_gnn_Wk"])], axis=2)
    A["l0_wvs"] = np.concatenate([chunks(i["L0_gnn_Wv"]), chunks(i["L0_gnn_Ws"])], axis=-1)
    A["l1_w"] = chunks(i["L1_gnn_W"].transpose(1, 0, 2).reshape(D, D))
    A["l2_w"] = chunks(i["L2_gnn_W"])
    A["l3_w"] = np.stack([chunks(i["L3_gnn_w1"].T), chunks(i["L3_gnn_w2"].T)], axis=1)
    A["l3_wg"] = chunks(i["L3_gnn_w_gcn"].T)
    for s in ("0", "1", "2"):
        for w, name in (("W1", "w1"), ("W2", "w2")):
            c = chunks(i[f"L{s}_ffn_{w}"])
            A[f"l{s}_{name}"] = c.reshape(EXPERTS, P, -1)
    A["l2_b1"] = i["L2_ffn_b1"].reshape(EXPERTS, 4, 128).transpose(0, 2, 1)
    w13 = np.stack([chunks(i["L3_ffn_w1"].transpose(0, 2, 1)), chunks(i["L3_ffn_w3"].transpose(0, 2, 1))], axis=2)
    A["l3_w13"] = w13.reshape(EXPERTS, P, -1)
    A["l3_w2"] = chunks(pad_rows(i["L3_ffn_w2"].transpose(0, 2, 1), 128 * len(HID3))).reshape(EXPERTS, P, -1)

    nc = bacc.Bacc("TRN2", target_bir_lowering=False, num_devices=1)
    arrays, aps = {}, {}
    for name, arr in A.items():
        arr = np.ascontiguousarray(arr)
        arrays[f"in_{name}"] = arr
        aps[name] = nc.dram_tensor(f"in_{name}", arr.shape, mybir.dt.from_np(arr.dtype), kind="ExternalInput").ap()
    out = nc.dram_tensor("out", (R, T, D), F32, kind="ExternalOutput").ap()
    graph_network(nc, aps, out)
    r = run_bass_kernel_spmd(nc, [arrays], core_ids=[0])
    return np.ascontiguousarray(r.results[0]["out"].transpose(1, 0, 2)).reshape(N, D)
```

```python
from contextlib import ExitStack

import concourse.bass as bass
import concourse.mybir as mybir

F32 = mybir.dt.float32
F16 = mybir.dt.float16
F32R = mybir.dt.float32r
I32 = mybir.dt.int32
U32 = mybir.dt.uint32
ALU = mybir.AluOpType
ACT = mybir.ActivationFunctionType
AX = mybir.AxisListType

N, D, EDGES = 625, 256, 20000
R, T = 125, 5
P, KC = 128, D // 128
SPLITS = [(0, 512), (512, N - 512)]
HALF = 313
FIELD = 12
PER_BLOCK, BLOCKS, GROUPS = R, EDGES // R, 5
GROUP = BLOCKS // GROUPS
RING = 4
NEVER = -1.0e30
EXPERTS = 8
FLOOR = -1.0e29
LAYERS = 3
EPS = 1e-5
HID01, HID2 = [128] * 8, [128] * 4
HID3 = [128] * 5 + [682 - 640]
SLOTS = 128
TOKEN_BLOCKS = (2 * N - EXPERTS) // SLOTS + EXPERTS
LOOPED = (TOKEN_BLOCKS - 5) // 2

V = {}
_at = 0
for _name, _n in [("bq", 6), ("bk", 6), ("bn_g", 4), ("bn_b", 4), ("l1_as", 2), ("l1_ad", 2), ("l2_as", 2), ("l2_ad", 2), ("l3_b1", 2),
                  ("l3_g", 2), ("l3_b", 2), ("l3_b2", 2)]:
    V[_name] = _at
    _at += _n
NV = _at
W = {}
_at = 0
for _name, _n in [("bvs", 3 * 512), ("bg", 8), ("br1", 8), ("br2", 8), ("bias2", D), ("ln_w", D), ("ln_b", D),
                  ("gamma", D), ("beta", D), ("b_gcn", D)]:
    W[_name] = _at
    _at += _n
NW = _at


class Steps:

    def __init__(self, eng, sem):
        self.eng, self.sem, self.base, self.n = eng, sem, 0, 0

    def step(self, ins):
        ins.then_inc(self.sem, 1)
        self.n += 1

    def wait(self):
        self.eng.wait_ge(self.sem, self.base + self.n)

    def enter(self, i, per):
        self.base0, self.n0 = self.base, self.n
        self.base, self.n = self.base + self.n + i * per, 0

    def leave(self, count, per):
        assert self.n == per, self.n
        self.base, self.n = self.base0, self.n0 + count * per


def graph_network(nc, a, out):
    with ExitStack() as ctx:
        def sb(name, shape, dt=F32):
            return ctx.enter_context(nc.sbuf_tensor(name, shape, dt))

        def sem(name):
            return ctx.enter_context(nc.semaphore(name))

        X = sb("X", [R, T, D])
        Z = sb("Z", [R, T, D])
        XT = sb("XT", [P, KC, N])
        QT = sb("QT", [P, KC, N])
        KT = sb("KT", [P, KC, N])
        VS = sb("VS", [R, T, 2 * D])
        HT = sb("HT", [P, 8, N])
        C = sb("C", [R, T, 2 * HALF])
        LNC = sb("LNC", [R, T, 2 * HALF])
        LNC2 = sb("LNC2", [R, T, 2 * HALF])
        CT = sb("CT", [R, T, N])
        WA = [sb(f"WA{s}", [P, 2 * KC * 682]) for s in range(2)]
        WB = [sb(f"WB{s}", [P, 8 * D]) for s in range(2)]
        GQK = sb("GQK", [P, 2, KC, D])
        GVS = sb("GVS", [P, KC, 2 * D])
        B1S = sb("B1S", [P, 2, 4])
        vec = sb("vec", [P, NV])
        bq8 = sb("bq8", [P, 6])
        rows = sb("rows", [R, NW])
        wr = sb("wr", [P, 4, KC, EXPERTS])
        b2 = sb("b2", [EXPERTS, 3, D])
        PT = sb("PT", [R, 2, T, R])
        edge_space = PT[:, :, :, :].rearrange("p a t r -> p (a t r)")
        src_i, dst_i = [edge_space[:, k * BLOCKS:(k + 1) * BLOCKS].bitcast(I32) for k in range(2)]
        src_f, dst_f, src_field, src_lo, src_val = [edge_space[:, k * BLOCKS:(k + 1) * BLOCKS] for k in range(2, 7)]
        iota8 = sb("iota8", [R, T, EXPERTS])
        ident = sb("ident", [P, P])
        mean_of = sb("mean_of", [R, R])
        half = sb("half", [P, 8])
        SG = sb("SG", [P, 2, N])
        OHD = SG[0:R, :, :].bitcast(F16).rearrange("p a (b n) -> p (a b) n", n=N)
        OHS = QT[0:R, :, :].rearrange("p c n -> p (c n)")[:, 0:RING * HALF // 2].bitcast(F16)\
            .rearrange("p (b n) -> p b n", n=HALF)
        CI = VS[:, :, 0:HALF].bitcast(I32)
        CF = HT[0:R, 0:T, 0:HALF].bitcast(I32)
        c_space = C[:, :, :].rearrange("p t n -> p (t n)")
        SM, PR = [c_space[:, k * 2 * N:(k + 1) * 2 * N].rearrange("p (a n) -> p a n", a=2) for k in range(2)]
        T1, T2 = KT[0:R, 0, :], KT[0:R, 1, :]
        mx = sb("mx", [R, 2])
        nmx = sb("nmx", [R, 2])
        den = sb("den", [R, T, 8])
        rden = sb("rden", [R, T, 8])
        ON = sb("ON", [R, D])
        AB = sb("AB", [P, KC, R])
        AD = sb("AD", [P, KC, 8])
        ED = sb("ED", [R, T, 8])
        ST = sb("ST", [R, T, 6])
        MV = sb("MV", [R, T, 2])
        VE = sb("VE", [R, 8])
        RS = sb("RS", [R, 8])
        FST = sb("FST", [P, KC, 2, 6])
        FMV = sb("FMV", [P, KC, 2])
        FVE = sb("FVE", [P, KC])
        FRS = sb("FRS", [P, KC])
        FSC = sb("FSC", [P, KC])
        FBI = sb("FBI", [P, KC])
        LG = sb("LG", [R, T, EXPERTS])
        LX = sb("LX", [R, T, EXPERTS])
        LE = sb("LE", [R, T, EXPERTS])
        M8 = sb("M8", [R, T, 8])
        I8 = sb("I8", [R, T, 8], U32)
        IF = sb("IF", [R, T, 2])
        E2 = sb("E2", [R, T])
        ZS = sb("ZS", [R, T])
        TW = sb("TW", [R, T, 2])
        OH0 = sb("OH0", [R, T, EXPERTS])
        WD = sb("WD", [R, T, EXPERTS])
        WT = sb("WT", [EXPERTS, T, R])
        ZH, ZL = sb("ZH", [R, T, D], F32R), sb("ZL", [R, T, D], F32R)
        PM = sb("PM", [R, T, SLOTS], F32R)
        BL = 18
        slot_work = [c_space[:, k * BL * 2 * T:(k + 1) * BL * 2 * T].rearrange("p (b t) -> p b t", b=BL) for k in range(2)]
        slot_of = sb("slot_of", [R, BL, T])
        iota_p = sb("iota_p", [R, BL])
        XB = sb("XB", [P, 2, KC, SLOTS])
        SS = sb("SS", [P, N], F32R)
        YS = SG[:, 0, SLOTS:SLOTS + D]
        YH, YL = sb("YH", [P, D], F32R), sb("YL", [P, D], F32R)
        iota_s = sb("iota_s", [P, SLOTS])
        iota_n = sb("iota_n", [P, N + 1], F16)
        iota_b = sb("iota_b", [P, BL])
        iota_e = sb("iota_e", [P, EXPERTS])
        before = sb("before", [R, R])
        ones = sb("ones", [R, P])
        SEL = sb("SEL", [R, T, EXPERTS])
        OHK = sb("OHK", [R, T, 2, EXPERTS])
        WDT = sb("WDT", [R, T, EXPERTS + 1])
        CNT = sb("CNT", [P, EXPERTS])
        CNI = sb("CNI", [P, EXPERTS], I32)
        NB = sb("NB", [P, EXPERTS])
        INC = sb("INC", [P, EXPERTS])
        BASE = sb("BASE", [P, EXPERTS])
        RK = sb("RK", [R, T, EXPERTS])
        POS = sb("POS", [R, T, 2])
        EOB = sb("EOB", [P, BL])
        EOU = sb("EOU", [P, BL], U32)
        EOH = sb("EOH", [P, BL, EXPERTS])
        TI = sb("TI", [P, EXPERTS + 1])
        TW8 = sb("TW8", [P, EXPERTS])
        WSL = sb("WSL", [P, 1])
        deg = sb("deg", [R, T])
        dinv = sb("dinv", [R, T])

        PS = ctx.enter_context(nc.psum_tensor("PS", [P, 8, 512], F32))
        flat = PS[:, :, :].rearrange("p b n -> p (b n)")
        H = [flat[:, 0:1024], flat[:, 1024:2048]]
        H5 = [h.rearrange("p (s n) -> p s n", n=128) for h in H]
        Y = [PS[:, 4, :], PS[:, 5, :]]
        G5 = flat[:, 3072:4096].rearrange("p (s n) -> p s n", n=128)
        G0, G1 = PS[:, 6, :], PS[:, 7, :]
        HB = [PS[:, 0, :], PS[:, 1, :]]
        GB = [PS[:, 2, :], PS[:, 4, :]]
        YB = PS[:, 3, :]
        OUT = [PS[:, 5 + t // 2, (t % 2) * D:(t % 2 + 1) * D] for t in range(T)]

        waits_taken = sem("waits_taken")
        in_edges = sem("in_edges")
        in_x = sem("in_x")
        in_small = sem("in_small")
        in_graph_w = sem("in_graph_w")
        in_WA = [sem(f"in_WA{s}") for s in range(2)]
        in_WB = [sem(f"in_WB{s}") for s in range(2)]
        consts = sem("consts")
        vec_step = sem("vec_step")
        act_step = sem("act_step")
        pool_step = sem("pool_step")
        onehot_ready = sem("onehot_ready")
        onehot_free = sem("onehot_free")
        counts_free = sem("counts_free")
        count_all = sem("count_all")
        lnc_in = sem("lnc_in")
        lnc_ln = sem("lnc_ln")
        count_turned = sem("count_turned")
        ct_copied = sem("ct_copied")
        ln_var = sem("ln_var")
        ln_rstd = sem("ln_rstd")
        ln_out = sem("ln_out")
        bn_var = sem("bn_var")
        bn_rstd = sem("bn_rstd")
        bn_affine = sem("bn_affine")
        turned = sem("turned")
        xt_ready = sem("xt_ready")
        qk_ready = sem("qk_ready")
        qk_done = sem("qk_done")
        vs_ready = sem("vs_ready")
        vs_done = sem("vs_done")
        ab_ready = sem("ab_ready")
        ed_ready = sem("ed_ready")
        es_ready = sem("es_ready")
        es_done = sem("es_done")
        score_ready = sem("score_ready")
        masked = sem("masked")
        negmax = sem("negmax")
        prob = sem("prob")
        prob_turned = sem("prob_turned")
        probT = sem("probT")
        mixed = sem("mixed")
        tile_out = sem("tile_out")
        logits = sem("logits")
        logits_sb = sem("logits_sb")
        mean_logits = sem("mean_logits")
        route_arg = sem("route_arg")
        route_exp = sem("route_exp")
        routed = sem("routed")
        picked = sem("picked")
        wt_ready = sem("wt_ready")
        wt_done = sem("wt_done")
        h_ready = sem("h_ready")
        h_free = sem("h_free")
        y_ready = sem("y_ready")
        y_free = sem("y_free")
        route_consts = sem("route_consts")
        slots_read = sem("slots_read")
        selected = sem("selected")
        ranked = sem("ranked")
        blocks_known = sem("blocks_known")
        parts_ready = sem("parts_ready")
        out_begun = sem("out_begun")
        perm_ready = sem("perm_ready")
        gathered = sem("gathered")
        xb_done = sem("xb_done")
        info_done = sem("info_done")
        hid_ready = sem("hid_ready")
        gate_done = sem("gate_done")
        hidden = sem("hidden")
        yb_ready = sem("yb_ready")
        y_parts = sem("y_parts")
        scattered = sem("scattered")
        in_sel = sem("in_sel")
        x_ready = sem("x_ready")
        out_sent = sem("out_sent")

        def vcol(name, k=0, n=1):
            return vec[:, V[name] + k:V[name] + k + n]

        def row(name, n, k=0):
            return rows[:, W[name] + k:W[name] + k + n]

        def over_tiles(ap, n):
            return ap.unsqueeze(1).broadcast_to([R, T, n])

        LN = {k: i for i, k in enumerate(["l0g", "l0f", "l1g", "l1f", "l1n", "l2g", "l2o", "l2f", "l2p", "l3g", "l3f"])}
        TURN = {k: i for i, k in enumerate(["l0_0", "l0_1", "l0_2", "l0f", "l1g", "l1f", "l2g", "l2f", "l3g", "l3f"])}
        ROUTE = {"l0": 0, "l1": 1, "l2": 2, "l3": 3}
        UNITS = {"l1": 60, "l2": 80}
        TILES = {"l1": 15, "l2": 20}
        HEADS = {"l1": 4, "l2": 8}
        STAGE = {"l0": 0, "l1": 1, "l3": 2}
        JOBS = {"l0": 4, "l1": 4, "l3": 6}
        JBASE = {"l0": 0, "l1": 4 * TOKEN_BLOCKS, "l3": 8 * TOKEN_BLOCKS}
        W1_COLS = {"l0": 2048 + 8, "l1": 2048 + 12, "l3": 2 * KC * 682}
        W2_COLS = {"l0": 8 * D, "l1": 8 * D, "l3": 6 * D}
        FILLS = {"l0": (0, 0), "l1": (9, 8), "l2": (18, 16), "l3": (19, 17)}

        def token_blocks(eng, body, steps=None, per=0):
            for b in range(3):
                body(b, b, 0)
            with eng.Fori(0, LOOPED) as i:
                if steps:
                    steps.enter(i, 2 * per)
                for c in (3, 4):
                    body(2 * i + c, c, i)
                if steps:
                    steps.leave(LOOPED, 2 * per)
            for b in range(2 * LOOPED + 3, TOKEN_BLOCKS):
                body(b, b, 0)

        block = ctx.enter_context(nc.Block())

        @block.sync
        def _(sp):
            sp.dma_start(src_i, a["src"]).then_inc(in_edges, 16)
            sp.dma_start(dst_i, a["dst"]).then_inc(in_edges, 16)
            sp.dma_start(X[:, :, :], a["x"]).then_inc(in_x, 16)

            def load_blocks(name, w1, w2):
                q, jobs, jbase = STAGE[name], JOBS[name], JBASE[name]
                sp.wait_ge(blocks_known, q + 1)

                def load(b, c, i):
                    e = sp.value_load(EOU[0:1, bass.ds(b, 1)], min_val=0, max_val=EXPERTS - 1)
                    if c >= 2:
                        sp.wait_ge(hidden, jobs * b + (jbase - jobs))
                    sp.dma_start(WA[c % 2][:, 0:W1_COLS[name]], w1[e]).then_inc(in_WA[c % 2], 16)
                    if c >= 2:
                        sp.wait_ge(yb_ready, b + (TOKEN_BLOCKS * q - 1))
                    if name == "l3":
                        sp.dma_start(WB[c % 2][:, 0:5 * D], w2[e, :, 0:5 * D]).then_inc(in_WB[c % 2], 16)
                        sp.dma_start(WB[c % 2][0:HID3[5], 5 * D:6 * D], w2[e, 0:HID3[5], 5 * D:6 * D])\
                          .then_inc(in_WB[c % 2], 16)
                    else:
                        sp.dma_start(WB[c % 2][:, 0:8 * D], w2[e]).then_inc(in_WB[c % 2], 16)

                token_blocks(sp, load)

            load_blocks("l0", a["l0_w1"], a["l0_w2"])
            load_blocks("l1", a["l1_w1"], a["l1_w2"])
            sp.wait_ge(picked, 1)
            for k in range(2):
                e = sp.value_load(I8[0:1, 0, k:k + 1], min_val=0, max_val=EXPERTS - 1)
                sp.dma_start(WA[k][:, 0:1024], a["l2_w1"][e]).then_inc(in_WA[k], 16)
                sp.dma_start(WB[k][:, 0:1024], a["l2_w2"][e]).then_inc(in_WB[k], 16)
                sp.dma_start(B1S[:, k, :], a["l2_b1"][e]).then_inc(in_sel, 16)
            load_blocks("l3", a["l3_w13"], a["l3_w2"])
            sp.wait_ge(x_ready, 1)
            sp.dma_start(out, X[:, :, :]).then_inc(out_sent, 16)
            sp.wait_ge(out_sent, 16)

        @block.gpsimd
        def _(pool):
            own = Steps(pool, pool_step)
            pool.dma_start(vec[:, :], a["vec"]).then_inc(in_small, 16)
            pool.dma_start(rows[:, :], a["rows"].partition_broadcast(R)).then_inc(in_small, 16)
            pool.dma_start(wr[:, :, :, :], a["wr"]).then_inc(in_small, 16)
            pool.dma_start(b2[:, :, :], a["b2"]).then_inc(in_small, 16)

            pool.iota(iota_n[:, :], [[1, N + 1]], base=1, channel_multiplier=0, allow_small_or_imprecise_dtypes=True)\
                .then_inc(consts, 1)
            pool.iota(iota8[:, :, :], [[0, T], [1, EXPERTS]], base=0, channel_multiplier=0,
                      allow_small_or_imprecise_dtypes=True).then_inc(consts, 1)
            pool.memset(half[:, :], -0.5).then_inc(consts, 1)
            pool.memset(mean_of[:, :], 1.0 / N).then_inc(consts, 1)
            own.step(pool.memset(ident[:, :], 0.0))
            own.wait()
            pool.affine_select(out=ident[:, :], in_=ident[:, :], compare_op=ALU.not_equal, fill=1.0, base=0,
                               pattern=[[-1, P]], channel_multiplier=1).then_inc(consts, 1)

            for tile, pattern, base in [(iota_s[:, :], [[1, SLOTS]], 0),
                                        (iota_p[:, :], [[SLOTS, BL]], 0),
                                        (iota_b[:, :], [[1, BL]], 0),
                                        (iota_e[:, :], [[1, EXPERTS]], 0)]:
                pool.iota(tile, pattern, base=base, channel_multiplier=0, allow_small_or_imprecise_dtypes=True)\
                    .then_inc(route_consts, 1)
            for t in range(T):
                pool.iota(WDT[:, t, EXPERTS:EXPERTS + 1], [[0, 1]], base=t * R + 1, channel_multiplier=1,
                          allow_small_or_imprecise_dtypes=True).then_inc(route_consts, 1)
            own.step(pool.memset(before[:, :], 1.0))
            own.wait()
            pool.affine_select(out=before[:, :], in_=before[:, :], compare_op=ALU.is_gt, fill=0.0, base=0,
                               pattern=[[1, R]], channel_multiplier=-1).then_inc(route_consts, 1)
            pool.memset(ones[:, :], 1.0).then_inc(route_consts, 1)

            def layer_weights(i):
                pool.dma_start(GQK[:, :, :, :], a["l0_wqk"][i]).then_inc(in_graph_w, 16)
                pool.dma_start(GVS[:, :, :], a["l0_wvs"][i]).then_inc(in_graph_w, 16)

            def power(out_, in_, n, wait, value, done):
                pool.wait_ge(wait, value)
                nc.gpsimd.tensor_tensor(out_, in_, half[0:n, 0:in_.shape[1]], ALU.pow).then_inc(done, 1)

            def ln_power(name):
                power(RS[:, 0:T], VE[:, 0:T], R, ln_var, LN[name] + 1, ln_rstd)

            layer_weights(0)
            pool.wait_ge(consts, 5)
            ln_power("l0g")
            with pool.Fori(0, LAYERS - 1) as i:
                pool.wait_ge(vs_ready, i * T + T)
                layer_weights(i + 1)
                power(FRS[:, :], FVE[:, :], P, bn_var, i + 1, bn_rstd)
            pool.wait_ge(vs_ready, LAYERS * T)
            pool.dma_start(GQK[:, 0, :, :], a["l1_w"]).then_inc(in_graph_w, 16)
            ln_power("l0f")
            ln_power("l1g")
            pool.wait_ge(qk_ready, 4 * LAYERS + 2)
            pool.dma_start(GQK[:, 1, :, :], a["l2_w"]).then_inc(in_graph_w, 16)
            pool.dma_start(GVS[:, :, 0:D], a["l3_wg"]).then_inc(in_graph_w, 16)
            for name in ["l1f", "l1n", "l2g", "l2o", "l2f", "l2p"]:
                ln_power(name)
            pool.dma_start(GQK[:, :, :, :], a["l3_w"]).then_inc(in_graph_w, 16)
            ln_power("l3g")
            power(FRS[:, :], FVE[:, :], P, bn_var, LAYERS, bn_rstd)
            power(dinv[:, :], deg[:, :], R, bn_affine, LAYERS, bn_rstd)
            ln_power("l3f")

        @block.tensor
        def _(pe):
            def turn(src, n, wait, value):
                pe.wait_ge(wait, value)
                for c in range(KC):
                    for t in range(T):
                        last = pe.transpose(H5[c][:, t, 0:R], src[:, t, c * 128:(c + 1) * 128], ident[0:R, 0:R])
                    last.then_inc(turned, 1)

            def wide(slot, lhs, rhs, rows_out, done):
                for lo, w in SPLITS:
                    for c in range(len(lhs)):
                        last = pe.matmul(slot[0:rows_out, lo:lo + w], lhs[c], rhs[c][:, lo:lo + w],
                                         start=(c == 0), stop=(c == len(lhs) - 1))
                last.then_inc(done, 1)

            pe.sem_inc(onehot_free, RING)
            with pe.Fori(0, GROUPS) as g:
                pe.wait_ge(counts_free, g + 1)
                for b in range(GROUP):
                    pe.wait_ge(onehot_ready, g * GROUP + (b + 1))
                    for t in range(T):
                        last = pe.matmul(PS[0:R, t, 0:HALF], OHD[:, b % RING, t * R:(t + 1) * R],
                                         OHS[:, b % RING, :], start=(b == 0), stop=(b == GROUP - 1))
                    last.then_inc(onehot_free, 1)

            pe.wait_ge(count_all, 1)
            pe.wait_ge(consts, 5)
            for t in range(T):
                if t >= 2:
                    pe.wait_ge(ct_copied, t - 1)
                for s in range(T):
                    last = pe.transpose(H5[t % 2][0:R, s, 0:R], C[:, t, s * R:(s + 1) * R], ident[0:R, 0:R])
                last.then_inc(count_turned, 1)
            pe.wait_ge(ct_copied, T)

            def attention(ubase, tbase, heads, dh, scored):
                units = T * heads

                def score(k):
                    t, h = divmod(k, heads)
                    if k >= 2:
                        pe.wait_ge(masked, ubase + (k - 1))
                    r = slice(dh * (h % 2), dh * (h % 2) + dh)
                    for lo, w in SPLITS:
                        last = pe.matmul(H[k % 2][0:R, lo:lo + w], QT[r, h // 2, t * R:(t + 1) * R],
                                         KT[r, h // 2, lo:lo + w], start=True, stop=True)
                    last.then_inc(score_ready, 1)

                def turn_probs(k):
                    pe.wait_ge(prob, ubase + (k + 1))
                    if k >= 1:
                        pe.wait_ge(probT, ubase + k)
                    for s in range(T):
                        last = pe.transpose(G5[0:R, s, 0:R], PR[:, k % 2, s * R:(s + 1) * R], ident[0:R, 0:R])
                    last.then_inc(prob_turned, 1)

                def mix(k):
                    t, h = divmod(k, heads)
                    pe.wait_ge(probT, ubase + (k + 1))
                    if h == 0 and t >= 2:
                        pe.wait_ge(tile_out, tbase + (t - 1))
                    for s in range(T):
                        last = pe.matmul(Y[t % 2][0:R, h * dh:(h + 1) * dh], PT[:, k % 2, s, :],
                                         VS[:, s, h * dh:(h + 1) * dh], start=(s == 0), stop=(s == T - 1))
                    last.then_inc(mixed, 1)

                for k in range(units + 2):
                    if scored and k < units:
                        score(k)
                    if 1 <= k <= units:
                        turn_probs(k - 1)
                    if k >= 2:
                        mix(k - 2)

            def l0_layer(i):
                pe.wait_ge(xt_ready, 2 * i + 2)
                pe.wait_ge(in_graph_w, 32 * i + 32)
                for j in range(4):
                    if j >= 2:
                        pe.wait_ge(qk_done, 4 * i + (j - 1))
                    q, m = divmod(j, 2)
                    wide(H[j % 2], [GQK[:, q, c, m * 128:(m + 1) * 128] for c in range(KC)],
                         [XT[:, c, :] for c in range(KC)], P, qk_ready)
                for t in range(T):
                    if t >= 2:
                        pe.wait_ge(vs_done, T * i + (t - 1))
                    for c in range(KC):
                        last = pe.matmul(Y[t % 2][0:R, :], XT[:, c, t * R:(t + 1) * R], GVS[:, c, :],
                                         start=(c == 0), stop=(c == KC - 1))
                    last.then_inc(vs_ready, 1)
                pe.wait_ge(qk_done, 4 * i + 4)
                pe.wait_ge(vs_done, T * i + T)
                attention(20 * i, T * i, 4, 64, True)

            turn(Z, 0, ln_out, LN["l0g"] + 1)
            with pe.Fori(0, LAYERS - 1) as i:
                l0_layer(i)
                turn(Z, i + 1, tile_out, T * i + T)
            l0_layer(LAYERS - 1)

            def route(k, n):
                pe.wait_ge(xt_ready, 2 * n + 2)
                pe.wait_ge(in_small, 64)
                for t in range(T):
                    for c in range(KC):
                        last = pe.matmul(G1[0:R, t * 8:t * 8 + 8], XT[:, c, t * R:(t + 1) * R], wr[:, k, c, :],
                                         start=(c == 0), stop=(c == KC - 1))
                last.then_inc(logits, 1)

            def experts(s):
                nh = len(HID2)
                pe.wait_ge(in_WA[s], 16 * (FILLS["l3"][s]))
                for m in range(nh):
                    pe.wait_ge(h_free, nh * s + m + 1)
                    wide(H[m % 2], [WA[s][:, c * 512 + m * 128:c * 512 + (m + 1) * 128] for c in range(KC)],
                         [XT[:, c, :] for c in range(KC)], P, h_ready)
                pe.wait_ge(in_WB[s], 16 * (FILLS["l3"][s]))
                for t in range(T):
                    pe.wait_ge(y_free, T * s + t + 1)
                    for m in range(nh):
                        if t == 0:
                            pe.wait_ge(h_free, nh * s + m + 3)
                        last = pe.matmul(Y[(T * s + t) % 2][0:R, 0:D], HT[:, m, t * R:(t + 1) * R],
                                         WB[s][:, m * D:(m + 1) * D], start=(m == 0), stop=(m == nh - 1))
                    last.then_inc(y_ready, 1)

            def sparse_experts(name):
                q, jobs, jbase = STAGE[name], JOBS[name], JBASE[name]
                hid = HID3 if name == "l3" else HID01
                n1 = 682 if name == "l3" else 1024
                pe.wait_ge(selected, q + 1)
                pe.wait_ge(route_consts, 11)
                for t in range(T):
                    for s in range(t + 1):
                        pe.matmul(G0[0:R, t * 8:t * 8 + 8], before[:, :] if s == t else ones[:, 0:R], SEL[:, s, :],
                                  start=(s == 0), stop=(s == t))
                for s in range(T):
                    last = pe.matmul(G0[:, 64:72], ones[:, :], SEL[:, s, :], start=(s == 0), stop=(s == T - 1))
                last.then_inc(ranked, 1)
                pe.wait_ge(blocks_known, q + 1)
                if name != "l3":
                    pe.wait_ge(routed, q + 1)
                    for t in range(T):
                        last = pe.transpose(G5[0:EXPERTS, t, 0:R], WD[:, t, :], ident[0:R, 0:R])
                    last.then_inc(wt_ready, 1)
                    pe.wait_ge(wt_done, q + 1)
                else:
                    pe.wait_ge(wt_done, 4)
                for t in range(T):
                    pe.matmul(OUT[t][0:R, :], WT[:, t, :], b2[:, q % 2, :], start=(t % 2 == 0), stop=(t == T - 1),
                              skip_group_check=True)

                def gather(b, c):
                    B = b + TOKEN_BLOCKS * q
                    bank = GB[c % 2]
                    pe.wait_ge(perm_ready, B + 1)
                    if c >= 2:
                        pe.wait_ge(slots_read, B - 1)
                    for f in range(KC):
                        for part in (ZH, ZL):
                            for t in range(T):
                                pe.matmul(bank[:, f * SLOTS:(f + 1) * SLOTS], part[:, t, f * 128:(f + 1) * 128],
                                          PM[:, t, :], start=(part is ZH and t == 0),
                                          stop=(part is ZL and t == T - 1))
                    for t in range(T):
                        last = pe.matmul(bank[:, 2 * SLOTS:2 * SLOTS + 9], PM[:, t, :].bitcast(F32), WDT[:, t, :],
                                         start=(t == 0), stop=(t == T - 1))
                    last.then_inc(gathered, 1)

                def scatter(b):
                    B = b + TOKEN_BLOCKS * q
                    pe.wait_ge(info_done, B + 1)
                    pe.wait_ge(y_parts, B + 1)
                    for t in range(T):
                        for part in (YH, YL):
                            last = pe.matmul(OUT[t][0:R, :], SS[:, t * R:(t + 1) * R], part[:, :],
                                             start=False, stop=False, skip_group_check=True)
                    last.then_inc(scattered, 1)

                def block_of_tokens(b, c, i):
                    B = b + TOKEN_BLOCKS * q
                    s = c % 2
                    last_block = isinstance(b, int) and b == TOKEN_BLOCKS - 1
                    if c == 0:
                        pe.wait_ge(parts_ready, q + 1)
                        gather(0, 0)
                    pe.wait_ge(in_WA[s], 16 * i + 16 * (FILLS[name][s] + c // 2 + 1))
                    pe.wait_ge(xb_done, B + 1)
                    for j in range(jobs):
                        if c >= 1 or j >= 2:
                            pe.wait_ge(hidden, jobs * b + (jbase + j - 1))
                        for k in range(2):
                            if name == "l3":
                                w, at = hid[j], 2 * k * n1 + j * 128
                            else:
                                w, at = 128, (2 * j + k) * 128
                            for f in range(KC):
                                last = pe.matmul(HB[j % 2][0:w, k * SLOTS:(k + 1) * SLOTS],
                                                 WA[s][:, f * n1 + at:f * n1 + at + w], XB[:, s, f, :],
                                                 start=(f == 0), stop=(f == KC - 1))
                        last.then_inc(hid_ready, 1)
                    if c >= 1:
                        scatter(b - 1)
                    if not last_block:
                        gather(b + 1, c + 1)
                    loads = 2 if name == "l3" else 1
                    pe.wait_ge(in_WB[s], 16 * loads * i + 16 * (FILLS[name][s] + loads * (c // 2 + 1)))
                    for m, w in enumerate(hid):
                        if name == "l3" or m % 2 == 0:
                            job = m if name == "l3" else m // 2
                            pe.wait_ge(hidden, jobs * b + (jbase + job + 1))
                        last = pe.matmul(YB[:, 0:D], HT[0:w, m, 0:SLOTS], WB[s][0:w, m * D:(m + 1) * D],
                                         start=(m == 0), stop=(m == len(hid) - 1))
                    last.then_inc(yb_ready, 1)
                    if last_block:
                        scatter(b)

                token_blocks(pe, block_of_tokens)

            turn(Z, TURN["l0f"], ln_out, LN["l0f"] + 1)
            route(0, TURN["l0f"])
            sparse_experts("l0")

            def gat(name, n, w, wload, qbase, vbase, esbase):
                heads = HEADS[name]
                dh = D // heads
                pe.wait_ge(xt_ready, 2 * n + 2)
                pe.wait_ge(in_graph_w, wload)
                for t in range(T):
                    if t >= 2:
                        pe.wait_ge(vs_done, vbase + t - 1)
                    for c in range(KC):
                        last = pe.matmul(Y[t % 2][0:R, 0:D], XT[:, c, t * R:(t + 1) * R], w[:, c, :],
                                         start=(c == 0), stop=(c == KC - 1))
                    last.then_inc(vs_ready, 1)
                for m in range(KC):
                    wide(H[m], [w[:, c, m * 128:(m + 1) * 128] for c in range(KC)],
                         [XT[:, c, :] for c in range(KC)], P, qk_ready)
                pe.wait_ge(qk_done, qbase + 2)
                k = {"l1": 0, "l2": 1}[name]
                pe.wait_ge(ab_ready, k + 1)
                for t in range(T):
                    for c in range(KC):
                        last = pe.matmul(G1[0:R, t * 8:t * 8 + heads], QT[:, c, t * R:(t + 1) * R],
                                         AD[:, c, 0:heads], start=(c == 0), stop=(c == KC - 1))
                last.then_inc(ed_ready, 1)
                per = P // dh
                for h in range(heads):
                    if h >= 2:
                        pe.wait_ge(es_done, esbase + h - 1)
                    r = slice(dh * (h % per), dh * (h % per) + dh)
                    wide(H[h % 2], [AB[r, h // per, :]], [QT[r, h // per, :]], R, es_ready)
                pe.wait_ge(vs_done, vbase + T)
                attention(UNITS[name], TILES[name], heads, dh, False)

            turn(Z, TURN["l1g"], ln_out, LN["l1g"] + 1)
            gat("l1", TURN["l1g"], GQK[:, 0, :, :], 112, 12, 15, 0)

            turn(Z, TURN["l1f"], ln_out, LN["l1f"] + 1)
            route(1, TURN["l1f"])
            sparse_experts("l1")

            turn(Z, TURN["l2g"], ln_out, LN["l2g"] + 1)
            gat("l2", TURN["l2g"], GQK[:, 1, :, :], 144, 14, 20, 4)

            turn(Z, TURN["l2f"], ln_out, LN["l2f"] + 1)
            route(2, TURN["l2f"])
            pe.wait_ge(logits_sb, 1)
            for t in range(T):
                last = pe.matmul(G0[0:R, 0:8], mean_of[:, :], LG[:, t, :], start=(t == 0), stop=(t == T - 1))
            last.then_inc(mean_logits, 1)
            for s in range(2):
                experts(s)
            pe.wait_ge(routed, 3)
            for t in range(T):
                last = pe.transpose(G5[0:EXPERTS, t, 0:R], WD[:, t, :], ident[0:R, 0:R])
            last.then_inc(wt_ready, 1)
            pe.wait_ge(wt_done, 3)
            for t in range(T):
                pe.wait_ge(y_free, 2 * T + t + 1)
                pe.matmul(Y[t % 2][0:R, 0:D], WT[:, t, :], b2[:, 2, :], start=True, stop=True).then_inc(y_ready, 1)

            turn(Z, TURN["l3g"], ln_out, LN["l3g"] + 1)
            pe.wait_ge(xt_ready, 2 * TURN["l3g"] + 2)
            pe.wait_ge(in_graph_w, 160)
            for m in range(KC):
                wide(H[m], [GQK[:, 0, c, m * 128:(m + 1) * 128] for c in range(KC)],
                     [XT[:, c, :] for c in range(KC)], P, qk_ready)
            pe.wait_ge(qk_done, 16 + 2)
            pe.wait_ge(es_done, 12 + 2)
            for m in range(KC):
                wide(H[m], [GQK[:, 1, c, m * 128:(m + 1) * 128] for c in range(KC)],
                     [KT[:, c, :] for c in range(KC)], P, qk_ready)
            pe.wait_ge(qk_done, 18 + 2)
            for t in range(T):
                if t >= 2:
                    pe.wait_ge(vs_done, 25 + t - 1)
                for c in range(KC):
                    last = pe.matmul(Y[t % 2][0:R, 0:D], QT[:, c, t * R:(t + 1) * R], GVS[:, c, 0:D],
                                     start=(c == 0), stop=(c == KC - 1))
                last.then_inc(vs_ready, 1)
            pe.wait_ge(vs_done, 25 + T)
            for t in range(T):
                if t >= 2:
                    pe.wait_ge(tile_out, 25 + t - 1)
                for s in range(T):
                    last = pe.matmul(Y[t % 2][0:R, 0:D], CT[:, s, t * R:(t + 1) * R], VS[:, s, 0:D],
                                     start=(s == 0), stop=(s == T - 1))
                last.then_inc(mixed, 1)

            turn(Z, TURN["l3f"], ln_out, LN["l3f"] + 1)
            route(3, TURN["l3f"])
            sparse_experts("l3")

        @block.scalar
        def _(act):
            own = Steps(act, act_step)
            act.sem_inc(h_free, 2)
            act.wait_ge(in_small, 64)
            own.step(act.activation(bq8[:, :], vcol("bq", 0, 6), ACT.Copy, scale=0.125))
            for k, L in enumerate([LNC, LNC2]):
                act.wait_ge(lnc_in, k + 1)
                act.activation(L[:, :, :], L[:, :, :], ACT.Ln).then_inc(lnc_ln, 1)
            for t in range(T):
                act.wait_ge(count_turned, t + 1)
                act.activation(CT[:, :, t * R:(t + 1) * R], H5[t % 2][0:R, 0:T, 0:R], ACT.Copy).then_inc(ct_copied, 1)

            def turned_in(n, dst):
                for c in range(KC):
                    act.wait_ge(turned, 2 * n + (c + 1))
                    act.activation(dst[:, c, :].rearrange("p (t r) -> p t r", r=R), H5[c][:, 0:T, 0:R], ACT.Copy)\
                       .then_inc(xt_ready, 1)

            def normal_relu(n, dst, done):
                for c in range(KC):
                    act.activation(dst[:, c, :].rearrange("p (t r) -> p t r", r=R), H5[c][:, 0:T, 0:R], ACT.Relu,
                                   bias=FBI[:, c:c + 1], scale=FSC[:, c:c + 1]).then_inc(done, 1)

            def attention(ubase, tbase, heads):
                units = T * heads

                def exps(k):
                    t, h = divmod(k, heads)
                    act.wait_ge(negmax, ubase + (k + 1))
                    if k >= 2:
                        act.wait_ge(prob_turned, ubase + (k - 1))
                    act.activation(PR[:, k % 2, :], SM[:, k % 2, :], ACT.Exp, bias=nmx[:, k % 2:k % 2 + 1],
                                   accum_out=den[:, t, h:h + 1]).then_inc(prob, 1)

                def copy(k):
                    act.wait_ge(prob_turned, ubase + (k + 1))
                    if k >= 2:
                        act.wait_ge(mixed, ubase + (k - 1))
                    act.activation(PT[:, k % 2, :, :], G5[0:R, 0:T, 0:R], ACT.Copy).then_inc(probT, 1)

                for k in range(units + 1):
                    if k < units:
                        exps(k)
                    if k >= 1:
                        copy(k - 1)

            def l0_layer(i):
                for j in range(4):
                    q, m = divmod(j, 2)
                    act.wait_ge(qk_ready, 4 * i + (j + 1))
                    if q == 0:
                        act.activation(QT[:, m, :], H[j % 2][:, 0:N], ACT.Identity,
                                       bias=bq8[:, bass.ds(2 * i + m, 1)], scale=0.125).then_inc(qk_done, 1)
                    else:
                        act.activation(KT[:, m, :], H[j % 2][:, 0:N], ACT.Identity,
                                       bias=vec[:, bass.ds(2 * i + (V["bk"] + m), 1)]).then_inc(qk_done, 1)
                attention(20 * i, T * i, 4)

            own.wait()
            turned_in(0, XT)
            with act.Fori(0, LAYERS - 1) as i:
                l0_layer(i)
                act.wait_ge(bn_affine, i + 1)
                normal_relu(i + 1, XT, xt_ready)
            l0_layer(LAYERS - 1)

            def route(k):
                act.wait_ge(route_arg, k + 1)
                if k == 3:
                    act.activation(LE[:, :, :], LX[:, :, :], ACT.Exp).then_inc(route_exp, 1)
                else:
                    act.activation(E2[:, :], E2[:, :], ACT.Exp).then_inc(route_exp, 1)

            def sparse_experts(name):
                q, jobs, jbase = STAGE[name], JOBS[name], JBASE[name]

                def block_of_tokens(b, c, i):
                    B = b + TOKEN_BLOCKS * q
                    s = c % 2
                    act.wait_ge(gathered, B + 1)
                    if name == "l1":
                        act.wait_ge(in_WA[s], 16 * i + 16 * (FILLS[name][s] + c // 2 + 1))
                    for f in range(KC):
                        src = GB[s][:, f * SLOTS:(f + 1) * SLOTS]
                        if name == "l1":
                            last = act.activation(XB[:, s, f, :], src, ACT.Identity,
                                                  bias=WA[s][:, 2058 + f:2059 + f], scale=WA[s][:, 2056 + f:2057 + f])
                        else:
                            last = act.activation(XB[:, s, f, :], src, ACT.Copy)
                    last.then_inc(xb_done, 1)
                    if name == "l0":
                        act.wait_ge(in_WA[s], 16 * i + 16 * (FILLS[name][s] + c // 2 + 1))
                    for j in range(jobs):
                        act.wait_ge(hid_ready, jobs * b + (jbase + j + 1))
                        if name == "l3":
                            if c >= 1 or j >= 2:
                                act.wait_ge(hidden, jobs * b + (jbase + j - 1))
                            w = HID3[j]
                            act.activation(SG[0:w, j % 2, 0:SLOTS], HB[j % 2][0:w, 0:SLOTS], ACT.Silu)\
                               .then_inc(gate_done, 1)
                        else:
                            for k in range(2):
                                m = 2 * j + k
                                last = act.activation(HT[:, m, 0:SLOTS], HB[j % 2][:, k * SLOTS:(k + 1) * SLOTS],
                                                      ACT.Gelu, bias=WA[s][:, 2048 + m:2049 + m])
                            last.then_inc(hidden, 1)

                token_blocks(act, block_of_tokens)

            turned_in(TURN["l0f"], XT)
            route(0)
            sparse_experts("l0")

            def gat(name, n, qbase, esbase):
                turned_in(n, XT)
                for m in range(KC):
                    act.wait_ge(qk_ready, qbase + m + 1)
                    act.activation(QT[:, m, :], H[m][:, 0:N], ACT.Copy).then_inc(qk_done, 1)
                for h in range(HEADS[name]):
                    act.wait_ge(es_ready, esbase + h + 1)
                    act.activation(HT[0:R, h, :], H[h % 2][0:R, 0:N], ACT.Copy).then_inc(es_done, 1)
                attention(UNITS[name], TILES[name], HEADS[name])

            gat("l1", TURN["l1g"], 12, 0)
            turned_in(TURN["l1f"], XT)
            route(1)
            sparse_experts("l1")
            gat("l2", TURN["l2g"], 14, 4)
            turned_in(TURN["l2f"], XT)
            for j in range(2):
                act.wait_ge(route_arg, 3 + j)
                act.activation(LE[:, 0, :], LX[:, 0, :], ACT.Exp, accum_out=ZS[:, 0:1]).then_inc(route_exp, 1)
            act.wait_ge(route_arg, 5)
            act.activation(E2[:, 0:1], E2[:, 0:1], ACT.Exp).then_inc(route_exp, 1)
            act.wait_ge(in_sel, 32)
            for s in range(2):
                for m in range(len(HID2)):
                    act.wait_ge(h_ready, len(HID2) * s + m + 1)
                    act.activation(HT[:, m, :], H[m % 2][:, 0:N], ACT.Gelu, bias=B1S[:, s, m:m + 1]).then_inc(h_free, 1)

            turned_in(TURN["l3g"], XT)
            for m in range(KC):
                act.wait_ge(qk_ready, 16 + m + 1)
                act.activation(QT[:, m, :], H[m][:, 0:N], ACT.Identity, bias=vcol("l3_b1", m)).then_inc(qk_done, 1)
            act.wait_ge(bn_affine, LAYERS + 1)
            for m in range(KC):
                act.activation(KT[:, m, :], QT[:, m, :], ACT.Relu, bias=FBI[:, m:m + 1], scale=FSC[:, m:m + 1])\
                   .then_inc(es_done, 1)
            for m in range(KC):
                act.wait_ge(qk_ready, 18 + m + 1)
                act.activation(QT[:, m, :], H[m][:, 0:N], ACT.Identity, bias=vcol("l3_b2", m)).then_inc(qk_done, 1)

            turned_in(TURN["l3f"], XT)
            act.wait_ge(route_arg, 6)
            act.activation(LE[:, :, :], LX[:, :, :], ACT.Exp).then_inc(route_exp, 1)
            sparse_experts("l3")

        @block.vector
        def _(dve):
            own = Steps(dve, vec_step)
            v = nc.vector
            v.sem_inc(y_free, 2)
            v.sem_inc(counts_free, 1)

            dve.wait_ge(in_edges, 32)
            own.step(v.tensor_scalar(src_f, src_i, 1.0, None, ALU.add))
            own.step(v.tensor_scalar(dst_f, dst_i, 1.0, None, ALU.add))
            own.wait()
            own.step(v.tensor_scalar(src_field, src_f, float(HALF + 1), None, ALU.is_ge))
            own.wait()
            own.step(v.scalar_tensor_tensor(src_lo, src_field, -float(HALF), src_f, ALU.mult, ALU.add))
            own.step(v.tensor_scalar(src_val, src_field, float(2 ** FIELD - 1), 1.0, ALU.mult, ALU.add))
            own.step(v.memset(C[:, :, :], 0.0))
            own.wait()
            dve.wait_ge(consts, 5)

            def normalise(name, src, dst):
                for t in range(T):
                    own.step(v.bn_stats(ST[:, t, :], src[:, t, :]))
                own.wait()
                for t in range(T):
                    own.step(v.bn_aggr(MV[:, t, :], ST[:, t, :]))
                own.wait()
                v.tensor_scalar(VE[:, 0:T], MV[:, :, 1], EPS, None, ALU.add).then_inc(ln_var, 1)
                dve.wait_ge(ln_rstd, LN[name] + 1)
                for t in range(T):
                    last = v.tensor_scalar(dst[:, t, :], src[:, t, :], MV[:, t, 0:1], RS[:, t:t + 1],
                                           ALU.subtract, ALU.mult)
                last.then_inc(ln_out, 1)

            dve.wait_ge(in_x, 16)
            normalise("l0g", X, Z)

            with dve.Fori(0, GROUPS) as g:
                own.enter(g, 4)
                for b in range(GROUP):
                    dve.wait_ge(onehot_free, g * GROUP + (b + 1))
                    v.tensor_scalar(OHD[:, b % RING, :], iota_n[0:R, 0:N], dst_f[:, bass.ds(g * GROUP + b, 1)], None,
                                    ALU.is_equal)
                    v.tensor_scalar(OHS[:, b % RING, :], iota_n[0:R, 0:HALF], src_lo[:, bass.ds(g * GROUP + b, 1)],
                                    src_val[:, bass.ds(g * GROUP + b, 1)], ALU.is_equal, ALU.mult)\
                     .then_inc(onehot_ready, 1)
                dve.wait_ge(onehot_free, g * GROUP + (GROUP + RING))
                v.tensor_copy(CI, PS[0:R, 0:T, 0:HALF]).then_inc(counts_free, 1)
                dve.wait_ge(counts_free, g + 2)
                own.step(v.tensor_scalar(CF, CI, 2 ** FIELD - 1, None, ALU.bitwise_and))
                own.wait()
                own.step(v.tensor_tensor(C[:, :, 0:HALF], C[:, :, 0:HALF], CF, ALU.add))
                own.wait()
                own.step(v.tensor_scalar(CF, CI, FIELD, None, ALU.logical_shift_right))
                own.wait()
                own.step(v.tensor_tensor(C[:, :, HALF:2 * HALF], C[:, :, HALF:2 * HALF], CF, ALU.add))
                own.wait()
                own.leave(GROUPS, 4)

            own.step(v.tensor_reduce(deg[:, :], C[:, :, 0:N], AX.X, ALU.add))
            v.tensor_scalar(LNC[:, :, :], C[:, :, :], 1.0, None, ALU.max).then_inc(count_all, 1)
            dve.wait_ge(count_all, 1)
            own.step(v.tensor_copy(LNC2[:, :, :], C[:, :, :]))
            own.wait()
            for t in range(T):
                diag = slice(t * R, (t + 1) * R)
                own.step(v.tensor_tensor(LNC2[:, t, diag], C[:, t, diag], ident[0:R, 0:R], ALU.add))
            own.wait()
            M1 = HT[0:R, :, :].rearrange("p a b -> p (a b)")[:, 0:T * 2 * HALF].rearrange("p (t n) -> p t n", t=T)
            v.engine_nop().then_inc(lnc_in, 1)
            own.step(v.tensor_scalar(M1, LNC2[:, :, :], 0.0, NEVER, ALU.is_equal, ALU.mult))
            own.wait()
            v.tensor_scalar(LNC2[:, :, :], LNC2[:, :, :], 1.0, None, ALU.max).then_inc(lnc_in, 1)
            dve.wait_ge(lnc_ln, 2)
            own.step(v.tensor_tensor(LNC2[:, :, :], LNC2[:, :, :], M1, ALU.add))
            own.wait()
            own.step(v.tensor_scalar(M1, C[:, :, :], 0.0, NEVER, ALU.is_equal, ALU.mult))
            own.wait()
            own.step(v.tensor_tensor(LNC[:, :, :], LNC[:, :, :], M1, ALU.add))
            own.wait()

            def take_waits():
                v.sem_inc(waits_taken, 1)

            def attention(ubase, tbase, heads, lnc, scores, finish):
                units = T * heads
                dh = D // heads

                def tile(t):
                    dve.wait_ge(mixed, ubase + heads * (t + 1))
                    own.step(v.tensor_scalar(rden[:, t, 0:heads], den[:, t, 0:heads], 1e-30, None, ALU.max))
                    own.wait()
                    own.step(v.reciprocal(rden[:, t, 0:heads], rden[:, t, 0:heads]))
                    own.wait()
                    own.step(v.tensor_tensor(
                        ON[:, :].rearrange("p (h d) -> p h d", h=heads),
                        Y[t % 2][0:R, 0:D].rearrange("p (h d) -> p h d", h=heads),
                        rden[:, t, 0:heads].unsqueeze(2).broadcast_to([R, heads, dh]), ALU.mult))
                    own.wait()
                    finish(t)

                for k in range(units + 3):
                    if k < units:
                        t, h = divmod(k, heads)
                        sc = scores(k, t, h)
                        if k >= 2:
                            dve.wait_ge(prob, ubase + (k - 1))
                        take_waits()
                        v.tensor_tensor_reduce(SM[:, k % 2, :], sc, lnc[:, t, 0:N], 1.0, FLOOR, ALU.add, ALU.max,
                                               mx[:, k % 2:k % 2 + 1]).then_inc(masked, 1)
                        dve.wait_ge(masked, ubase + (k + 1))
                        v.tensor_scalar(nmx[:, k % 2:k % 2 + 1], mx[:, k % 2:k % 2 + 1], -1.0, None, ALU.mult)\
                         .then_inc(negmax, 1)
                    if k - 2 >= heads and (k - 2) % heads == 0:
                        tile((k - 2) // heads - 1)

            def l0_layer(i):
                for t in range(T):
                    dve.wait_ge(vs_ready, T * i + (t + 1))
                    v.tensor_tensor(VS[:, t, :], Y[t % 2][0:R, :], rows[:, bass.ds(512 * i + W["bvs"], 512)], ALU.add)\
                     .then_inc(vs_done, 1)
                dve.wait_ge(vs_done, T * i + T)

                def scores(k, t, h):
                    dve.wait_ge(score_ready, 20 * i + (k + 1))
                    return H[k % 2][0:R, 0:N]

                def finish(t):
                    v.tensor_tensor(Z[:, t, :], ON[:, :], VS[:, t, D:2 * D], ALU.add).then_inc(tile_out, 1)

                attention(20 * i, T * i, 4, LNC, scores, finish)

            def affine(gamma, beta, count):
                own.wait()
                take_waits()
                for c in range(KC):
                    own.step(v.bn_aggr(FMV[:, c, :], FST[:, c, :, :].rearrange("p a b -> p (a b)")))
                own.wait()
                v.tensor_scalar(FVE[:, :], FMV[:, :, 1], EPS, None, ALU.add).then_inc(bn_var, 1)
                dve.wait_ge(bn_rstd, count + 1)
                own.step(v.tensor_tensor(FSC[:, :], gamma, FRS[:, :], ALU.mult))
                own.wait()
                own.step(v.tensor_tensor(FBI[:, :], FMV[:, :, 0], FSC[:, :], ALU.mult))
                own.wait()
                v.tensor_tensor(FBI[:, :], beta, FBI[:, :], ALU.subtract).then_inc(bn_affine, 1)

            PER_LAYER = 3 * T + 2 * KC + KC + 2
            dve.wait_ge(in_small, 64)
            with dve.Fori(0, LAYERS - 1) as i:
                own.enter(i, PER_LAYER)
                l0_layer(i)
                for c in range(KC):
                    dve.wait_ge(turned, 2 * i + (c + 3))
                    own.step(v.bn_stats(FST[:, c, 0, :], H5[c][:, 0:4, 0:R]))
                    own.step(v.bn_stats(FST[:, c, 1, :], H5[c][:, 4, 0:R]))
                affine(vec[:, bass.ds(2 * i + V["bn_g"], 2)], vec[:, bass.ds(2 * i + V["bn_b"], 2)], i)
                own.leave(LAYERS - 1, PER_LAYER)
            l0_layer(LAYERS - 1)
            dve.wait_ge(tile_out, LAYERS * T)
            own.step(v.tensor_tensor(X[:, :, :], X[:, :, :], Z[:, :, :], ALU.add))
            own.wait()

            def top_two(k, tiles):
                for t in tiles:
                    own.step(v.max(M8[:, t, :], LG[:, t, :]))
                own.wait()
                for t in tiles:
                    own.step(v.max_index(I8[:, t, :], M8[:, t, :], LG[:, t, :]))
                own.wait()

            def dense_weights():
                own.step(v.tensor_copy(IF[:, :, :], I8[:, :, 0:2]))
                own.wait()
                for j, dst in enumerate([OH0, WD]):
                    own.step(v.tensor_tensor(OHK[:, :, j, :], iota8[:, :, :],
                                             IF[:, :, j].unsqueeze(2).broadcast_to([R, T, EXPERTS]), ALU.is_equal))
                    own.wait()
                    own.step(v.tensor_tensor(dst[:, :, :], OHK[:, :, j, :],
                                             TW[:, :, j].unsqueeze(2).broadcast_to([R, T, EXPERTS]), ALU.mult))
                    own.wait()
                v.tensor_tensor(WD[:, :, :], WD[:, :, :], OH0[:, :, :], ALU.add).then_inc(routed, 1)

            def route(k, bias):
                dve.wait_ge(logits, k + 1)
                lg = G1[0:R, 0:T * EXPERTS].rearrange("p (t e) -> p t e", t=T)
                if bias is None:
                    own.step(v.tensor_copy(LG[:, :, :], lg))
                else:
                    own.step(v.tensor_tensor(LG[:, :, :], lg, over_tiles(bias, EXPERTS), ALU.add))
                own.wait()
                top_two(k, range(T))
                if k == 3:
                    v.tensor_tensor(LX[:, :, :], LG[:, :, :], M8[:, :, 0].unsqueeze(2).broadcast_to([R, T, EXPERTS]),
                                    ALU.subtract).then_inc(route_arg, 1)
                    dve.wait_ge(route_exp, 6)
                    own.step(v.tensor_reduce(ZS[:, :], LE[:, :, :], AX.X, ALU.add))
                    own.step(v.max(M8[:, 0, :], LE[:, 0, :]))
                    for t in range(1, T):
                        own.step(v.max(M8[:, t, :], LE[:, t, :]))
                    own.wait()
                    own.step(v.tensor_scalar(ZS[:, :], ZS[:, :], 1e-9, None, ALU.mult))
                    own.step(v.tensor_tensor(E2[:, :], M8[:, :, 0], M8[:, :, 1], ALU.add))
                    own.wait()
                    own.step(v.tensor_tensor(E2[:, :], E2[:, :], ZS[:, :], ALU.add))
                    own.wait()
                    own.step(v.reciprocal(E2[:, :], E2[:, :]))
                    own.wait()
                    own.step(v.tensor_tensor(TW[:, :, :], M8[:, :, 0:2],
                                             E2[:, :].unsqueeze(2).broadcast_to([R, T, 2]), ALU.mult))
                else:
                    v.tensor_tensor(E2[:, :], M8[:, :, 1], M8[:, :, 0], ALU.subtract).then_inc(route_arg, 1)
                    dve.wait_ge(route_exp, k + 1)
                    own.step(v.tensor_scalar(ZS[:, :], E2[:, :], 1.0, None, ALU.add))
                    own.wait()
                    own.step(v.reciprocal(TW[:, :, 0], ZS[:, :]))
                    own.wait()
                    own.step(v.tensor_tensor(TW[:, :, 1], TW[:, :, 0], E2[:, :], ALU.mult))
                own.wait()
                dense_weights()
                dve.wait_ge(routed, k + 1)

            def combine(s, acc, weight):
                for t in range(T):
                    idx = T * s + t
                    dve.wait_ge(y_ready, idx + 1)
                    dve.wait_ge(y_free, idx + 2)
                    v.scalar_tensor_tensor(acc[:, t, :], Y[idx % 2][0:R, 0:D], weight,
                                           acc[:, t, :], ALU.mult, ALU.add).then_inc(y_free, 1)

            def split(hi, lo, src):
                own.step(v.tensor_copy(hi, src))
                own.wait()
                own.step(v.tensor_tensor(lo, src, hi.bitcast(F32), ALU.subtract))

            def place_blocks(name):
                q = STAGE[name]
                own.step(v.tensor_tensor(SEL[:, :, :], OHK[:, :, 0, :], OHK[:, :, 1, :], ALU.add))
                own.wait()
                v.engine_nop().then_inc(selected, 1)
                if q == 0:
                    dve.wait_ge(route_consts, 11)
                own.step(v.tensor_copy(WDT[:, :, 0:EXPERTS], WD[:, :, :]))
                dve.wait_ge(ranked, q + 1)
                own.step(v.tensor_scalar(CNI[:, :], G0[:, 64:72], float(SLOTS - 1), None, ALU.add))
                own.step(v.tensor_copy(RK[:, :, :], G0[0:R, 0:T * 8].rearrange("p (t e) -> p t e", t=T)))
                own.wait()
                own.step(v.tensor_scalar(CNI[:, :], CNI[:, :], 7, None, ALU.logical_shift_right))
                own.wait()
                own.step(v.tensor_copy(NB[:, :], CNI[:, :]))
                own.step(v.tensor_copy(INC[:, :], CNI[:, :]))
                own.wait()
                for e in range(1, EXPERTS):
                    own.step(v.tensor_tensor(INC[:, e:e + 1], INC[:, e:e + 1], INC[:, e - 1:e], ALU.add))
                    own.wait()
                own.step(v.tensor_tensor(EOH[:, :, :], INC[:, :].unsqueeze(1).broadcast_to([P, BL, EXPERTS]),
                                         iota_b[:, :].unsqueeze(2).broadcast_to([P, BL, EXPERTS]), ALU.is_le))
                own.step(v.tensor_tensor(BASE[:, :], INC[:, :], NB[:, :], ALU.subtract))
                own.wait()
                own.step(v.tensor_reduce(EOB[:, :], EOH[:, :, :], AX.X, ALU.add))
                own.wait()
                own.step(v.tensor_scalar(EOB[:, :], EOB[:, :], float(EXPERTS - 1), None, ALU.min))
                own.wait()
                own.step(v.tensor_copy(EOU[:, :], EOB[:, :]))
                own.step(v.tensor_tensor(EOH[:, :, :], iota_e[:, :].unsqueeze(1).broadcast_to([P, BL, EXPERTS]),
                                         EOB[:, :].unsqueeze(2).broadcast_to([P, BL, EXPERTS]), ALU.is_equal))
                own.wait()
                v.engine_nop().then_inc(blocks_known, 1)
                own.step(v.tensor_scalar(BASE[:, :], BASE[:, :], float(SLOTS), None, ALU.mult))
                own.wait()
                own.step(v.tensor_tensor(RK[:, :, :], RK[:, :, :], over_tiles(BASE[0:R, :], EXPERTS), ALU.add))
                own.wait()
                for k in range(2):
                    own.step(v.tensor_tensor(OH0[:, :, :], OHK[:, :, k, :], RK[:, :, :], ALU.mult))
                    own.wait()
                    own.step(v.tensor_reduce(POS[:, :, k], OH0[:, :, :], AX.X, ALU.add))
                    own.wait()
                at, past = slot_work
                own.step(v.tensor_tensor(at, POS[:, :, :].rearrange("p t k -> p (t k)").unsqueeze(1)
                                         .broadcast_to([R, BL, 2 * T]), iota_p[:, :].unsqueeze(2).broadcast_to([R, BL, 2 * T]),
                                         ALU.subtract))
                own.wait()
                own.step(v.tensor_scalar(past, at, float(SLOTS), -1.0e6, ALU.is_ge, ALU.mult))
                own.wait()
                own.step(v.tensor_tensor(at, at, past, ALU.add))
                own.wait()
                own.step(v.tensor_tensor(slot_of[:, :, :], at[:, :, 0:2 * T:2], at[:, :, 1:2 * T:2], ALU.max))
                own.wait()

            def sparse_experts(name, source):
                q, jobs, jbase = STAGE[name], JOBS[name], JBASE[name]
                place_blocks(name)
                if name != "l3":
                    dve.wait_ge(wt_ready, q + 1)
                    v.tensor_copy(WT[:, :, :], G5[0:EXPERTS, 0:T, 0:R]).then_inc(wt_done, 1)
                else:
                    v.memset(WT[:, :, :], 0.0).then_inc(wt_done, 1)
                split(ZH[:, :, :], ZL[:, :, :], source)
                own.wait()
                v.engine_nop().then_inc(parts_ready, 1)

                def permutation(b):
                    B = b + TOKEN_BLOCKS * q
                    if not isinstance(b, int) or b >= 1:
                        dve.wait_ge(gathered, B)
                    for t in range(T):
                        last = v.tensor_scalar(PM[:, t, :], iota_s[0:R, :],
                                               slot_of[:, bass.ds(b, 1), t:t + 1].rearrange("p a t -> p (a t)"),
                                               None, ALU.is_equal)
                    last.then_inc(perm_ready, 1)

                def block_of_tokens(b, c, i):
                    B = b + TOKEN_BLOCKS * q
                    s = c % 2
                    last_block = isinstance(b, int) and b == TOKEN_BLOCKS - 1
                    if c == 0:
                        permutation(0)
                    dve.wait_ge(xb_done, B + 1)
                    v.tensor_copy(TI[:, :], GB[s][:, 2 * SLOTS:2 * SLOTS + 9]).then_inc(slots_read, 1)
                    dve.wait_ge(slots_read, B + 1)
                    own.step(v.tensor_tensor(TW8[:, :], TI[:, 0:EXPERTS],
                                             EOH[:, bass.ds(b, 1), :].rearrange("p a e -> p (a e)"), ALU.mult))
                    own.wait()
                    own.step(v.tensor_reduce(WSL[:, :], TW8[:, :], AX.X, ALU.add))
                    if not last_block:
                        permutation(b + 1)
                    if name == "l3":
                        for j in range(jobs):
                            w = HID3[j]
                            dve.wait_ge(gate_done, jobs * b + (j + 1))
                            v.tensor_tensor(HT[0:w, j, 0:SLOTS], HB[j % 2][0:w, SLOTS:2 * SLOTS],
                                            SG[0:w, j % 2, 0:SLOTS], ALU.mult).then_inc(hidden, 1)
                    if c >= 1:
                        dve.wait_ge(scattered, B)
                    v.tensor_scalar(SS[:, :], iota_n[:, 0:N], TI[:, EXPERTS:EXPERTS + 1], None, ALU.is_equal)\
                     .then_inc(info_done, 1)
                    dve.wait_ge(yb_ready, B + 1)
                    own.wait()
                    own.step(v.tensor_scalar(YS, YB[:, 0:D], WSL[:, 0:1], None, ALU.mult))
                    own.wait()
                    own.step(v.tensor_copy(YH[:, :], YS))
                    own.wait()
                    v.tensor_tensor(YL[:, :], YS, YH[:, :].bitcast(F32), ALU.subtract).then_inc(y_parts, 1)
                    dve.wait_ge(y_parts, B + 1)

                token_blocks(dve, block_of_tokens, own, 4)
                dve.wait_ge(scattered, TOKEN_BLOCKS * (q + 1))
                for t in range(T):
                    own.step(v.tensor_tensor(X[:, t, :], X[:, t, :], OUT[t][0:R, :], ALU.add))
                own.wait()

            normalise("l0f", X, Z)
            route(0, row("bg", 8))
            sparse_experts("l0", Z[:, :, :])

            def gat(name, slope, lnc, vbase, finish):
                heads = HEADS[name]
                dh = D // heads
                per = P // dh
                own.step(v.memset(AD[:, :, :], 0.0))
                own.step(v.tensor_copy(AB[:, :, :], vcol(name + "_as", 0, 2).unsqueeze(2).broadcast_to([P, KC, R])))
                own.wait()
                for h in range(heads):
                    r = slice(dh * (h % per), dh * (h % per) + dh)
                    c = h // per
                    last = v.tensor_copy(AD[r, c, h:h + 1], vec[r, V[name + "_ad"] + c:V[name + "_ad"] + c + 1])
                last.then_inc(ab_ready, 1)
                for t in range(T):
                    dve.wait_ge(vs_ready, vbase + t + 1)
                    v.tensor_copy(VS[:, t, 0:D], Y[t % 2][0:R, 0:D]).then_inc(vs_done, 1)
                k = {"l1": 0, "l2": 1}[name]
                dve.wait_ge(ed_ready, k + 1)
                own.step(v.tensor_copy(ED[:, :, 0:heads],
                                       G1[0:R, 0:T * 8].rearrange("p (t e) -> p t e", t=T)[:, :, 0:heads]))
                own.wait()
                dve.wait_ge(es_done, {"l1": 4, "l2": 12}[name])

                def scores(k, t, h):
                    es, ed = HT[0:R, h, :], ED[:, t, h:h + 1]
                    own.step(v.tensor_scalar(T1, es, ed, slope, ALU.add, ALU.mult))
                    own.wait()
                    own.step(v.scalar_tensor_tensor(T2, es, ed, T1, ALU.add, ALU.max))
                    own.wait()
                    if name == "l1":
                        own.step(v.tensor_scalar(T1, T2, 0.0, -1000.0, ALU.is_equal, ALU.mult))
                        own.wait()
                        own.step(v.tensor_tensor(T2, T2, T1, ALU.add))
                        own.wait()
                    return T2

                attention(UNITS[name], TILES[name], heads, lnc, scores, finish)

            normalise("l1g", X, Z)

            def add_to_x(t):
                v.tensor_tensor(X[:, t, :], X[:, t, :], ON[:, :], ALU.add).then_inc(tile_out, 1)

            gat("l1", 0.01, LNC, 15, add_to_x)
            dve.wait_ge(tile_out, 20)

            normalise("l1f", X, Z)
            dve.wait_ge(ln_out, LN["l1f"] + 1)
            normalise("l1n", Z, VS[:, :, 0:D])
            route(1, row("br1", 8))

            dve.wait_ge(ln_out, LN["l1n"] + 1)
            sparse_experts("l1", VS[:, :, 0:D])

            normalise("l2g", X, Z)

            def add_bias_and_input(t):
                own.step(v.tensor_tensor(ON[:, :], ON[:, :], row("bias2", D), ALU.add))
                own.wait()
                v.tensor_tensor(Z[:, t, :], Z[:, t, :], ON[:, :], ALU.add).then_inc(tile_out, 1)

            gat("l2", 0.2, LNC2, 20, add_bias_and_input)
            dve.wait_ge(tile_out, 25)

            def affine_add(scale, shift, name):
                dve.wait_ge(ln_out, LN[name] + 1)
                own.step(v.tensor_tensor(Z[:, :, :], Z[:, :, :], over_tiles(scale, D), ALU.mult))
                own.wait()
                own.step(v.tensor_tensor(Z[:, :, :], Z[:, :, :], over_tiles(shift, D), ALU.add))
                own.wait()
                own.step(v.tensor_tensor(X[:, :, :], X[:, :, :], Z[:, :, :], ALU.add))
                own.wait()

            normalise("l2o", Z, Z)
            affine_add(row("ln_w", D), row("ln_b", D), "l2o")

            normalise("l2f", X, Z)
            dve.wait_ge(logits, 3)
            v.tensor_copy(LG[:, :, :], G1[0:R, 0:T * EXPERTS].rearrange("p (t e) -> p t e", t=T)).then_inc(logits_sb, 1)
            dve.wait_ge(mean_logits, 1)
            one = LG[:, 0, :]
            own.step(v.tensor_tensor(one, G0[0:R, 0:EXPERTS], row("br2", 8), ALU.add))
            own.wait()

            def softmax_row(n):
                own.step(v.tensor_reduce(M8[:, 0, 0:1], one, AX.X, ALU.max))
                own.wait()
                v.tensor_scalar(LX[:, 0, :], one, M8[:, 0, 0:1], None, ALU.subtract).then_inc(route_arg, 1)
                dve.wait_ge(route_exp, n)
                own.step(v.reciprocal(ZS[:, 1:2], ZS[:, 0:1]))
                own.wait()
                own.step(v.tensor_scalar(one, LE[:, 0, :], ZS[:, 1:2], None, ALU.mult))
                own.wait()

            softmax_row(3)
            load, cap = OH0[:, 0, :], OH0[:, 1, :]
            own.step(v.tensor_scalar(load, one, float(N), None, ALU.mult))
            own.wait()
            own.step(v.tensor_scalar(load, load, 98.0, 1.0 / 98.0, ALU.max, ALU.mult))
            own.wait()
            own.step(v.reciprocal(cap, load))
            own.wait()
            own.step(v.tensor_tensor(one, one, cap, ALU.mult))
            own.wait()
            softmax_row(4)
            own.step(v.max(M8[:, 0, :], one))
            own.wait()
            v.max_index(I8[:, 0, :], M8[:, 0, :], one).then_inc(picked, 1)
            v.tensor_tensor(E2[:, 0:1], M8[:, 0, 1:2], M8[:, 0, 0:1], ALU.subtract).then_inc(route_arg, 1)
            dve.wait_ge(route_exp, 5)
            own.step(v.tensor_scalar(ZS[:, 0:1], E2[:, 0:1], 1.0, None, ALU.add))
            own.wait()
            own.step(v.reciprocal(TW[:, 0, 0:1], ZS[:, 0:1]))
            own.wait()
            own.step(v.tensor_tensor(TW[:, 0, 1:2], TW[:, 0, 0:1], E2[:, 0:1], ALU.mult))
            own.wait()
            dve.wait_ge(picked, 1)
            for t in range(1, T):
                own.step(v.tensor_copy(TW[:, t, :], TW[:, 0, :]))
                own.step(v.tensor_copy(I8[:, t, :], I8[:, 0, :]))
            own.wait()
            dense_weights()
            dve.wait_ge(routed, 3)
            for s in range(2):
                combine(s, Z, TW[:, 0, s:s + 1])
            dve.wait_ge(wt_ready, 3)
            v.tensor_copy(WT[:, :, :], G5[0:EXPERTS, 0:T, 0:R]).then_inc(wt_done, 1)
            for t in range(T):
                idx = 2 * T + t
                dve.wait_ge(y_ready, idx + 1)
                dve.wait_ge(y_free, idx + 2)
                v.tensor_tensor(Z[:, t, :], Z[:, t, :], Y[idx % 2][0:R, 0:D], ALU.add).then_inc(y_free, 1)
            dve.wait_ge(y_free, 3 * T + 2)
            normalise("l2p", Z, Z)
            affine_add(row("gamma", D), row("beta", D), "l2p")

            own.step(v.tensor_scalar(deg[:, :], deg[:, :], 1.0, None, ALU.add))
            own.wait()
            v.engine_nop().then_inc(bn_affine, 1)
            normalise("l3g", X, Z)
            for c in range(KC):
                dve.wait_ge(qk_done, 16 + c + 1)
                own.step(v.bn_stats(FST[:, c, 0, :], QT[:, c, 0:500]))
                own.step(v.bn_stats(FST[:, c, 1, :], QT[:, c, 500:N]))
            affine(vcol("l3_g", 0, 2), vcol("l3_b", 0, 2), LAYERS - 1)
            dve.wait_ge(bn_rstd, LAYERS + 1)
            for t in range(T):
                dve.wait_ge(vs_ready, 25 + t + 1)
                v.tensor_scalar(VS[:, t, 0:D], Y[t % 2][0:R, 0:D], dinv[:, t:t + 1], None, ALU.mult).then_inc(vs_done, 1)
            dve.wait_ge(vs_done, 25 + T)
            for t in range(T):
                dve.wait_ge(mixed, 120 + t + 1)
                dve.wait_ge(tile_out, 25 + t)
                own.step(v.tensor_tensor(ON[:, :], Y[t % 2][0:R, 0:D], VS[:, t, 0:D], ALU.add))
                own.wait()
                own.step(v.scalar_tensor_tensor(ON[:, :], ON[:, :], dinv[:, t:t + 1], row("b_gcn", D), ALU.mult, ALU.add))
                own.wait()
                v.tensor_tensor(X[:, t, :], X[:, t, :], ON[:, :], ALU.add).then_inc(tile_out, 1)
            dve.wait_ge(tile_out, 25 + T)

            normalise("l3f", X, Z)
            route(3, None)
            sparse_experts("l3", Z[:, :, :])
            v.engine_nop().then_inc(x_ready, 1)


def kernel(**inp):
    import numpy as np
    import concourse.bacc as bacc
    from concourse.bass_utils import run_bass_kernel_spmd

    def features(v):
        v = v.reshape(-1, v.shape[-1] // 128, 128)
        return v.reshape(-1, 128).T

    def chunks(w):
        k, m = w.shape[-2:]
        return np.moveaxis(w.reshape(w.shape[:-2] + (k // 128, 128, m)), -3, -2)

    def pad_rows(w, n):
        full = np.zeros(w.shape[:-2] + (n, w.shape[-1]), w.dtype)
        full[..., :w.shape[-2], :] = w
        return full

    i = {k: np.asarray(v) for k, v in inp.items()}
    A = {}
    A["x"] = i["x"].reshape(T, R, D).transpose(1, 0, 2)
    A["src"] = i["src"].reshape(R, BLOCKS)
    A["dst"] = i["dst"].reshape(R, BLOCKS)
    A["vec"] = np.concatenate([
        features(i["L0_gnn_bq"]), features(i["L0_gnn_bk"]), features(i["L0_gnn_bn_gamma"]),
        features(i["L0_gnn_bn_beta"]),
        features(i["L1_gnn_att"][:, :64].reshape(1, D)), features(i["L1_gnn_att"][:, 64:].reshape(1, D)),
        features(i["L2_gnn_att_src"].reshape(1, D)), features(i["L2_gnn_att_dst"].reshape(1, D)),
        features(i["L3_gnn_b1"][None]), features(i["L3_gnn_gamma"][None]), features(i["L3_gnn_beta"][None]),
        features(i["L3_gnn_b2"][None])], axis=1)
    bvs = np.concatenate([i["L0_gnn_bv"], i["L0_gnn_bs"]], axis=1).reshape(-1)
    A["rows"] = np.concatenate([bvs, i["L0_ffn_bg"], i["L1_ffn_br"], i["L2_ffn_br"], i["L2_gnn_bias"],
                                i["L2_gnn_ln_w"], i["L2_gnn_ln_b"], i["L2_ffn_gamma"], i["L2_ffn_beta"],
                                i["L3_gnn_b_gcn"]])
    A["wr"] = np.stack([chunks(i["L0_ffn_Wg"]), chunks(i["L1_ffn_Wr"]), chunks(i["L2_ffn_Wr"]),
                        chunks(i["L3_ffn_router_w"].T)], axis=1)
    A["b2"] = np.stack([i["L0_ffn_b2"], i["L1_ffn_b2"], i["L2_ffn_b2"]], axis=1)
    A["l0_wqk"] = np.stack([chunks(i["L0_gnn_Wq"]), chunks(i["L0_gnn_Wk"])], axis=2)
    A["l0_wvs"] = np.concatenate([chunks(i["L0_gnn_Wv"]), chunks(i["L0_gnn_Ws"])], axis=-1)
    A["l1_w"] = chunks(i["L1_gnn_W"].transpose(1, 0, 2).reshape(D, D))
    A["l2_w"] = chunks(i["L2_gnn_W"])
    A["l3_w"] = np.stack([chunks(i["L3_gnn_w1"].T), chunks(i["L3_gnn_w2"].T)], axis=1)
    A["l3_wg"] = chunks(i["L3_gnn_w_gcn"].T)
    for s in ("0", "1", "2"):
        for w, name in (("W1", "w1"), ("W2", "w2")):
            A[f"l{s}_{name}"] = chunks(i[f"L{s}_ffn_{w}"]).reshape(EXPERTS, P, -1)

    def per_expert(v):
        return v.reshape(EXPERTS, -1, P).transpose(0, 2, 1)

    A["l0_w1"] = np.concatenate([A["l0_w1"], per_expert(i["L0_ffn_b1"])], axis=2)
    A["l1_w1"] = np.concatenate([A["l1_w1"], per_expert(i["L1_ffn_b1"]), per_expert(i["L1_ffn_ln_g"]),
                                 per_expert(i["L1_ffn_ln_b"])], axis=2)
    A["l2_b1"] = i["L2_ffn_b1"].reshape(EXPERTS, 4, 128).transpose(0, 2, 1)
    w13 = np.stack([chunks(i["L3_ffn_w1"].transpose(0, 2, 1)), chunks(i["L3_ffn_w3"].transpose(0, 2, 1))], axis=2)
    A["l3_w13"] = w13.reshape(EXPERTS, P, -1)
    A["l3_w2"] = chunks(pad_rows(i["L3_ffn_w2"].transpose(0, 2, 1), 128 * len(HID3))).reshape(EXPERTS, P, -1)

    nc = bacc.Bacc("TRN2", target_bir_lowering=False, num_devices=1)
    arrays, aps = {}, {}
    for name, arr in A.items():
        arr = np.ascontiguousarray(arr)
        arrays[f"in_{name}"] = arr
        aps[name] = nc.dram_tensor(f"in_{name}", arr.shape, mybir.dt.from_np(arr.dtype), kind="ExternalInput").ap()
    out = nc.dram_tensor("out", (R, T, D), F32, kind="ExternalOutput").ap()
    graph_network(nc, aps, out)
    r = run_bass_kernel_spmd(nc, [arrays], core_ids=[0])
    return np.ascontiguousarray(r.results[0]["out"].transpose(1, 0, 2)).reshape(N, D)
```

```python
from contextlib import ExitStack

import concourse.bass as bass
import concourse.mybir as mybir

F32 = mybir.dt.float32
F16 = mybir.dt.float16
F32R = mybir.dt.float32r
I32 = mybir.dt.int32
U32 = mybir.dt.uint32
ALU = mybir.AluOpType
ACT = mybir.ActivationFunctionType
AX = mybir.AxisListType

N, D, EDGES = 625, 256, 20000
R, T = 125, 5
P, KC = 128, D // 128
SPLITS = [(0, 512), (512, N - 512)]
HALF = 313
FIELD = 12
PER_BLOCK, BLOCKS, GROUPS = R, EDGES // R, 5
GROUP = BLOCKS // GROUPS
RING = 4
NEVER = -1.0e30
LEAST = 2.0 ** -60
EXPERTS = 8
FLOOR = -1.0e29
LAYERS = 3
EPS = 1e-5
HID01, HID2 = [128] * 8, [128] * 4
HID3 = [128] * 5 + [682 - 640]
SLOTS = 128
TOKEN_BLOCKS = (2 * N - EXPERTS) // SLOTS + EXPERTS
LOOPED = (TOKEN_BLOCKS - 5) // 2
PAIRS = (TOKEN_BLOCKS + 1) // 2
INFO = 2 * EXPERTS + 2

V = {}
_at = 0
for _name, _n in [("bq", 6), ("bk", 6), ("bn_g", 4), ("bn_b", 4), ("l1_as", 2), ("l1_ad", 2), ("l2_as", 2), ("l2_ad", 2), ("l3_b1", 2),
                  ("l3_g", 2), ("l3_b", 2), ("l3_b2", 2)]:
    V[_name] = _at
    _at += _n
NV = _at
W = {}
_at = 0
for _name, _n in [("bvs", 3 * 512), ("bg", 8), ("br1", 8), ("br2", 8), ("bias2", D), ("ln_w", D), ("ln_b", D),
                  ("gamma", D), ("beta", D), ("b_gcn", D)]:
    W[_name] = _at
    _at += _n
NW = _at


class Steps:

    def __init__(self, eng, sem):
        self.eng, self.sem, self.base, self.n = eng, sem, 0, 0

    def step(self, ins):
        ins.then_inc(self.sem, 1)
        self.n += 1

    def wait(self):
        self.eng.wait_ge(self.sem, self.base + self.n)

    def enter(self, i, per):
        self.base0, self.n0 = self.base, self.n
        self.base, self.n = self.base + self.n + i * per, 0

    def leave(self, count, per):
        assert self.n == per, self.n
        self.base, self.n = self.base0, self.n0 + count * per


def graph_network(nc, a, out):
    with ExitStack() as ctx:
        def sb(name, shape, dt=F32):
            return ctx.enter_context(nc.sbuf_tensor(name, shape, dt))

        def sem(name):
            return ctx.enter_context(nc.semaphore(name))

        X = sb("X", [R, T, D])
        Z = sb("Z", [R, T, D])
        XT = sb("XT", [P, KC, N])
        QT = sb("QT", [P, KC, N])
        KT = sb("KT", [P, KC, N])
        VS = sb("VS", [R, T, 2 * D])
        HT = sb("HT", [P, 8, N])
        C = sb("C", [R, T, 2 * HALF])
        LNC = sb("LNC", [R, T, 2 * HALF])
        LNC2 = sb("LNC2", [R, T, 2 * HALF])
        CT = sb("CT", [R, T, N])
        WA = [sb(f"WA{s}", [P, 2 * KC * 682]) for s in range(2)]
        WB = [sb(f"WB{s}", [P, 8 * D]) for s in range(2)]
        GQK = sb("GQK", [P, 2, KC, D])
        GVS = sb("GVS", [P, KC, 2 * D])
        B1S = sb("B1S", [P, 2, 4])
        vec = sb("vec", [P, NV])
        bq8 = sb("bq8", [P, 6])
        rows = sb("rows", [R, NW])
        wr = sb("wr", [P, 4, KC, EXPERTS])
        b2 = sb("b2", [EXPERTS, 3, D])
        PT = sb("PT", [R, 2, T, R])
        edge_space = PT[:, :, :, :].rearrange("p a t r -> p (a t r)")
        src_i, dst_i = [edge_space[:, k * BLOCKS:(k + 1) * BLOCKS].bitcast(I32) for k in range(2)]
        src_f, dst_f, src_field, src_lo, src_val = [edge_space[:, k * BLOCKS:(k + 1) * BLOCKS] for k in range(2, 7)]
        iota8 = sb("iota8", [R, T, EXPERTS])
        ident = sb("ident", [P, P])
        mean_of = sb("mean_of", [R, R])
        half = sb("half", [P, 8])
        SG = sb("SG", [P, 2, N])
        OHD = SG[0:R, :, :].bitcast(F16).rearrange("p a (b n) -> p (a b) n", n=N)
        OHS = QT[0:R, :, :].rearrange("p c n -> p (c n)")[:, 0:RING * HALF // 2].bitcast(F16)\
            .rearrange("p (b n) -> p b n", n=HALF)
        CI = VS[:, :, 0:HALF].bitcast(I32)
        FIELDS = LNC[:, :, :].bitcast(I32)
        c_space = C[:, :, :].rearrange("p t n -> p (t n)")
        SM, PR = [c_space[:, k * 2 * N:(k + 1) * 2 * N].rearrange("p (a n) -> p a n", a=2) for k in range(2)]
        SC = [KT[0:R, 0, :], KT[0:R, 1, :]]
        SLOPED = [XT[0:R, 0, :], XT[0:R, 1, :]]
        RELU = QT[0:R, 0, :]
        ZERO = [QT[0:R, 0, :], QT[0:R, 1, :]]
        mx = sb("mx", [R, 2])
        nmx = sb("nmx", [R, 2])
        den = sb("den", [R, T, 8])
        rden = sb("rden", [R, T, 8])
        ON = SG[0:R, 1, SLOTS:SLOTS + D]
        AB = SG[:, :, :].rearrange("p a n -> p (a n)")[:, 384:384 + KC * R].rearrange("p (c n) -> p c n", n=R)
        AD = sb("AD", [P, KC, 8])
        ED = sb("ED", [R, T, 8])
        EDR = sb("EDR", [R, T, 8])
        ST = sb("ST", [R, T, 6])
        MV = sb("MV", [R, T, 2])
        VE = sb("VE", [R, 8])
        RS = sb("RS", [R, 8])
        FST = sb("FST", [P, KC, 2, 6])
        FMV = sb("FMV", [P, KC, 2])
        FVE = sb("FVE", [P, KC])
        FRS = sb("FRS", [P, KC])
        FSC = sb("FSC", [P, KC])
        FBI = sb("FBI", [P, KC])
        LG = sb("LG", [R, T, EXPERTS])
        LX = sb("LX", [R, T, EXPERTS])
        LE = sb("LE", [R, T, EXPERTS])
        M8 = sb("M8", [R, T, 8])
        I8 = sb("I8", [R, T, 8], U32)
        IF = sb("IF", [R, T, 2])
        E2 = sb("E2", [R, T])
        ZS = sb("ZS", [R, T])
        TW = sb("TW", [R, T, 2])
        OH0 = sb("OH0", [R, T, EXPERTS])
        WD = sb("WD", [R, T, EXPERTS])
        WT = HT[0:EXPERTS, 7, :].rearrange("p (t r) -> p t r", r=R)
        ZH, ZL = sb("ZH", [R, T, D], F32R), sb("ZL", [R, T, D], F32R)
        PM = sb("PM", [R, T, 2 * SLOTS], F32R)
        BL = 18
        slot_work = [c_space[:, k * BL * 2 * T:(k + 1) * BL * 2 * T].rearrange("p (b t) -> p b t", b=BL) for k in range(2)]
        slot_of = sb("slot_of", [R, BL, T])
        iota_p = sb("iota_p", [R, BL])
        XB = sb("XB", [P, 2, KC, SLOTS])
        SS = sb("SS", [P, N], F32R)
        YS = SG[:, 0, SLOTS:SLOTS + D]
        YH, YL = sb("YH", [P, D], F32R), sb("YL", [P, D], F32R)
        iota_s = sb("iota_s", [P, SLOTS])
        iota_n = sb("iota_n", [P, N + 1], F16)
        iota_b = sb("iota_b", [P, BL])
        iota_e = sb("iota_e", [P, EXPERTS])
        before = sb("before", [R, R])
        ones = sb("ones", [R, P])
        SEL = sb("SEL", [R, T, EXPERTS])
        OHK = sb("OHK", [R, T, 2, EXPERTS])
        WDT = sb("WDT", [R, T, INFO], F32R)
        node_of = sb("node_of", [R, T, 1])
        CNT = sb("CNT", [P, EXPERTS])
        CNI = sb("CNI", [P, EXPERTS], I32)
        NB = sb("NB", [P, EXPERTS])
        INC = sb("INC", [P, EXPERTS])
        BASE = sb("BASE", [P, EXPERTS])
        RK = sb("RK", [R, T, EXPERTS])
        POS = sb("POS", [R, T, 2])
        EOB = sb("EOB", [P, BL])
        EOU = sb("EOU", [P, BL], U32)
        EOH = sb("EOH", [P, BL, EXPERTS])
        TI = sb("TI", [P, 2, INFO])
        TW8 = sb("TW8", [P, 2, 2 * EXPERTS])
        WSL = sb("WSL", [P, 3])
        deg = sb("deg", [R, T])
        dinv = sb("dinv", [R, T])

        PS = ctx.enter_context(nc.psum_tensor("PS", [P, 8, 512], F32))
        flat = PS[:, :, :].rearrange("p b n -> p (b n)")
        H = [flat[:, 0:1024], flat[:, 1024:2048]]
        H5 = [h.rearrange("p (s n) -> p s n", n=128) for h in H]
        Y = [PS[:, 4, :], PS[:, 5, :]]
        G5 = flat[:, 3072:4096].rearrange("p (s n) -> p s n", n=128)
        G0, G1 = PS[:, 6, :], PS[:, 7, :]
        HB = [PS[:, 0, :], PS[:, 1, :]]
        GB = PS[:, 2, :].rearrange("p (f n) -> p f n", f=KC)
        IB = PS[:, 4, 0:2 * INFO].rearrange("p (b n) -> p b n", b=2)
        YB = PS[:, 3, :]
        OUT = [PS[:, 5 + t // 2, (t % 2) * D:(t % 2 + 1) * D] for t in range(T)]

        waits_taken = sem("waits_taken")
        in_edges = sem("in_edges")
        in_x = sem("in_x")
        in_small = sem("in_small")
        in_graph_w = sem("in_graph_w")
        in_WA = [sem(f"in_WA{s}") for s in range(2)]
        in_WB = [sem(f"in_WB{s}") for s in range(2)]
        consts = sem("consts")
        vec_step = sem("vec_step")
        act_step = sem("act_step")
        pool_step = sem("pool_step")
        onehot_ready = sem("onehot_ready")
        onehot_free = sem("onehot_free")
        counts_free = sem("counts_free")
        fields_out = sem("fields_out")
        converted = sem("converted")
        counted = sem("counted")
        count_all = sem("count_all")
        self_loops = sem("self_loops")
        deg_ready = sem("deg_ready")
        lnc_in = sem("lnc_in")
        lnc_ln = sem("lnc_ln")
        count_turned = sem("count_turned")
        ct_copied = sem("ct_copied")
        ln_var = sem("ln_var")
        ln_rstd = sem("ln_rstd")
        ln_out = sem("ln_out")
        bn_var = sem("bn_var")
        bn_rstd = sem("bn_rstd")
        bn_affine = sem("bn_affine")
        turned = sem("turned")
        xt_ready = sem("xt_ready")
        qk_ready = sem("qk_ready")
        qk_done = sem("qk_done")
        vs_ready = sem("vs_ready")
        vs_done = sem("vs_done")
        ab_ready = sem("ab_ready")
        ed_ready = sem("ed_ready")
        es_ready = sem("es_ready")
        es_done = sem("es_done")
        ed_done = sem("ed_done")
        sloped = sem("sloped")
        zeros = sem("zeros")
        maxed = sem("maxed")
        relued = sem("relued")
        leaky_done = sem("leaky_done")
        score_ready = sem("score_ready")
        masked = sem("masked")
        negmax = sem("negmax")
        prob = sem("prob")
        prob_turned = sem("prob_turned")
        probT = sem("probT")
        mixed = sem("mixed")
        tile_out = sem("tile_out")
        logits = sem("logits")
        logits_sb = sem("logits_sb")
        mean_logits = sem("mean_logits")
        route_arg = sem("route_arg")
        route_exp = sem("route_exp")
        routed = sem("routed")
        picked = sem("picked")
        wt_ready = sem("wt_ready")
        wt_done = sem("wt_done")
        h_ready = sem("h_ready")
        h_free = sem("h_free")
        y_ready = sem("y_ready")
        y_free = sem("y_free")
        route_consts = sem("route_consts")
        slots_read = sem("slots_read")
        selected = sem("selected")
        ranked = sem("ranked")
        blocks_known = sem("blocks_known")
        parts_ready = sem("parts_ready")
        out_begun = sem("out_begun")
        perm_ready = sem("perm_ready")
        gathered = sem("gathered")
        xb_done = sem("xb_done")
        info_done = sem("info_done")
        hid_ready = sem("hid_ready")
        gate_done = sem("gate_done")
        hidden = sem("hidden")
        yb_ready = sem("yb_ready")
        y_parts = sem("y_parts")
        scattered = sem("scattered")
        in_sel = sem("in_sel")
        x_ready = sem("x_ready")
        out_sent = sem("out_sent")

        def vcol(name, k=0, n=1):
            return vec[:, V[name] + k:V[name] + k + n]

        def row(name, n, k=0):
            return rows[:, W[name] + k:W[name] + k + n]

        def over_tiles(ap, n):
            return ap.unsqueeze(1).broadcast_to([R, T, n])

        LN = {k: i for i, k in enumerate(["l0g", "l0f", "l1g", "l1f", "l1n", "l2g", "l2o", "l2f", "l2p", "l3g", "l3f"])}
        TURN = {k: i for i, k in enumerate(["l0_0", "l0_1", "l0_2", "l0f", "l1g", "l1f", "l2g", "l2f", "l3g", "l3f"])}
        ROUTE = {"l0": 0, "l1": 1, "l2": 2, "l3": 3}
        UNITS = {"l1": 60, "l2": 80}
        TILES = {"l1": 15, "l2": 20}
        HEADS = {"l1": 4, "l2": 8}
        SLOPE = {"l1": 0.01, "l2": 0.2}
        STAGE = {"l0": 0, "l1": 1, "l3": 2}
        JOBS = {"l0": 4, "l1": 4, "l3": 6}
        JBASE = {"l0": 0, "l1": 4 * TOKEN_BLOCKS, "l3": 8 * TOKEN_BLOCKS}
        W1_COLS = {"l0": 2048 + 8, "l1": 2048 + 12, "l3": 2 * KC * 682}
        W2_COLS = {"l0": 8 * D, "l1": 8 * D, "l3": 6 * D}
        FILLS = {"l0": (0, 0), "l1": (9, 8), "l2": (18, 16), "l3": (19, 17)}

        def pair_of(c, i):
            return i + (c + 1) // 2

        def token_blocks(eng, body, steps=None, per=0):
            for b in range(3):
                body(b, b, 0)
            with eng.Fori(0, LOOPED) as i:
                if steps:
                    steps.enter(i, per)
                for c in (3, 4):
                    body(2 * i + c, c, i)
                if steps:
                    steps.leave(LOOPED, per)
            for b in range(2 * LOOPED + 3, TOKEN_BLOCKS):
                body(b, b, 0)

        block = ctx.enter_context(nc.Block())

        @block.sync
        def _(sp):
            sp.dma_start(src_i, a["src"]).then_inc(in_edges, 16)
            sp.dma_start(dst_i, a["dst"]).then_inc(in_edges, 16)
            sp.dma_start(X[:, :, :], a["x"]).then_inc(in_x, 16)

            def load_blocks(name, w1, w2):
                q, jobs, jbase = STAGE[name], JOBS[name], JBASE[name]
                sp.wait_ge(blocks_known, q + 1)

                def load(b, c, i):
                    e = sp.value_load(EOU[0:1, bass.ds(b, 1)], min_val=0, max_val=EXPERTS - 1)
                    if c >= 2:
                        sp.wait_ge(hidden, jobs * b + (jbase - jobs))
                    sp.dma_start(WA[c % 2][:, 0:W1_COLS[name]], w1[e]).then_inc(in_WA[c % 2], 16)
                    if c >= 2:
                        sp.wait_ge(yb_ready, b + (TOKEN_BLOCKS * q - 1))
                    if name == "l3":
                        sp.dma_start(WB[c % 2][:, 0:5 * D], w2[e, :, 0:5 * D]).then_inc(in_WB[c % 2], 16)
                        sp.dma_start(WB[c % 2][0:HID3[5], 5 * D:6 * D], w2[e, 0:HID3[5], 5 * D:6 * D])\
                          .then_inc(in_WB[c % 2], 16)
                    else:
                        sp.dma_start(WB[c % 2][:, 0:8 * D], w2[e]).then_inc(in_WB[c % 2], 16)

                token_blocks(sp, load)

            load_blocks("l0", a["l0_w1"], a["l0_w2"])
            load_blocks("l1", a["l1_w1"], a["l1_w2"])
            sp.wait_ge(picked, 1)
            for k in range(2):
                e = sp.value_load(I8[0:1, 0, k:k + 1], min_val=0, max_val=EXPERTS - 1)
                sp.dma_start(WA[k][:, 0:1024], a["l2_w1"][e]).then_inc(in_WA[k], 16)
                sp.dma_start(WB[k][:, 0:1024], a["l2_w2"][e]).then_inc(in_WB[k], 16)
                sp.dma_start(B1S[:, k, :], a["l2_b1"][e]).then_inc(in_sel, 16)
            load_blocks("l3", a["l3_w13"], a["l3_w2"])
            sp.wait_ge(x_ready, 1)
            sp.dma_start(out, X[:, :, :]).then_inc(out_sent, 16)
            sp.wait_ge(out_sent, 16)

        @block.gpsimd
        def _(pool):
            own = Steps(pool, pool_step)
            pool.dma_start(vec[:, :], a["vec"]).then_inc(in_small, 16)
            pool.dma_start(rows[:, :], a["rows"].partition_broadcast(R)).then_inc(in_small, 16)
            pool.dma_start(wr[:, :, :, :], a["wr"]).then_inc(in_small, 16)
            pool.dma_start(b2[:, :, :], a["b2"]).then_inc(in_small, 16)

            pool.iota(iota_n[:, :], [[1, N + 1]], base=1, channel_multiplier=0, allow_small_or_imprecise_dtypes=True)\
                .then_inc(consts, 1)
            pool.iota(iota8[:, :, :], [[0, T], [1, EXPERTS]], base=0, channel_multiplier=0,
                      allow_small_or_imprecise_dtypes=True).then_inc(consts, 1)
            pool.memset(half[:, :], -0.5).then_inc(consts, 1)
            pool.memset(mean_of[:, :], 1.0 / N).then_inc(consts, 1)
            own.step(pool.memset(ident[:, :], 0.0))
            own.wait()
            pool.affine_select(out=ident[:, :], in_=ident[:, :], compare_op=ALU.not_equal, fill=1.0, base=0,
                               pattern=[[-1, P]], channel_multiplier=1).then_inc(consts, 1)

            for tile, pattern, base in [(iota_s[:, :], [[1, SLOTS]], 0),
                                        (iota_p[:, :], [[SLOTS, BL]], 0),
                                        (iota_b[:, :], [[1, BL]], 0),
                                        (iota_e[:, :], [[1, EXPERTS]], 0)]:
                pool.iota(tile, pattern, base=base, channel_multiplier=0, allow_small_or_imprecise_dtypes=True)\
                    .then_inc(route_consts, 1)
            for t in range(T):
                pool.iota(node_of[:, t, :], [[0, 1]], base=t * R + 1, channel_multiplier=1,
                          allow_small_or_imprecise_dtypes=True).then_inc(route_consts, 1)
            own.step(pool.memset(before[:, :], 1.0))
            own.wait()
            pool.affine_select(out=before[:, :], in_=before[:, :], compare_op=ALU.is_gt, fill=0.0, base=0,
                               pattern=[[1, R]], channel_multiplier=-1).then_inc(route_consts, 1)
            pool.memset(ones[:, :], 1.0).then_inc(route_consts, 1)

            def layer_weights(i):
                pool.dma_start(GQK[:, :, :, :], a["l0_wqk"][i]).then_inc(in_graph_w, 16)
                pool.dma_start(GVS[:, :, :], a["l0_wvs"][i]).then_inc(in_graph_w, 16)

            def power(out_, in_, n, wait, value, done):
                pool.wait_ge(wait, value)
                nc.gpsimd.tensor_tensor(out_, in_, half[0:n, 0:in_.shape[1]], ALU.pow).then_inc(done, 1)

            def ln_power(name):
                power(RS[:, 0:T], VE[:, 0:T], R, ln_var, LN[name] + 1, ln_rstd)

            def slope_of(name, k):
                t, h = divmod(k, HEADS[name])
                return nc.gpsimd.tensor_scalar(SLOPED[k % 2], HT[0:R, h, :], ED[:, t, h:h + 1], SLOPE[name],
                                               ALU.add, ALU.mult)

            def zeros_added():
                units = UNITS["l2"] - UNITS["l1"]
                pool.wait_ge(ed_done, 1)
                pool.wait_ge(es_done, 4)
                slope_of("l1", 0).then_inc(sloped, 1)
                for k in range(units):
                    if k + 1 < units:
                        if k >= 1:
                            pool.wait_ge(maxed, k)
                        slope_of("l1", k + 1).then_inc(sloped, 1)
                    pool.wait_ge(zeros, k + 1)
                    nc.gpsimd.tensor_tensor(SC[k % 2], SC[k % 2], ZERO[k % 2], ALU.add).then_inc(leaky_done, 1)

            def two_parts():
                pool.wait_ge(ed_done, 2)
                pool.wait_ge(es_done, 12)
                for k in range(1, T * HEADS["l2"], 2):
                    own.step(slope_of("l2", k))
                    own.wait()
                    pool.wait_ge(relued, k // 2 + 1)
                    if k >= 2:
                        pool.wait_ge(masked, UNITS["l2"] + (k - 1))
                    nc.gpsimd.tensor_tensor(SC[1], RELU, SLOPED[1], ALU.add).then_inc(leaky_done, 1)
                    pool.wait_ge(leaky_done, T * HEADS["l1"] + k // 2 + 1)

            layer_weights(0)
            pool.wait_ge(consts, 5)
            ln_power("l0g")
            pool.sem_inc(counted, 1)
            with pool.Fori(0, GROUPS) as g:
                pool.wait_ge(counted, g + 1)
                pool.wait_ge(converted, g + 2)
                nc.gpsimd.tensor_tensor(C[:, :, :], C[:, :, :], LNC2[:, :, :], ALU.add).then_inc(counted, 1)
            pool.wait_ge(counted, GROUPS + 1)
            pool.wait_ge(count_all, 1)
            own.step(nc.gpsimd.tensor_scalar(LNC2[:, :, :], C[:, :, :], 1.0, None, ALU.mult))
            own.wait()
            for t in range(T):
                diag = slice(t * R, (t + 1) * R)
                last = nc.gpsimd.tensor_tensor(LNC2[:, t, diag], LNC2[:, t, diag], ident[0:R, 0:R], ALU.add)
            last.then_inc(self_loops, 1)
            with pool.Fori(0, LAYERS - 1) as i:
                pool.wait_ge(vs_ready, i * T + T)
                layer_weights(i + 1)
                power(FRS[:, :], FVE[:, :], P, bn_var, i + 1, bn_rstd)
            pool.wait_ge(vs_ready, LAYERS * T)
            pool.dma_start(GQK[:, 0, :, :], a["l1_w"]).then_inc(in_graph_w, 16)
            ln_power("l0f")
            ln_power("l1g")
            pool.wait_ge(qk_ready, 4 * LAYERS + 2)
            pool.dma_start(GQK[:, 1, :, :], a["l2_w"]).then_inc(in_graph_w, 16)
            pool.dma_start(GVS[:, :, 0:D], a["l3_wg"]).then_inc(in_graph_w, 16)
            zeros_added()
            for name in ["l1f", "l1n", "l2g"]:
                ln_power(name)
            two_parts()
            for name in ["l2o", "l2f", "l2p"]:
                ln_power(name)
            pool.dma_start(GQK[:, :, :, :], a["l3_w"]).then_inc(in_graph_w, 16)
            ln_power("l3g")
            power(FRS[:, :], FVE[:, :], P, bn_var, LAYERS, bn_rstd)
            power(dinv[:, :], deg[:, :], R, bn_affine, LAYERS, bn_rstd)
            ln_power("l3f")

        @block.tensor
        def _(pe):
            def turn(src, n, wait, value):
                pe.wait_ge(wait, value)
                for c in range(KC):
                    for t in range(T):
                        last = pe.transpose(H5[c][:, t, 0:R], src[:, t, c * 128:(c + 1) * 128], ident[0:R, 0:R])
                    last.then_inc(turned, 1)

            def wide(slot, lhs, rhs, rows_out, done):
                for lo, w in SPLITS:
                    for c in range(len(lhs)):
                        last = pe.matmul(slot[0:rows_out, lo:lo + w], lhs[c], rhs[c][:, lo:lo + w],
                                         start=(c == 0), stop=(c == len(lhs) - 1))
                last.then_inc(done, 1)

            pe.sem_inc(onehot_free, RING)
            with pe.Fori(0, GROUPS) as g:
                for b in range(GROUP):
                    pe.wait_ge(onehot_ready, g * GROUP + (b + 1))
                    for t in range(T):
                        if b == 0:
                            pe.wait_ge(counts_free, g * T + (t + 1))
                        last = pe.matmul(PS[0:R, t, 0:HALF], OHD[:, b % RING, t * R:(t + 1) * R],
                                         OHS[:, b % RING, :], start=(b == 0), stop=(b == GROUP - 1))
                    last.then_inc(onehot_free, 1)
            pe.wait_ge(counts_free, T * GROUPS + T)
            pe.wait_ge(consts, 5)

            def turn_counts():
                pe.wait_ge(count_all, 1)
                for t in range(T):
                    if t >= 2:
                        pe.wait_ge(ct_copied, t - 1)
                    for s in range(T):
                        last = pe.transpose(H5[t % 2][0:R, s, 0:R], C[:, t, s * R:(s + 1) * R], ident[0:R, 0:R])
                    last.then_inc(count_turned, 1)
                pe.wait_ge(ct_copied, T)

            def keep_warm(bank, n):
                for _ in range(n):
                    pe.matmul(bank, ident[:, :], ident[:, :], start=True, stop=True)

            def attention(ubase, tbase, heads, dh, scored):
                units = T * heads

                def score(k):
                    t, h = divmod(k, heads)
                    if k >= 2:
                        pe.wait_ge(masked, ubase + (k - 1))
                    r = slice(dh * (h % 2), dh * (h % 2) + dh)
                    for lo, w in SPLITS:
                        last = pe.matmul(H[k % 2][0:R, lo:lo + w], QT[r, h // 2, t * R:(t + 1) * R],
                                         KT[r, h // 2, lo:lo + w], start=True, stop=True)
                    last.then_inc(score_ready, 1)

                def turn_probs(k):
                    pe.wait_ge(prob, ubase + (k + 1))
                    if k >= 1:
                        pe.wait_ge(probT, ubase + k)
                    for s in range(T):
                        last = pe.transpose(G5[0:R, s, 0:R], PR[:, k % 2, s * R:(s + 1) * R], ident[0:R, 0:R])
                    last.then_inc(prob_turned, 1)

                def mix(k):
                    t, h = divmod(k, heads)
                    pe.wait_ge(probT, ubase + (k + 1))
                    if h == 0 and t >= 2:
                        pe.wait_ge(tile_out, tbase + (t - 1))
                    for s in range(T):
                        last = pe.matmul(Y[t % 2][0:R, h * dh:(h + 1) * dh], PT[:, k % 2, s, :],
                                         VS[:, s, h * dh:(h + 1) * dh], start=(s == 0), stop=(s == T - 1))
                    last.then_inc(mixed, 1)

                for k in range(units + 3):
                    if scored and k < units:
                        score(k)
                    if k <= 2 or not scored:
                        keep_warm(PS[:, 4, 256:384] if scored else PS[:, 0, 0:128],
                                  2 if k > 2 else 6 if scored or k > 0 else 16)
                    if 2 <= k <= units + 1:
                        turn_probs(k - 2)
                    if k >= 3:
                        mix(k - 3)

            def l0_project(i):
                pe.wait_ge(xt_ready, 2 * i + 2)
                pe.wait_ge(in_graph_w, 32 * i + 32)
                for j in range(4):
                    if j >= 2:
                        pe.wait_ge(qk_done, 4 * i + (j - 1))
                    q, m = divmod(j, 2)
                    wide(H[j % 2], [GQK[:, q, c, m * 128:(m + 1) * 128] for c in range(KC)],
                         [XT[:, c, :] for c in range(KC)], P, qk_ready)
                for t in range(T):
                    if t >= 2:
                        pe.wait_ge(vs_done, T * i + (t - 1))
                    for c in range(KC):
                        last = pe.matmul(Y[t % 2][0:R, :], XT[:, c, t * R:(t + 1) * R], GVS[:, c, :],
                                         start=(c == 0), stop=(c == KC - 1))
                    last.then_inc(vs_ready, 1)
                pe.wait_ge(qk_done, 4 * i + 4)
                pe.wait_ge(vs_done, T * i + T)

            turn(Z, 0, ln_out, LN["l0g"] + 1)
            l0_project(0)
            turn_counts()
            with pe.Fori(0, LAYERS - 1) as i:
                attention(20 * i, T * i, 4, 64, True)
                turn(Z, i + 1, tile_out, T * i + T)
                l0_project(i + 1)
            attention(20 * (LAYERS - 1), T * (LAYERS - 1), 4, 64, True)

            def route(k, n):
                pe.wait_ge(xt_ready, 2 * n + 2)
                pe.wait_ge(in_small, 64)
                for t in range(T):
                    for c in range(KC):
                        last = pe.matmul(G1[0:R, t * 8:t * 8 + 8], XT[:, c, t * R:(t + 1) * R], wr[:, k, c, :],
                                         start=(c == 0), stop=(c == KC - 1))
                last.then_inc(logits, 1)

            def experts(s):
                nh = len(HID2)
                pe.wait_ge(in_WA[s], 16 * (FILLS["l3"][s]))
                for m in range(nh):
                    pe.wait_ge(h_free, nh * s + m + 1)
                    wide(H[m % 2], [WA[s][:, c * 512 + m * 128:c * 512 + (m + 1) * 128] for c in range(KC)],
                         [XT[:, c, :] for c in range(KC)], P, h_ready)
                pe.wait_ge(in_WB[s], 16 * (FILLS["l3"][s]))
                for t in range(T):
                    pe.wait_ge(y_free, T * s + t + 1)
                    for m in range(nh):
                        if t == 0:
                            pe.wait_ge(h_free, nh * s + m + 3)
                        last = pe.matmul(Y[(T * s + t) % 2][0:R, 0:D], HT[:, m, t * R:(t + 1) * R],
                                         WB[s][:, m * D:(m + 1) * D], start=(m == 0), stop=(m == nh - 1))
                    last.then_inc(y_ready, 1)

            def sparse_experts(name):
                q, jobs, jbase = STAGE[name], JOBS[name], JBASE[name]
                hid = HID3 if name == "l3" else HID01
                n1 = 682 if name == "l3" else 1024
                pe.wait_ge(selected, q + 1)
                pe.wait_ge(route_consts, 11)
                for t in range(T):
                    for s in range(t + 1):
                        pe.matmul(G0[0:R, t * 8:t * 8 + 8], before[:, :] if s == t else ones[:, 0:R], SEL[:, s, :],
                                  start=(s == 0), stop=(s == t))
                for s in range(T):
                    last = pe.matmul(G0[:, 64:72], ones[:, :], SEL[:, s, :], start=(s == 0), stop=(s == T - 1))
                last.then_inc(ranked, 1)
                pe.wait_ge(blocks_known, q + 1)
                if name != "l3":
                    pe.wait_ge(routed, q + 1)
                    for t in range(T):
                        last = pe.transpose(G5[0:EXPERTS, t, 0:R], WD[:, t, :], ident[0:R, 0:R])
                    last.then_inc(wt_ready, 1)
                    pe.wait_ge(wt_done, q + 1)
                else:
                    pe.wait_ge(wt_done, 4)
                for t in range(T):
                    pe.matmul(OUT[t][0:R, :], WT[:, t, :], b2[:, q % 2, :], start=(t % 2 == 0), stop=(t == T - 1),
                              skip_group_check=True)

                def gather(pair, subs):
                    g = pair + PAIRS * q
                    wanted = PM[:, :, subs[0] * SLOTS:2 * SLOTS]
                    pe.wait_ge(perm_ready, g + 1)
                    if not isinstance(pair, int) or pair >= 1:
                        pe.wait_ge(slots_read, g)
                    for f in range(KC):
                        for part in (ZH, ZL):
                            for t in range(T):
                                pe.matmul(GB[:, f, subs[0] * SLOTS:2 * SLOTS], part[:, t, f * 128:(f + 1) * 128],
                                          wanted[:, t, :], start=(part is ZH and t == 0),
                                          stop=(part is ZL and t == T - 1))
                    for k in subs:
                        for t in range(T):
                            last = pe.matmul(IB[:, k, :], PM[:, t, k * SLOTS:(k + 1) * SLOTS], WDT[:, t, :],
                                             start=(t == 0), stop=(t == T - 1))
                    last.then_inc(gathered, 1)

                def scatter(b):
                    B = b + TOKEN_BLOCKS * q
                    pe.wait_ge(info_done, B + 1)
                    pe.wait_ge(y_parts, B + 1)
                    for t in range(T):
                        for part in (YH, YL):
                            last = pe.matmul(OUT[t][0:R, :], SS[:, t * R:(t + 1) * R], part[:, :],
                                             start=False, stop=False, skip_group_check=True)
                    last.then_inc(scattered, 1)

                def block_of_tokens(b, c, i):
                    B = b + TOKEN_BLOCKS * q
                    s = c % 2
                    last_block = isinstance(b, int) and b == TOKEN_BLOCKS - 1
                    if c == 0:
                        pe.wait_ge(parts_ready, q + 1)
                        gather(0, [1])
                    pe.wait_ge(in_WA[s], 16 * i + 16 * (FILLS[name][s] + c // 2 + 1))
                    pe.wait_ge(xb_done, B + 1)
                    for j in range(jobs):
                        if c >= 1 or j >= 2:
                            pe.wait_ge(hidden, jobs * b + (jbase + j - 1))
                        for k in range(2):
                            if name == "l3":
                                w, at = hid[j], 2 * k * n1 + j * 128
                            else:
                                w, at = 128, (2 * j + k) * 128
                            for f in range(KC):
                                last = pe.matmul(HB[j % 2][0:w, k * SLOTS:(k + 1) * SLOTS],
                                                 WA[s][:, f * n1 + at:f * n1 + at + w], XB[:, s, f, :],
                                                 start=(f == 0), stop=(f == KC - 1))
                        last.then_inc(hid_ready, 1)
                    if c >= 1:
                        scatter(b - 1)
                    if c % 2 == 0 and not last_block:
                        gather(pair_of(c + 1, i), [0, 1])
                    loads = 2 if name == "l3" else 1
                    pe.wait_ge(in_WB[s], 16 * loads * i + 16 * (FILLS[name][s] + loads * (c // 2 + 1)))
                    for m, w in enumerate(hid):
                        if name == "l3" or m % 2 == 0:
                            job = m if name == "l3" else m // 2
                            pe.wait_ge(hidden, jobs * b + (jbase + job + 1))
                        last = pe.matmul(YB[:, 0:D], HT[0:w, m, 0:SLOTS], WB[s][0:w, m * D:(m + 1) * D],
                                         start=(m == 0), stop=(m == len(hid) - 1))
                    last.then_inc(yb_ready, 1)
                    if last_block:
                        scatter(b)

                token_blocks(pe, block_of_tokens)

            turn(Z, TURN["l0f"], ln_out, LN["l0f"] + 1)
            route(0, TURN["l0f"])
            sparse_experts("l0")

            def gat(name, n, w, wload, qbase, vbase, esbase):
                heads = HEADS[name]
                dh = D // heads
                pe.wait_ge(xt_ready, 2 * n + 2)
                pe.wait_ge(in_graph_w, wload)
                for t in range(T):
                    if t >= 2:
                        pe.wait_ge(vs_done, vbase + t - 1)
                    for c in range(KC):
                        last = pe.matmul(Y[t % 2][0:R, 0:D], XT[:, c, t * R:(t + 1) * R], w[:, c, :],
                                         start=(c == 0), stop=(c == KC - 1))
                    last.then_inc(vs_ready, 1)
                for m in range(KC):
                    wide(H[m], [w[:, c, m * 128:(m + 1) * 128] for c in range(KC)],
                         [XT[:, c, :] for c in range(KC)], P, qk_ready)
                pe.wait_ge(qk_done, qbase + 2)
                k = {"l1": 0, "l2": 1}[name]
                pe.wait_ge(ab_ready, k + 1)
                for t in range(T):
                    for c in range(KC):
                        last = pe.matmul(G1[0:R, t * 8:t * 8 + heads], QT[:, c, t * R:(t + 1) * R],
                                         AD[:, c, 0:heads], start=(c == 0), stop=(c == KC - 1))
                last.then_inc(ed_ready, 1)
                per = P // dh
                for h in range(heads):
                    if h >= 2:
                        pe.wait_ge(es_done, esbase + h - 1)
                    r = slice(dh * (h % per), dh * (h % per) + dh)
                    wide(H[h % 2], [AB[r, h // per, :]], [QT[r, h // per, :]], R, es_ready)
                pe.wait_ge(vs_done, vbase + T)
                pe.wait_ge(es_done, esbase + heads)
                attention(UNITS[name], TILES[name], heads, dh, False)

            turn(Z, TURN["l1g"], ln_out, LN["l1g"] + 1)
            gat("l1", TURN["l1g"], GQK[:, 0, :, :], 112, 12, 15, 0)

            turn(Z, TURN["l1f"], ln_out, LN["l1f"] + 1)
            route(1, TURN["l1f"])
            sparse_experts("l1")

            turn(Z, TURN["l2g"], ln_out, LN["l2g"] + 1)
            gat("l2", TURN["l2g"], GQK[:, 1, :, :], 144, 14, 20, 4)

            turn(Z, TURN["l2f"], ln_out, LN["l2f"] + 1)
            route(2, TURN["l2f"])
            pe.wait_ge(logits_sb, 1)
            for t in range(T):
                last = pe.matmul(G0[0:R, 0:8], mean_of[:, :], LG[:, t, :], start=(t == 0), stop=(t == T - 1))
            last.then_inc(mean_logits, 1)
            for s in range(2):
                experts(s)
            pe.wait_ge(routed, 3)
            for t in range(T):
                last = pe.transpose(G5[0:EXPERTS, t, 0:R], WD[:, t, :], ident[0:R, 0:R])
            last.then_inc(wt_ready, 1)
            pe.wait_ge(wt_done, 3)
            for t in range(T):
                pe.wait_ge(y_free, 2 * T + t + 1)
                pe.matmul(Y[t % 2][0:R, 0:D], WT[:, t, :], b2[:, 2, :], start=True, stop=True).then_inc(y_ready, 1)

            for t in range(T):
                for k in range(T):
                    last = pe.matmul(G0[0:R, t:t + 1], CT[:, k, t * R:(t + 1) * R], ones[:, 0:1],
                                     start=(k == 0), stop=(k == T - 1))
            last.then_inc(deg_ready, 1)

            turn(Z, TURN["l3g"], ln_out, LN["l3g"] + 1)
            pe.wait_ge(xt_ready, 2 * TURN["l3g"] + 2)
            pe.wait_ge(in_graph_w, 160)
            for m in range(KC):
                wide(H[m], [GQK[:, 0, c, m * 128:(m + 1) * 128] for c in range(KC)],
                     [XT[:, c, :] for c in range(KC)], P, qk_ready)
            pe.wait_ge(qk_done, 16 + 2)
            pe.wait_ge(es_done, 12 + 2)
            for m in range(KC):
                wide(H[m], [GQK[:, 1, c, m * 128:(m + 1) * 128] for c in range(KC)],
                     [KT[:, c, :] for c in range(KC)], P, qk_ready)
            pe.wait_ge(qk_done, 18 + 2)
            for t in range(T):
                if t >= 2:
                    pe.wait_ge(vs_done, 25 + t - 1)
                for c in range(KC):
                    last = pe.matmul(Y[t % 2][0:R, 0:D], QT[:, c, t * R:(t + 1) * R], GVS[:, c, 0:D],
                                     start=(c == 0), stop=(c == KC - 1))
                last.then_inc(vs_ready, 1)
            pe.wait_ge(vs_done, 25 + T)
            for t in range(T):
                if t >= 2:
                    pe.wait_ge(tile_out, 25 + t - 1)
                for s in range(T):
                    last = pe.matmul(Y[t % 2][0:R, 0:D], CT[:, s, t * R:(t + 1) * R], VS[:, s, 0:D],
                                     start=(s == 0), stop=(s == T - 1))
                last.then_inc(mixed, 1)

            turn(Z, TURN["l3f"], ln_out, LN["l3f"] + 1)
            route(3, TURN["l3f"])
            sparse_experts("l3")

        @block.scalar
        def _(act):
            own = Steps(act, act_step)
            act.sem_inc(h_free, 2)
            act.wait_ge(in_small, 64)
            own.step(act.activation(bq8[:, :], vcol("bq", 0, 6), ACT.Copy, scale=0.125))
            act.sem_inc(converted, 1)
            with act.Fori(0, GROUPS) as g:
                act.wait_ge(fields_out, 2 * g + 2)
                act.wait_ge(counted, g + 1)
                act.activation(LNC2[:, :, :], FIELDS, ACT.Copy).then_inc(converted, 1)
                act.wait_ge(onehot_free, g * GROUP + (GROUP + RING))
                for t in range(T):
                    act.activation(CI[:, t, :], PS[0:R, t, 0:HALF], ACT.Copy).then_inc(counts_free, 1)

            def turned_in(n, dst):
                for c in range(KC):
                    act.wait_ge(turned, 2 * n + (c + 1))
                    act.activation(dst[:, c, :].rearrange("p (t r) -> p t r", r=R), H5[c][:, 0:T, 0:R], ACT.Copy)\
                       .then_inc(xt_ready, 1)

            def normal_relu(n, dst, done):
                for c in range(KC):
                    act.activation(dst[:, c, :].rearrange("p (t r) -> p t r", r=R), H5[c][:, 0:T, 0:R], ACT.Relu,
                                   bias=FBI[:, c:c + 1], scale=FSC[:, c:c + 1]).then_inc(done, 1)

            def attention(ubase, tbase, heads, relu=None):
                units = T * heads

                def exps(k):
                    t, h = divmod(k, heads)
                    act.wait_ge(negmax, ubase + (k + 1))
                    if k >= 2:
                        act.wait_ge(prob_turned, ubase + (k - 1))
                    act.activation(PR[:, k % 2, :], SM[:, k % 2, :], ACT.Exp, bias=nmx[:, k % 2:k % 2 + 1],
                                   accum_out=den[:, t, h:h + 1]).then_inc(prob, 1)

                def copy(k):
                    act.wait_ge(prob_turned, ubase + (k + 1))
                    if k >= 2:
                        act.wait_ge(mixed, ubase + (k - 1))
                    act.activation(PT[:, k % 2, :, :], G5[0:R, 0:T, 0:R], ACT.Copy).then_inc(probT, 1)

                if relu:
                    relu(1)
                for k in range(units + 2):
                    if relu and k % 2 == 0 and k + 3 < units:
                        relu(k + 3)
                    if k >= 2:
                        copy(k - 2)
                    if k < units:
                        exps(k)

            def log_counts(k, L):
                act.wait_ge(lnc_in, k + 1)
                act.activation(L[:, :, :], L[:, :, :], ACT.Ln).then_inc(lnc_ln, 1)

            def l0_project(i):
                for j in range(4):
                    if isinstance(i, int) and j == 2:
                        log_counts(0, LNC)
                    q, m = divmod(j, 2)
                    act.wait_ge(qk_ready, 4 * i + (j + 1))
                    if q == 0:
                        act.activation(QT[:, m, :], H[j % 2][:, 0:N], ACT.Identity,
                                       bias=bq8[:, bass.ds(2 * i + m, 1)], scale=0.125).then_inc(qk_done, 1)
                    else:
                        act.activation(KT[:, m, :], H[j % 2][:, 0:N], ACT.Identity,
                                       bias=vec[:, bass.ds(2 * i + (V["bk"] + m), 1)]).then_inc(qk_done, 1)

            own.wait()
            turned_in(0, XT)
            l0_project(0)
            log_counts(1, LNC2)
            for t in range(T):
                act.wait_ge(count_turned, t + 1)
                act.activation(CT[:, :, t * R:(t + 1) * R], H5[t % 2][0:R, 0:T, 0:R], ACT.Copy).then_inc(ct_copied, 1)
            with act.Fori(0, LAYERS - 1) as i:
                attention(20 * i, T * i, 4)
                act.wait_ge(bn_affine, i + 1)
                normal_relu(i + 1, XT, xt_ready)
                l0_project(i + 1)
            attention(20 * (LAYERS - 1), T * (LAYERS - 1), 4)

            def route(k):
                act.wait_ge(route_arg, k + 1)
                if k == 3:
                    act.activation(LE[:, :, :], LX[:, :, :], ACT.Exp).then_inc(route_exp, 1)
                else:
                    act.activation(E2[:, :], E2[:, :], ACT.Exp).then_inc(route_exp, 1)

            def sparse_experts(name):
                q, jobs, jbase = STAGE[name], JOBS[name], JBASE[name]

                def block_of_tokens(b, c, i):
                    B = b + TOKEN_BLOCKS * q
                    s = c % 2
                    act.wait_ge(gathered, pair_of(c, i) + (PAIRS * q + 1))
                    if name == "l1":
                        act.wait_ge(in_WA[s], 16 * i + 16 * (FILLS[name][s] + c // 2 + 1))
                    for f in range(KC):
                        src = GB[:, f, (1 - s) * SLOTS:(2 - s) * SLOTS]
                        if name == "l1":
                            last = act.activation(XB[:, s, f, :], src, ACT.Identity,
                                                  bias=WA[s][:, 2058 + f:2059 + f], scale=WA[s][:, 2056 + f:2057 + f])
                        else:
                            last = act.activation(XB[:, s, f, :], src, ACT.Copy)
                    last.then_inc(xb_done, 1)
                    if name == "l0":
                        act.wait_ge(in_WA[s], 16 * i + 16 * (FILLS[name][s] + c // 2 + 1))
                    for j in range(jobs):
                        act.wait_ge(hid_ready, jobs * b + (jbase + j + 1))
                        if name == "l3":
                            if c >= 1 or j >= 2:
                                act.wait_ge(hidden, jobs * b + (jbase + j - 1))
                            w = HID3[j]
                            act.activation(SG[0:w, j % 2, 0:SLOTS], HB[j % 2][0:w, 0:SLOTS], ACT.Silu)\
                               .then_inc(gate_done, 1)
                        else:
                            for k in range(2):
                                m = 2 * j + k
                                last = act.activation(HT[:, m, 0:SLOTS], HB[j % 2][:, k * SLOTS:(k + 1) * SLOTS],
                                                      ACT.Gelu, bias=WA[s][:, 2048 + m:2049 + m])
                            last.then_inc(hidden, 1)

                token_blocks(act, block_of_tokens)

            turned_in(TURN["l0f"], XT)
            route(0)
            sparse_experts("l0")

            def gat(name, n, qbase, esbase):
                turned_in(n, XT)
                for m in range(KC):
                    act.wait_ge(qk_ready, qbase + m + 1)
                    act.activation(QT[:, m, :], H[m][:, 0:N], ACT.Copy).then_inc(qk_done, 1)
                for h in range(HEADS[name]):
                    act.wait_ge(es_ready, esbase + h + 1)
                    act.activation(HT[0:R, h, :], H[h % 2][0:R, 0:N], ACT.Copy).then_inc(es_done, 1)

                def relu(k):
                    t, h = divmod(k, HEADS[name])
                    if k >= 2:
                        act.wait_ge(leaky_done, T * HEADS["l1"] + k // 2)
                    act.activation(RELU, HT[0:R, h, :], ACT.Relu, bias=EDR[:, t, h:h + 1], scale=1.0 - SLOPE["l2"])\
                       .then_inc(relued, 1)

                if name == "l2":
                    act.wait_ge(ed_done, 2)
                    attention(UNITS[name], TILES[name], HEADS[name], relu)
                else:
                    attention(UNITS[name], TILES[name], HEADS[name])

            gat("l1", TURN["l1g"], 12, 0)
            turned_in(TURN["l1f"], XT)
            route(1)
            sparse_experts("l1")
            gat("l2", TURN["l2g"], 14, 4)
            turned_in(TURN["l2f"], XT)
            for j in range(2):
                act.wait_ge(route_arg, 3 + j)
                act.activation(LE[:, 0, :], LX[:, 0, :], ACT.Exp, accum_out=ZS[:, 0:1]).then_inc(route_exp, 1)
            act.wait_ge(route_arg, 5)
            act.activation(E2[:, 0:1], E2[:, 0:1], ACT.Exp).then_inc(route_exp, 1)
            act.wait_ge(in_sel, 32)
            for s in range(2):
                for m in range(len(HID2)):
                    act.wait_ge(h_ready, len(HID2) * s + m + 1)
                    act.activation(HT[:, m, :], H[m % 2][:, 0:N], ACT.Gelu, bias=B1S[:, s, m:m + 1]).then_inc(h_free, 1)

            turned_in(TURN["l3g"], XT)
            for m in range(KC):
                act.wait_ge(qk_ready, 16 + m + 1)
                act.activation(QT[:, m, :], H[m][:, 0:N], ACT.Identity, bias=vcol("l3_b1", m)).then_inc(qk_done, 1)
            act.wait_ge(bn_affine, LAYERS + 1)
            for m in range(KC):
                act.activation(KT[:, m, :], QT[:, m, :], ACT.Relu, bias=FBI[:, m:m + 1], scale=FSC[:, m:m + 1])\
                   .then_inc(es_done, 1)
            for m in range(KC):
                act.wait_ge(qk_ready, 18 + m + 1)
                act.activation(QT[:, m, :], H[m][:, 0:N], ACT.Identity, bias=vcol("l3_b2", m)).then_inc(qk_done, 1)

            turned_in(TURN["l3f"], XT)
            act.wait_ge(route_arg, 6)
            act.activation(LE[:, :, :], LX[:, :, :], ACT.Exp).then_inc(route_exp, 1)
            sparse_experts("l3")

        @block.vector
        def _(dve):
            own = Steps(dve, vec_step)
            v = nc.vector
            v.sem_inc(y_free, 2)
            v.sem_inc(counts_free, T)

            dve.wait_ge(in_edges, 32)
            own.step(v.tensor_scalar(src_f, src_i, 1.0, None, ALU.add))
            own.step(v.tensor_scalar(dst_f, dst_i, 1.0, None, ALU.add))
            own.wait()
            own.step(v.tensor_scalar(src_field, src_f, float(HALF + 1), None, ALU.is_ge))
            own.wait()
            own.step(v.scalar_tensor_tensor(src_lo, src_field, -float(HALF), src_f, ALU.mult, ALU.add))
            own.step(v.tensor_scalar(src_val, src_field, float(2 ** FIELD - 1), 1.0, ALU.mult, ALU.add))
            own.step(v.memset(C[:, :, :], 0.0))
            own.step(v.memset(VS[:, :, 0:HALF], 0.0))
            own.wait()
            dve.wait_ge(consts, 5)

            def normalise(name, src, dst):
                for t in range(T):
                    own.step(v.bn_stats(ST[:, t, :], src[:, t, :]))
                own.wait()
                for t in range(T):
                    own.step(v.bn_aggr(MV[:, t, :], ST[:, t, :]))
                own.wait()
                v.tensor_scalar(VE[:, 0:T], MV[:, :, 1], EPS, None, ALU.add).then_inc(ln_var, 1)
                dve.wait_ge(ln_rstd, LN[name] + 1)
                for t in range(T):
                    last = v.tensor_scalar(dst[:, t, :], src[:, t, :], MV[:, t, 0:1], RS[:, t:t + 1],
                                           ALU.subtract, ALU.mult)
                last.then_inc(ln_out, 1)

            dve.wait_ge(in_x, 16)
            normalise("l0g", X, Z)

            def unpack():
                return (v.tensor_scalar(FIELDS[:, :, 0:HALF], CI, 2 ** FIELD - 1, None, ALU.bitwise_and),
                        v.tensor_scalar(FIELDS[:, :, HALF:2 * HALF], CI, FIELD, None, ALU.logical_shift_right))

            with dve.Fori(0, GROUPS) as g:
                for b in range(GROUP):
                    dve.wait_ge(onehot_free, g * GROUP + (b + 1))
                    v.tensor_scalar(OHD[:, b % RING, :], iota_n[0:R, 0:N], dst_f[:, bass.ds(g * GROUP + b, 1)], None,
                                    ALU.is_equal)
                    v.tensor_scalar(OHS[:, b % RING, :], iota_n[0:R, 0:HALF], src_lo[:, bass.ds(g * GROUP + b, 1)],
                                    src_val[:, bass.ds(g * GROUP + b, 1)], ALU.is_equal, ALU.mult)\
                     .then_inc(onehot_ready, 1)
                    if b == 2 * RING:
                        dve.wait_ge(counts_free, g * T + T)
                        dve.wait_ge(converted, g + 1)
                        for field in unpack():
                            field.then_inc(fields_out, 1)
            dve.wait_ge(counts_free, GROUPS * T + T)
            dve.wait_ge(converted, GROUPS + 1)
            for field in unpack():
                own.step(field)
            dve.wait_ge(counted, GROUPS + 1)
            own.wait()
            v.tensor_tensor(C[:, :, :], C[:, :, :], FIELDS, ALU.add).then_inc(count_all, 1)
            dve.wait_ge(count_all, 1)

            v.tensor_scalar(LNC[:, :, :], C[:, :, :], LEAST, None, ALU.max).then_inc(lnc_in, 1)
            M1 = HT[0:R, :, :].rearrange("p a b -> p (a b)")[:, 0:T * 2 * HALF].rearrange("p (t n) -> p t n", t=T)
            dve.wait_ge(self_loops, 1)
            v.tensor_scalar(LNC2[:, :, :], LNC2[:, :, :], LEAST, None, ALU.max).then_inc(lnc_in, 1)

            def never(into, logs):
                own.step(v.tensor_scalar(into, logs, -1.0, NEVER, ALU.is_lt, ALU.mult))
                own.wait()

            def take_waits():
                v.sem_inc(waits_taken, 1)

            def attention(ubase, tbase, heads, lnc, scores, finish):
                units = T * heads
                dh = D // heads

                def tile(t):
                    dve.wait_ge(mixed, ubase + heads * (t + 1))
                    own.step(v.tensor_scalar(rden[:, t, 0:heads], den[:, t, 0:heads], 1e-30, None, ALU.max))
                    own.wait()
                    own.step(v.reciprocal(rden[:, t, 0:heads], rden[:, t, 0:heads]))
                    own.wait()
                    own.step(v.tensor_tensor(
                        ON.rearrange("p (h d) -> p h d", h=heads),
                        Y[t % 2][0:R, 0:D].rearrange("p (h d) -> p h d", h=heads),
                        rden[:, t, 0:heads].unsqueeze(2).broadcast_to([R, heads, dh]), ALU.mult))
                    own.wait()
                    finish(t)

                for k in range(units + 4):
                    if k < units:
                        t, h = divmod(k, heads)
                        sc = scores(k, t, h)
                        if k >= 2:
                            dve.wait_ge(prob, ubase + (k - 1))
                        take_waits()
                        v.tensor_tensor_reduce(SM[:, k % 2, :], sc, lnc[:, t, 0:N], 1.0, FLOOR, ALU.add, ALU.max,
                                               mx[:, k % 2:k % 2 + 1]).then_inc(masked, 1)
                        dve.wait_ge(masked, ubase + (k + 1))
                        v.tensor_scalar(nmx[:, k % 2:k % 2 + 1], mx[:, k % 2:k % 2 + 1], -1.0, None, ALU.mult)\
                         .then_inc(negmax, 1)
                    if k - 3 >= heads and (k - 3) % heads == 0:
                        tile((k - 3) // heads - 1)

            def l0_project(i):
                for t in range(T):
                    dve.wait_ge(vs_ready, T * i + (t + 1))
                    v.tensor_tensor(VS[:, t, :], Y[t % 2][0:R, :], rows[:, bass.ds(512 * i + W["bvs"], 512)], ALU.add)\
                     .then_inc(vs_done, 1)
                dve.wait_ge(vs_done, T * i + T)

            def l0_attention(i):
                def scores(k, t, h):
                    dve.wait_ge(score_ready, 20 * i + (k + 1))
                    return H[k % 2][0:R, 0:N]

                def finish(t):
                    v.tensor_tensor(Z[:, t, :], ON, VS[:, t, D:2 * D], ALU.add).then_inc(tile_out, 1)

                attention(20 * i, T * i, 4, LNC, scores, finish)

            def affine(gamma, beta, count):
                own.wait()
                take_waits()
                for c in range(KC):
                    own.step(v.bn_aggr(FMV[:, c, :], FST[:, c, :, :].rearrange("p a b -> p (a b)")))
                own.wait()
                v.tensor_scalar(FVE[:, :], FMV[:, :, 1], EPS, None, ALU.add).then_inc(bn_var, 1)
                dve.wait_ge(bn_rstd, count + 1)
                own.step(v.tensor_tensor(FSC[:, :], gamma, FRS[:, :], ALU.mult))
                own.wait()
                own.step(v.tensor_tensor(FBI[:, :], FMV[:, :, 0], FSC[:, :], ALU.mult))
                own.wait()
                v.tensor_tensor(FBI[:, :], beta, FBI[:, :], ALU.subtract).then_inc(bn_affine, 1)

            PER_LAYER = 3 * T + 2 * KC + KC + 2
            dve.wait_ge(in_small, 64)
            dve.wait_ge(lnc_ln, 1)
            never(M1, LNC[:, :, :])
            l0_project(0)
            own.step(v.tensor_tensor(LNC[:, :, :], LNC[:, :, :], M1, ALU.add))
            own.wait()
            dve.wait_ge(ct_copied, T)
            dve.wait_ge(lnc_ln, 2)
            with dve.Fori(0, LAYERS - 1) as i:
                own.enter(i, PER_LAYER)
                l0_attention(i)
                for c in range(KC):
                    dve.wait_ge(turned, 2 * i + (c + 3))
                    own.step(v.bn_stats(FST[:, c, 0, :], H5[c][:, 0:4, 0:R]))
                    own.step(v.bn_stats(FST[:, c, 1, :], H5[c][:, 4, 0:R]))
                affine(vec[:, bass.ds(2 * i + V["bn_g"], 2)], vec[:, bass.ds(2 * i + V["bn_b"], 2)], i)
                l0_project(i + 1)
                own.leave(LAYERS - 1, PER_LAYER)
            l0_attention(LAYERS - 1)
            dve.wait_ge(tile_out, LAYERS * T)
            own.step(v.tensor_tensor(X[:, :, :], X[:, :, :], Z[:, :, :], ALU.add))
            own.wait()

            def top_two(k, tiles):
                for t in tiles:
                    own.step(v.max(M8[:, t, :], LG[:, t, :]))
                own.wait()
                for t in tiles:
                    own.step(v.max_index(I8[:, t, :], M8[:, t, :], LG[:, t, :]))
                own.wait()

            def dense_weights():
                own.step(v.tensor_copy(IF[:, :, :], I8[:, :, 0:2]))
                own.wait()
                for j, dst in enumerate([OH0, WD]):
                    own.step(v.tensor_tensor(OHK[:, :, j, :], iota8[:, :, :],
                                             IF[:, :, j].unsqueeze(2).broadcast_to([R, T, EXPERTS]), ALU.is_equal))
                    own.wait()
                    own.step(v.tensor_tensor(dst[:, :, :], OHK[:, :, j, :],
                                             TW[:, :, j].unsqueeze(2).broadcast_to([R, T, EXPERTS]), ALU.mult))
                    own.wait()
                v.tensor_tensor(WD[:, :, :], WD[:, :, :], OH0[:, :, :], ALU.add).then_inc(routed, 1)

            def route(k, bias):
                dve.wait_ge(logits, k + 1)
                lg = G1[0:R, 0:T * EXPERTS].rearrange("p (t e) -> p t e", t=T)
                if bias is None:
                    own.step(v.tensor_copy(LG[:, :, :], lg))
                else:
                    own.step(v.tensor_tensor(LG[:, :, :], lg, over_tiles(bias, EXPERTS), ALU.add))
                own.wait()
                top_two(k, range(T))
                if k == 3:
                    v.tensor_tensor(LX[:, :, :], LG[:, :, :], M8[:, :, 0].unsqueeze(2).broadcast_to([R, T, EXPERTS]),
                                    ALU.subtract).then_inc(route_arg, 1)
                    dve.wait_ge(route_exp, 6)
                    own.step(v.tensor_reduce(ZS[:, :], LE[:, :, :], AX.X, ALU.add))
                    own.step(v.max(M8[:, 0, :], LE[:, 0, :]))
                    for t in range(1, T):
                        own.step(v.max(M8[:, t, :], LE[:, t, :]))
                    own.wait()
                    own.step(v.tensor_scalar(ZS[:, :], ZS[:, :], 1e-9, None, ALU.mult))
                    own.step(v.tensor_tensor(E2[:, :], M8[:, :, 0], M8[:, :, 1], ALU.add))
                    own.wait()
                    own.step(v.tensor_tensor(E2[:, :], E2[:, :], ZS[:, :], ALU.add))
                    own.wait()
                    own.step(v.reciprocal(E2[:, :], E2[:, :]))
                    own.wait()
                    own.step(v.tensor_tensor(TW[:, :, :], M8[:, :, 0:2],
                                             E2[:, :].unsqueeze(2).broadcast_to([R, T, 2]), ALU.mult))
                else:
                    v.tensor_tensor(E2[:, :], M8[:, :, 1], M8[:, :, 0], ALU.subtract).then_inc(route_arg, 1)
                    dve.wait_ge(route_exp, k + 1)
                    own.step(v.tensor_scalar(ZS[:, :], E2[:, :], 1.0, None, ALU.add))
                    own.wait()
                    own.step(v.reciprocal(TW[:, :, 0], ZS[:, :]))
                    own.wait()
                    own.step(v.tensor_tensor(TW[:, :, 1], TW[:, :, 0], E2[:, :], ALU.mult))
                own.wait()
                dense_weights()
                dve.wait_ge(routed, k + 1)

            def combine(s, acc, weight):
                for t in range(T):
                    idx = T * s + t
                    dve.wait_ge(y_ready, idx + 1)
                    dve.wait_ge(y_free, idx + 2)
                    v.scalar_tensor_tensor(acc[:, t, :], Y[idx % 2][0:R, 0:D], weight,
                                           acc[:, t, :], ALU.mult, ALU.add).then_inc(y_free, 1)

            def split(hi, lo, src):
                own.step(v.tensor_copy(hi, src))
                own.wait()
                own.step(v.tensor_tensor(lo, src, hi.bitcast(F32), ALU.subtract))

            def place_blocks(name):
                q = STAGE[name]
                own.step(v.tensor_tensor(SEL[:, :, :], OHK[:, :, 0, :], OHK[:, :, 1, :], ALU.add))
                own.wait()
                v.engine_nop().then_inc(selected, 1)
                if q == 0:
                    dve.wait_ge(route_consts, 11)
                    own.step(v.tensor_copy(WDT[:, :, 2 * EXPERTS:INFO], node_of[:, :, :].broadcast_to([R, T, 2])))
                split(WDT[:, :, 0:EXPERTS], WDT[:, :, EXPERTS:2 * EXPERTS], WD[:, :, :])
                dve.wait_ge(ranked, q + 1)
                own.step(v.tensor_scalar(CNI[:, :], G0[:, 64:72], float(SLOTS - 1), None, ALU.add))
                own.step(v.tensor_copy(RK[:, :, :], G0[0:R, 0:T * 8].rearrange("p (t e) -> p t e", t=T)))
                own.wait()
                own.step(v.tensor_scalar(CNI[:, :], CNI[:, :], 7, None, ALU.logical_shift_right))
                own.wait()
                own.step(v.tensor_copy(NB[:, :], CNI[:, :]))
                own.step(v.tensor_copy(INC[:, :], CNI[:, :]))
                own.wait()
                for e in range(1, EXPERTS):
                    own.step(v.tensor_tensor(INC[:, e:e + 1], INC[:, e:e + 1], INC[:, e - 1:e], ALU.add))
                    own.wait()
                own.step(v.tensor_tensor(EOH[:, :, :], INC[:, :].unsqueeze(1).broadcast_to([P, BL, EXPERTS]),
                                         iota_b[:, :].unsqueeze(2).broadcast_to([P, BL, EXPERTS]), ALU.is_le))
                own.step(v.tensor_tensor(BASE[:, :], INC[:, :], NB[:, :], ALU.subtract))
                own.wait()
                own.step(v.tensor_reduce(EOB[:, :], EOH[:, :, :], AX.X, ALU.add))
                own.wait()
                own.step(v.tensor_scalar(EOB[:, :], EOB[:, :], float(EXPERTS - 1), None, ALU.min))
                own.wait()
                own.step(v.tensor_copy(EOU[:, :], EOB[:, :]))
                own.step(v.tensor_tensor(EOH[:, :, :], iota_e[:, :].unsqueeze(1).broadcast_to([P, BL, EXPERTS]),
                                         EOB[:, :].unsqueeze(2).broadcast_to([P, BL, EXPERTS]), ALU.is_equal))
                own.wait()
                v.engine_nop().then_inc(blocks_known, 1)
                own.step(v.tensor_scalar(BASE[:, :], BASE[:, :], float(SLOTS), None, ALU.mult))
                own.wait()
                own.step(v.tensor_tensor(RK[:, :, :], RK[:, :, :], over_tiles(BASE[0:R, :], EXPERTS), ALU.add))
                own.wait()
                for k in range(2):
                    own.step(v.tensor_tensor(OH0[:, :, :], OHK[:, :, k, :], RK[:, :, :], ALU.mult))
                    own.wait()
                    own.step(v.tensor_reduce(POS[:, :, k], OH0[:, :, :], AX.X, ALU.add))
                    own.wait()
                at, past = slot_work
                own.step(v.tensor_tensor(at, POS[:, :, :].rearrange("p t k -> p (t k)").unsqueeze(1)
                                         .broadcast_to([R, BL, 2 * T]), iota_p[:, :].unsqueeze(2).broadcast_to([R, BL, 2 * T]),
                                         ALU.subtract))
                own.wait()
                own.step(v.tensor_scalar(past, at, float(SLOTS), -1.0e6, ALU.is_ge, ALU.mult))
                own.wait()
                own.step(v.tensor_tensor(at, at, past, ALU.add))
                own.wait()
                own.step(v.tensor_tensor(slot_of[:, :, :], at[:, :, 0:2 * T:2], at[:, :, 1:2 * T:2], ALU.max))
                own.wait()

            def sparse_experts(name, source):
                q, jobs, jbase = STAGE[name], JOBS[name], JBASE[name]
                place_blocks(name)
                if name != "l3":
                    dve.wait_ge(wt_ready, q + 1)
                    v.tensor_copy(WT[:, :, :], G5[0:EXPERTS, 0:T, 0:R]).then_inc(wt_done, 1)
                else:
                    v.memset(WT[:, :, :], 0.0).then_inc(wt_done, 1)
                split(ZH[:, :, :], ZL[:, :, :], source)
                own.wait()
                v.engine_nop().then_inc(parts_ready, 1)

                def permutation(b, k):
                    for t in range(T):
                        last = v.tensor_scalar(PM[:, t, k * SLOTS:(k + 1) * SLOTS], iota_s[0:R, :],
                                               slot_of[:, bass.ds(b, 1), t:t + 1].rearrange("p a t -> p (a t)"),
                                               None, ALU.is_equal)
                    return last

                def weighted(b, col):
                    dve.wait_ge(yb_ready, b + (TOKEN_BLOCKS * q + 1))
                    own.wait()
                    own.step(v.tensor_scalar(YS, YB[:, 0:D], WSL[:, col:col + 1], None, ALU.mult))
                    own.wait()
                    own.step(v.tensor_copy(YH[:, :], YS))
                    own.wait()
                    v.tensor_tensor(YL[:, :], YS, YH[:, :].bitcast(F32), ALU.subtract).then_inc(y_parts, 1)
                    dve.wait_ge(y_parts, b + (TOKEN_BLOCKS * q + 1))

                def block_of_tokens(b, c, i):
                    B = b + TOKEN_BLOCKS * q
                    last_block = isinstance(b, int) and b == TOKEN_BLOCKS - 1
                    if c == 0:
                        permutation(0, 1).then_inc(perm_ready, 1)
                    if c == 0 or c % 2 == 1:
                        subs = [1] if c == 0 else [0, 1]
                        g = pair_of(c, i) + PAIRS * q
                        dve.wait_ge(gathered, g + 1)
                        if not isinstance(B, int) or B >= 1:
                            dve.wait_ge(info_done, B)
                        if c >= 1:
                            own.wait()
                            own.step(v.tensor_copy(WSL[:, 2:3], WSL[:, 1:2]))
                        v.tensor_copy(TI[:, subs[0]:2, :], IB[:, subs[0]:2, :]).then_inc(slots_read, 1)
                        dve.wait_ge(slots_read, g + 1)
                        n = len(subs)
                        own.step(v.tensor_tensor(
                            TW8[:, subs[0]:2, :].rearrange("p b (h e) -> p b h e", h=2),
                            TI[:, subs[0]:2, 0:2 * EXPERTS].rearrange("p b (h e) -> p b h e", h=2),
                            EOH[:, bass.ds(b, n), :].unsqueeze(2).broadcast_to([P, n, 2, EXPERTS]), ALU.mult))
                        own.wait()
                        own.step(v.tensor_reduce(WSL[:, subs[0]:2], TW8[:, subs[0]:2, :], AX.X, ALU.add))
                        if not (isinstance(b, int) and b + n >= TOKEN_BLOCKS):
                            permutation(b + n, 0)
                            permutation(b + (n + 1), 1).then_inc(perm_ready, 1)
                    if c >= 1:
                        weighted(b - 1, 2 if c % 2 == 1 else 0)
                    if name == "l3":
                        for j in range(jobs):
                            w = HID3[j]
                            dve.wait_ge(gate_done, jobs * b + (j + 1))
                            v.tensor_tensor(HT[0:w, j, 0:SLOTS], HB[j % 2][0:w, SLOTS:2 * SLOTS],
                                            SG[0:w, j % 2, 0:SLOTS], ALU.mult).then_inc(hidden, 1)
                    if c >= 1:
                        dve.wait_ge(scattered, B)
                    own.wait()
                    v.tensor_scalar(SS[:, :], iota_n[:, 0:N], TI[:, 1 - c % 2, INFO - 1:INFO], None, ALU.is_equal)\
                     .then_inc(info_done, 1)
                    if last_block:
                        weighted(b, 1)
                    if name == "l0" and isinstance(b, int):
                        t = b if b < 3 else b - TOKEN_BLOCKS + T
                        never(KT[0:R, 0, :], LNC2[:, t, 0:N])
                        own.step(v.tensor_tensor(LNC2[:, t, 0:N], LNC2[:, t, 0:N], KT[0:R, 0, :], ALU.add))
                        own.wait()

                token_blocks(dve, block_of_tokens, own, 7)
                dve.wait_ge(scattered, TOKEN_BLOCKS * (q + 1))
                for t in range(T):
                    own.step(v.tensor_tensor(X[:, t, :], X[:, t, :], OUT[t][0:R, :], ALU.add))
                own.wait()

            normalise("l0f", X, Z)
            route(0, row("bg", 8))
            sparse_experts("l0", Z[:, :, :])

            def gat(name, lnc, vbase, finish):
                heads, slope = HEADS[name], SLOPE[name]
                dh = D // heads
                per = P // dh
                own.step(v.memset(AD[:, :, :], 0.0))
                own.step(v.tensor_copy(AB[:, :, :], vcol(name + "_as", 0, 2).unsqueeze(2).broadcast_to([P, KC, R])))
                own.wait()
                for h in range(heads):
                    r = slice(dh * (h % per), dh * (h % per) + dh)
                    c = h // per
                    last = v.tensor_copy(AD[r, c, h:h + 1], vec[r, V[name + "_ad"] + c:V[name + "_ad"] + c + 1])
                last.then_inc(ab_ready, 1)
                for t in range(T):
                    dve.wait_ge(vs_ready, vbase + t + 1)
                    v.tensor_copy(VS[:, t, 0:D], Y[t % 2][0:R, 0:D]).then_inc(vs_done, 1)
                k, gbase = {"l1": (0, 0), "l2": (1, T * HEADS["l1"])}[name]
                dve.wait_ge(ed_ready, k + 1)
                own.step(v.tensor_copy(ED[:, :, 0:heads],
                                       G1[0:R, 0:T * 8].rearrange("p (t e) -> p t e", t=T)[:, :, 0:heads]))
                own.wait()
                v.tensor_scalar(EDR[:, :, 0:heads], ED[:, :, 0:heads], 1.0 - slope, None, ALU.mult)\
                 .then_inc(ed_done, 1)
                dve.wait_ge(ed_done, k + 1)
                dve.wait_ge(es_done, {"l1": 4, "l2": 12}[name])

                def leaky(k):
                    t, h = divmod(k, heads)
                    if k >= 2:
                        dve.wait_ge(masked, UNITS[name] + (k - 1))
                    if name == "l1":
                        dve.wait_ge(sloped, k + 1)
                    else:
                        own.step(v.tensor_scalar(SLOPED[0], HT[0:R, h, :], ED[:, t, h:h + 1], slope, ALU.add, ALU.mult))
                        own.wait()
                    if name == "l1":
                        if k >= 2:
                            dve.wait_ge(leaky_done, k - 1)
                    v.scalar_tensor_tensor(SC[k % 2], HT[0:R, h, :], ED[:, t, h:h + 1], SLOPED[k % 2],
                                           ALU.add, ALU.max).then_inc(maxed, 1)
                    dve.wait_ge(maxed, k + 1 if name == "l1" else T * HEADS["l1"] + k // 2 + 1)
                    if name == "l1":
                        v.tensor_scalar(ZERO[k % 2], SC[k % 2], 0.0, -1000.0, ALU.is_equal, ALU.mult)\
                         .then_inc(zeros, 1)

                if name == "l1":
                    leaky(0)

                def scores(k, t, h):
                    if name == "l1":
                        if k + 1 < T * heads:
                            leaky(k + 1)
                        dve.wait_ge(leaky_done, k + 1)
                    elif k % 2 == 0:
                        leaky(k)
                    else:
                        dve.wait_ge(leaky_done, gbase + (k // 2 + 1))
                    return SC[k % 2]

                attention(UNITS[name], TILES[name], heads, lnc, scores, finish)

            normalise("l1g", X, Z)

            def add_to_x(t):
                v.tensor_tensor(X[:, t, :], X[:, t, :], ON, ALU.add).then_inc(tile_out, 1)

            gat("l1", LNC, 15, add_to_x)
            dve.wait_ge(tile_out, 20)

            normalise("l1f", X, Z)
            dve.wait_ge(ln_out, LN["l1f"] + 1)
            normalise("l1n", Z, VS[:, :, 0:D])
            route(1, row("br1", 8))

            dve.wait_ge(ln_out, LN["l1n"] + 1)
            sparse_experts("l1", VS[:, :, 0:D])

            normalise("l2g", X, Z)

            def add_bias_and_input(t):
                own.step(v.tensor_tensor(ON, ON, row("bias2", D), ALU.add))
                own.wait()
                v.tensor_tensor(Z[:, t, :], Z[:, t, :], ON, ALU.add).then_inc(tile_out, 1)

            gat("l2", LNC2, 20, add_bias_and_input)
            dve.wait_ge(tile_out, 25)

            def affine_add(scale, shift, name):
                dve.wait_ge(ln_out, LN[name] + 1)
                own.step(v.tensor_tensor(Z[:, :, :], Z[:, :, :], over_tiles(scale, D), ALU.mult))
                own.wait()
                own.step(v.tensor_tensor(Z[:, :, :], Z[:, :, :], over_tiles(shift, D), ALU.add))
                own.wait()
                own.step(v.tensor_tensor(X[:, :, :], X[:, :, :], Z[:, :, :], ALU.add))
                own.wait()

            normalise("l2o", Z, Z)
            affine_add(row("ln_w", D), row("ln_b", D), "l2o")

            normalise("l2f", X, Z)
            dve.wait_ge(logits, 3)
            v.tensor_copy(LG[:, :, :], G1[0:R, 0:T * EXPERTS].rearrange("p (t e) -> p t e", t=T)).then_inc(logits_sb, 1)
            dve.wait_ge(mean_logits, 1)
            one = LG[:, 0, :]
            own.step(v.tensor_tensor(one, G0[0:R, 0:EXPERTS], row("br2", 8), ALU.add))
            own.wait()

            def softmax_row(n):
                own.step(v.tensor_reduce(M8[:, 0, 0:1], one, AX.X, ALU.max))
                own.wait()
                v.tensor_scalar(LX[:, 0, :], one, M8[:, 0, 0:1], None, ALU.subtract).then_inc(route_arg, 1)
                dve.wait_ge(route_exp, n)
                own.step(v.reciprocal(ZS[:, 1:2], ZS[:, 0:1]))
                own.wait()
                own.step(v.tensor_scalar(one, LE[:, 0, :], ZS[:, 1:2], None, ALU.mult))
                own.wait()

            softmax_row(3)
            load, cap = OH0[:, 0, :], OH0[:, 1, :]
            own.step(v.tensor_scalar(load, one, float(N), None, ALU.mult))
            own.wait()
            own.step(v.tensor_scalar(load, load, 98.0, 1.0 / 98.0, ALU.max, ALU.mult))
            own.wait()
            own.step(v.reciprocal(cap, load))
            own.wait()
            own.step(v.tensor_tensor(one, one, cap, ALU.mult))
            own.wait()
            softmax_row(4)
            own.step(v.max(M8[:, 0, :], one))
            own.wait()
            v.max_index(I8[:, 0, :], M8[:, 0, :], one).then_inc(picked, 1)
            v.tensor_tensor(E2[:, 0:1], M8[:, 0, 1:2], M8[:, 0, 0:1], ALU.subtract).then_inc(route_arg, 1)
            dve.wait_ge(route_exp, 5)
            own.step(v.tensor_scalar(ZS[:, 0:1], E2[:, 0:1], 1.0, None, ALU.add))
            own.wait()
            own.step(v.reciprocal(TW[:, 0, 0:1], ZS[:, 0:1]))
            own.wait()
            own.step(v.tensor_tensor(TW[:, 0, 1:2], TW[:, 0, 0:1], E2[:, 0:1], ALU.mult))
            own.wait()
            dve.wait_ge(picked, 1)
            for t in range(1, T):
                own.step(v.tensor_copy(TW[:, t, :], TW[:, 0, :]))
                own.step(v.tensor_copy(I8[:, t, :], I8[:, 0, :]))
            own.wait()
            dense_weights()
            dve.wait_ge(routed, 3)
            for s in range(2):
                combine(s, Z, TW[:, 0, s:s + 1])
            dve.wait_ge(wt_ready, 3)
            v.tensor_copy(WT[:, :, :], G5[0:EXPERTS, 0:T, 0:R]).then_inc(wt_done, 1)
            for t in range(T):
                idx = 2 * T + t
                dve.wait_ge(y_ready, idx + 1)
                dve.wait_ge(y_free, idx + 2)
                v.tensor_tensor(Z[:, t, :], Z[:, t, :], Y[idx % 2][0:R, 0:D], ALU.add).then_inc(y_free, 1)
            dve.wait_ge(y_free, 3 * T + 2)
            normalise("l2p", Z, Z)
            affine_add(row("gamma", D), row("beta", D), "l2p")

            dve.wait_ge(deg_ready, 1)
            own.step(v.tensor_scalar(deg[:, :], G0[0:R, 0:T], 1.0, None, ALU.add))
            own.wait()
            v.engine_nop().then_inc(bn_affine, 1)
            normalise("l3g", X, Z)
            for c in range(KC):
                dve.wait_ge(qk_done, 16 + c + 1)
                own.step(v.bn_stats(FST[:, c, 0, :], QT[:, c, 0:500]))
                own.step(v.bn_stats(FST[:, c, 1, :], QT[:, c, 500:N]))
            affine(vcol("l3_g", 0, 2), vcol("l3_b", 0, 2), LAYERS - 1)
            dve.wait_ge(bn_rstd, LAYERS + 1)
            for t in range(T):
                dve.wait_ge(vs_ready, 25 + t + 1)
                v.tensor_scalar(VS[:, t, 0:D], Y[t % 2][0:R, 0:D], dinv[:, t:t + 1], None, ALU.mult).then_inc(vs_done, 1)
            dve.wait_ge(vs_done, 25 + T)
            for t in range(T):
                dve.wait_ge(mixed, 120 + t + 1)
                dve.wait_ge(tile_out, 25 + t)
                own.step(v.tensor_tensor(ON, Y[t % 2][0:R, 0:D], VS[:, t, 0:D], ALU.add))
                own.wait()
                own.step(v.scalar_tensor_tensor(ON, ON, dinv[:, t:t + 1], row("b_gcn", D), ALU.mult, ALU.add))
                own.wait()
                v.tensor_tensor(X[:, t, :], X[:, t, :], ON, ALU.add).then_inc(tile_out, 1)
            dve.wait_ge(tile_out, 25 + T)

            normalise("l3f", X, Z)
            route(3, None)
            sparse_experts("l3", Z[:, :, :])
            v.engine_nop().then_inc(x_ready, 1)


def kernel(**inp):
    import numpy as np
    import concourse.bacc as bacc
    from concourse.bass_utils import run_bass_kernel_spmd

    def features(v):
        v = v.reshape(-1, v.shape[-1] // 128, 128)
        return v.reshape(-1, 128).T

    def chunks(w):
        k, m = w.shape[-2:]
        return np.moveaxis(w.reshape(w.shape[:-2] + (k // 128, 128, m)), -3, -2)

    def pad_rows(w, n):
        full = np.zeros(w.shape[:-2] + (n, w.shape[-1]), w.dtype)
        full[..., :w.shape[-2], :] = w
        return full

    i = {k: np.asarray(v) for k, v in inp.items()}
    A = {}
    A["x"] = i["x"].reshape(T, R, D).transpose(1, 0, 2)
    A["src"] = i["src"].reshape(R, BLOCKS)
    A["dst"] = i["dst"].reshape(R, BLOCKS)
    A["vec"] = np.concatenate([
        features(i["L0_gnn_bq"]), features(i["L0_gnn_bk"]), features(i["L0_gnn_bn_gamma"]),
        features(i["L0_gnn_bn_beta"]),
        features(i["L1_gnn_att"][:, :64].reshape(1, D)), features(i["L1_gnn_att"][:, 64:].reshape(1, D)),
        features(i["L2_gnn_att_src"].reshape(1, D)), features(i["L2_gnn_att_dst"].reshape(1, D)),
        features(i["L3_gnn_b1"][None]), features(i["L3_gnn_gamma"][None]), features(i["L3_gnn_beta"][None]),
        features(i["L3_gnn_b2"][None])], axis=1)
    bvs = np.concatenate([i["L0_gnn_bv"], i["L0_gnn_bs"]], axis=1).reshape(-1)
    A["rows"] = np.concatenate([bvs, i["L0_ffn_bg"], i["L1_ffn_br"], i["L2_ffn_br"], i["L2_gnn_bias"],
                                i["L2_gnn_ln_w"], i["L2_gnn_ln_b"], i["L2_ffn_gamma"], i["L2_ffn_beta"],
                                i["L3_gnn_b_gcn"]])
    A["wr"] = np.stack([chunks(i["L0_ffn_Wg"]), chunks(i["L1_ffn_Wr"]), chunks(i["L2_ffn_Wr"]),
                        chunks(i["L3_ffn_router_w"].T)], axis=1)
    A["b2"] = np.stack([i["L0_ffn_b2"], i["L1_ffn_b2"], i["L2_ffn_b2"]], axis=1)
    A["l0_wqk"] = np.stack([chunks(i["L0_gnn_Wq"]), chunks(i["L0_gnn_Wk"])], axis=2)
    A["l0_wvs"] = np.concatenate([chunks(i["L0_gnn_Wv"]), chunks(i["L0_gnn_Ws"])], axis=-1)
    A["l1_w"] = chunks(i["L1_gnn_W"].transpose(1, 0, 2).reshape(D, D))
    A["l2_w"] = chunks(i["L2_gnn_W"])
    A["l3_w"] = np.stack([chunks(i["L3_gnn_w1"].T), chunks(i["L3_gnn_w2"].T)], axis=1)
    A["l3_wg"] = chunks(i["L3_gnn_w_gcn"].T)
    for s in ("0", "1", "2"):
        for w, name in (("W1", "w1"), ("W2", "w2")):
            A[f"l{s}_{name}"] = chunks(i[f"L{s}_ffn_{w}"]).reshape(EXPERTS, P, -1)

    def per_expert(v):
        return v.reshape(EXPERTS, -1, P).transpose(0, 2, 1)

    A["l0_w1"] = np.concatenate([A["l0_w1"], per_expert(i["L0_ffn_b1"])], axis=2)
    A["l1_w1"] = np.concatenate([A["l1_w1"], per_expert(i["L1_ffn_b1"]), per_expert(i["L1_ffn_ln_g"]),
                                 per_expert(i["L1_ffn_ln_b"])], axis=2)
    A["l2_b1"] = i["L2_ffn_b1"].reshape(EXPERTS, 4, 128).transpose(0, 2, 1)
    w13 = np.stack([chunks(i["L3_ffn_w1"].transpose(0, 2, 1)), chunks(i["L3_ffn_w3"].transpose(0, 2, 1))], axis=2)
    A["l3_w13"] = w13.reshape(EXPERTS, P, -1)
    A["l3_w2"] = chunks(pad_rows(i["L3_ffn_w2"].transpose(0, 2, 1), 128 * len(HID3))).reshape(EXPERTS, P, -1)

    nc = bacc.Bacc("TRN2", target_bir_lowering=False, num_devices=1)
    arrays, aps = {}, {}
    for name, arr in A.items():
        arr = np.ascontiguousarray(arr)
        arrays[f"in_{name}"] = arr
        aps[name] = nc.dram_tensor(f"in_{name}", arr.shape, mybir.dt.from_np(arr.dtype), kind="ExternalInput").ap()
    out = nc.dram_tensor("out", (R, T, D), F32, kind="ExternalOutput").ap()
    graph_network(nc, aps, out)
    r = run_bass_kernel_spmd(nc, [arrays], core_ids=[0])
    return np.ascontiguousarray(r.results[0]["out"].transpose(1, 0, 2)).reshape(N, D)
```
